# Optimizing a Trainium2 kernel written in Bass

```python
import numpy as np
import jax
import jax.numpy as jnp

def _softmax(x, axis=-1):
    return jax.nn.softmax(x, axis=axis)

def _gelu(x):
    return jax.nn.gelu(x, approximate=True)

def _silu(x):
    return jax.nn.silu(x)

def _sigmoid(x):
    return jax.nn.sigmoid(x)

def _layernorm(x, axis=-1, eps=1e-05):
    m = jnp.mean(x, axis=axis, keepdims=True)
    v = jnp.var(x, axis=axis, keepdims=True)
    return (x - m) / jnp.sqrt(v + eps)

def _scatter_add(tgt, idx, src, axis=0):
    return tgt.at[idx].add(src)

def _segment_sum(src, seg, n):
    return jax.ops.segment_sum(src, seg, n)
kernel_name = 'mk_gnn_ffn_d1_gnn_r8_95961a'

def setup_inputs(seed: int=0):
    np.random.seed(seed)
    _w = jnp.asarray

    def _rec_inputs():
        import jax
        import jax.numpy as jnp
        _gk = jax.random.key(seed)
        x = -0.0003713 + 1 * jax.random.normal(jax.random.fold_in(_gk, 1), (6250, 256), jnp.float32)
        _s = jax.random.randint(jax.random.fold_in(_gk, 2), (50000,), 0, 6250, jnp.int32)
        _d = jax.random.randint(jax.random.fold_in(_gk, 3), (50000,), 0, 6250, jnp.int32)
        _loop = jnp.arange(6250, dtype=jnp.int32)
        src = jnp.concatenate([_s, _d, _loop])
        dst = jnp.concatenate([_d, _s, _loop])
        _o = jnp.argsort(dst, stable=True)
        src = src[_o]
        dst = dst[_o]
        edge_attr_32 = 0.000189758 + 1.00013 * jax.random.normal(jax.random.fold_in(_gk, 11), (106250, 32), jnp.float32)
        return (x, src, dst, edge_attr_32)
    x, src, dst, edge_attr_32 = _rec_inputs()

    def _L0_gnn_setup():
        import jax, jax.numpy as jnp
        import numpy as np
        N_NODES = 6250
        N_EDGES = 200000
        IN_CH = 256
        ADAPTER = 64
        EDGE_DIM = 32
        key = jax.random.key(seed)
        ks = jax.random.split(key, 12)
        s = lambda k, shape: jax.random.normal(k, shape, dtype=jnp.float32) * 0.05
        x = jax.random.normal(ks[0], (N_NODES, IN_CH), dtype=jnp.float32)
        edge_index = jax.random.randint(ks[1], (2, N_EDGES), 0, N_NODES, dtype=jnp.int64)
        edge_attr = jax.random.normal(ks[2], (N_EDGES, EDGE_DIM), dtype=jnp.float32)
        return {'x': x, 'edge_index': edge_index, 'edge_attr': edge_attr, 'W_down': s(ks[3], (ADAPTER, IN_CH)), 'b_down': jnp.zeros((ADAPTER,), jnp.float32), 'W_time': s(ks[4], (ADAPTER, EDGE_DIM)), 'b_time': jnp.zeros((ADAPTER,), jnp.float32), 'W_fusion': s(ks[5], (ADAPTER, 2 * ADAPTER)), 'b_fusion': jnp.zeros((ADAPTER,), jnp.float32), 'W_up': s(ks[6], (IN_CH, ADAPTER)), 'b_up': jnp.zeros((IN_CH,), jnp.float32)}
    _L0_gnn_all = _L0_gnn_setup()
    _L0_gnn_in = {k: v for k, v in _L0_gnn_all.items() if k in ('W_down', 'b_down', 'W_time', 'b_time', 'W_fusion', 'b_fusion', 'W_up', 'b_up')}
    del _L0_gnn_all

    def _L0_ffn_setup():
        import jax, jax.numpy as jnp
        import numpy as np
        TOP_K = 2
        LN_EPS = 1e-05
        key = jax.random.key(seed)
        ks = jax.random.split(key, 8)
        B, S, D, E, H = (16, 1024, 256, 8, 1024)
        x = jax.random.normal(ks[0], (B, S, D), dtype=jnp.float32)
        Wr = jax.random.normal(ks[1], (D, E), dtype=jnp.float32) * 0.1
        br = jnp.zeros((E,), dtype=jnp.float32)
        ln_g = jnp.ones((E, D), dtype=jnp.float32)
        ln_b = jnp.zeros((E, D), dtype=jnp.float32)
        W1 = jax.random.normal(ks[2], (E, D, H), dtype=jnp.float32) * (1.0 / np.sqrt(D))
        b1 = jnp.zeros((E, H), dtype=jnp.float32)
        W2 = jax.random.normal(ks[3], (E, H, D), dtype=jnp.float32) * (1.0 / np.sqrt(H))
        b2 = jnp.zeros((E, D), dtype=jnp.float32)
        return {'x': x, 'Wr': Wr, 'br': br, 'ln_g': ln_g, 'ln_b': ln_b, 'W1': W1, 'b1': b1, 'W2': W2, 'b2': b2}
    _L0_ffn_all = _L0_ffn_setup()
    _L0_ffn_in = {k: v for k, v in _L0_ffn_all.items() if k in ('Wr', 'br', 'ln_g', 'ln_b', 'W1', 'b1', 'W2', 'b2')}
    del _L0_ffn_all
    return {'x': x, 'src': src, 'dst': dst, 'edge_attr_32': edge_attr_32, 'L0_gnn_W_down': _L0_gnn_in['W_down'], 'L0_gnn_b_down': _L0_gnn_in['b_down'], 'L0_gnn_W_time': _L0_gnn_in['W_time'], 'L0_gnn_b_time': _L0_gnn_in['b_time'], 'L0_gnn_W_fusion': _L0_gnn_in['W_fusion'], 'L0_gnn_b_fusion': _L0_gnn_in['b_fusion'], 'L0_gnn_W_up': _L0_gnn_in['W_up'], 'L0_gnn_b_up': _L0_gnn_in['b_up'], 'L0_ffn_Wr': _L0_ffn_in['Wr'], 'L0_ffn_br': _L0_ffn_in['br'], 'L0_ffn_ln_g': _L0_ffn_in['ln_g'], 'L0_ffn_ln_b': _L0_ffn_in['ln_b'], 'L0_ffn_W1': _L0_ffn_in['W1'], 'L0_ffn_b1': _L0_ffn_in['b1'], 'L0_ffn_W2': _L0_ffn_in['W2'], 'L0_ffn_b2': _L0_ffn_in['b2']}

def reference(x, src, dst, edge_attr_32, L0_gnn_W_down, L0_gnn_b_down, L0_gnn_W_time, L0_gnn_b_time, L0_gnn_W_fusion, L0_gnn_b_fusion, L0_gnn_W_up, L0_gnn_b_up, L0_ffn_Wr, L0_ffn_br, L0_ffn_ln_g, L0_ffn_ln_b, L0_ffn_W1, L0_ffn_b1, L0_ffn_W2, L0_ffn_b2):
    import jax
    import jax.numpy as jnp

    def _L0_gnn_ref(x, edge_index, edge_attr, W_down, b_down, W_time, b_time, W_fusion, b_fusion, W_up, b_up):
        import jax, jax.numpy as jnp
        import numpy as np
        N_NODES = 6250
        N_EDGES = 200000
        IN_CH = 256
        ADAPTER = 64
        EDGE_DIM = 32
        n = x.shape[0]
        node_feat = jax.nn.relu(x @ W_down.T + b_down)
        time_feat = jax.nn.relu(edge_attr @ W_time.T + b_time)
        src = edge_index[0]
        sums = jax.ops.segment_sum(time_feat, src, num_segments=n)
        counts = jax.ops.segment_sum(jnp.ones((time_feat.shape[0],), jnp.float32), src, num_segments=n)
        node_time_feat = sums / jnp.maximum(counts, 1.0)[:, None]
        combined = jnp.concatenate([node_feat, node_time_feat], axis=-1)
        fused = jax.nn.relu(combined @ W_fusion.T + b_fusion)
        out = fused @ W_up.T + b_up
        return x + out

    def _L0_ffn_ref(x, Wr, br, ln_g, ln_b, W1, b1, W2, b2):
        import jax, jax.numpy as jnp
        import numpy as np
        TOP_K = 2
        LN_EPS = 1e-05
        B, S, D = x.shape
        N = B * S
        xt = x.reshape(N, D)
        logits = xt @ Wr + br
        probs = jax.nn.softmax(logits, axis=-1)
        top_p, top_idx = jax.lax.top_k(probs, TOP_K)
        weights = top_p / top_p.sum(axis=-1, keepdims=True)
        mu = xt.mean(axis=-1, keepdims=True)
        var = ((xt - mu) ** 2).mean(axis=-1, keepdims=True)
        xn = (xt - mu) * jax.lax.rsqrt(var + LN_EPS)
        xe = xn[None, :, :] * ln_g[:, None, :] + ln_b[:, None, :]
        h = jax.nn.gelu(jnp.einsum('end,edh->enh', xe, W1) + b1[:, None, :], approximate=False)
        y = jnp.einsum('enh,ehd->end', h, W2) + b2[:, None, :]
        y_tok = jnp.transpose(y, (1, 0, 2))
        sel = jnp.take_along_axis(y_tok, top_idx[:, :, None], axis=1)
        out = (weights[:, :, None] * sel).sum(axis=1)
        return out.reshape(B, S, D)
    edge_index = jnp.stack([src, dst])
    x = x + _L0_gnn_ref(_layernorm(x, axis=-1), edge_index, edge_attr_32, L0_gnn_W_down, L0_gnn_b_down, L0_gnn_W_time, L0_gnn_b_time, L0_gnn_W_fusion, L0_gnn_b_fusion, L0_gnn_W_up, L0_gnn_b_up)
    x = x + _L0_ffn_ref(_layernorm(x, axis=-1)[None], L0_ffn_Wr, L0_ffn_br, L0_ffn_ln_g, L0_ffn_ln_b, L0_ffn_W1, L0_ffn_b1, L0_ffn_W2, L0_ffn_b2)[0]
    return x

_drawn_inputs = setup_inputs


def setup_inputs(seed=0):
    import zlib

    import numpy as np

    out = dict(_drawn_inputs(seed))
    spreads = {'L0_gnn_b_down': (0.0, 0.8),
     'L0_gnn_b_time': (0.0, 2.0),
     'L0_gnn_b_fusion': (0.0, 0.28),
     'L0_gnn_b_up': (0.0, 0.1),
     'L0_ffn_br': (0.0, 0.1),
     'L0_ffn_ln_g': (1.0, 0.2),
     'L0_ffn_ln_b': (0.0, 0.308),
     'L0_ffn_b1': (0.0, 0.306),
     'L0_ffn_b2': (0.0, 0.1)}
    factors = {'edge_attr_32': 7.463, 'L0_gnn_W_time': 7.496}
    for name, (base, spread) in spreads.items():
        noise = np.random.default_rng([zlib.crc32(name.encode()), seed]).standard_normal(out[name].shape)
        drawn = base * np.exp(spread * noise) if base else spread * noise
        out[name] = jnp.asarray(drawn.astype(out[name].dtype))
    for name, factor in factors.items():
        out[name] = (out[name] * factor).astype(out[name].dtype)
    return out
```

```python
from contextlib import ExitStack

import concourse.bass as bass
from concourse import mybir

P = 128
F32 = mybir.dt.float32
BF16 = mybir.dt.bfloat16
I32 = mybir.dt.int32
ALU = mybir.AluOpType
ACT = mybir.ActivationFunctionType
AX_X = mybir.AxisListType.X
EPS = 1e-5


def ceil_div(a, b):
    return -(-a // b)


N = 6250
D = 256
TPP = ceil_div(N, P)
NPAD = TPP * P
KD = D // P
E = 106250
FE = 32
GT = 8
EPP = ceil_div(ceil_div(E, P), 2 * GT) * 2 * GT
EPAD = EPP * P
ITERS = EPP // (2 * GT)
A = 64
AC = A + 1
X = 8
H = 1024
HC = H // P
TILES = (2 * N + X * (P - 1)) // P
MT = TILES + 2
ROWS = NPAD + P
TABLES = 4
BATCH = 7
NB = TPP // BATCH
MAP_ROWS = P * MT + 2 * TPP
BIG = 3.0e38


class Steps:

    def __init__(self, eng, sem):
        self.eng, self.sem, self.n = eng, sem, 0

    def step(self, ins):
        ins.then_inc(self.sem, 1)
        self.n = self.n + 1

    def settle(self):
        self.eng.wait_ge(self.sem, self.n)


def program(nc, x, src, edge, W_down, b_down, W_time, b_time, W_fusion, b_fusion, W_up, b_up,
            Wr, br, ln_g, ln_b, W1, b1, W2, b2, out):
    tables = [nc.dram_tensor(f"sums_{k}", [ROWS, AC], F32).ap() for k in range(TABLES)]
    xtab = nc.dram_tensor("xn_parts", [ROWS, 2 * D], BF16).ap()
    skip = nc.dram_tensor("x_plus_xn", [NPAD, D], F32).ap()
    rowmap = nc.dram_tensor("row_map", [MAP_ROWS, 2], I32).ap()

    ctx = ExitStack()
    with ctx:
        def sb(name, shape, dt=F32, scope=ctx):
            return scope.enter_context(nc.sbuf_tensor(name, shape, dt))

        def sem(name, scope=ctx):
            return scope.enter_context(nc.semaphore(name))

        bank = [ctx.enter_context(nc.psum_tensor(f"bank{i}", [P, 512], F32)) for i in range(8)]

        w1s = sb("w1s", [P, X, KD, 2, H], BF16)
        w2s = sb("w2s", [P, X, HC, 2, D], BF16)
        b1p = sb("b1p", [P, X * HC])
        ident = sb("ident", [P, P])
        identb = sb("identb", [P, P], BF16)
        ones = sb("ones", [P, P])
        before = sb("before", [P, P])
        trash = sb("trash", [P, 1])
        eps = sb("eps", [P, 1])
        eps2 = sb("eps2", [P, 1])
        wfa = sb("wfa", [A, P])
        wfb = sb("wfb", [A, P])
        wup = sb("wup", [A + 1, D])
        wr = sb("wr", [P, KD, X])
        brb = sb("brb", [P, X])
        bfu = sb("bfu", [A, 1])
        logits = sb("logits", [P, TPP, X])
        parts_stored = sem("parts_stored")
        added = sem("added")

        with ExitStack() as gnn:
            nodeT = sb("nodeT", [A, TPP * P], F32, gnn)
            with ExitStack() as one:
                edges_and_nodes(nc, one, sb, sem, bank, locals())
            node_update(nc, sb, sem, bank, locals())
        with ExitStack() as moe:
            route_and_experts(nc, moe, sb, sem, bank, locals())


def edges_and_nodes(nc, ctx, sb_, sem_, bank, env):
    g = env
    def sb(name, shape, dt=F32):
        return sb_(name, shape, dt, ctx)
    def sem(name):
        return sem_(name, ctx)
    x, src, edge, tables, xtab, skip, rowmap, out = (g[k] for k in ("x", "src", "edge", "tables", "xtab", "skip", "rowmap", "out"))
    w1s, w2s, b1p, ident, identb, ones, before, trash = (g[k] for k in ("w1s", "w2s", "b1p", "ident", "identb", "ones", "before", "trash"))
    eps, eps2, wfa, wfb, wup, wr, brb, bfu, nodeT = (g[k] for k in ("eps", "eps2", "wfa", "wfb", "wup", "wr", "brb", "bfu", "nodeT"))

    upto = sb("upto", [P, P])
    srci = sb("srci", [P, EPP], I32)
    srcf = sb("srcf", [P, EPP])
    srcg = sb("srcg", [P, 2 * GT])
    zero = sb("zero", [P, 650])
    preset = sb("preset", [P, MT, 2], I32)
    wd_raw = sb("wd_raw", [A, D])
    wt_raw = sb("wt_raw", [A, 4, FE])
    wf_raw = sb("wf_raw", [A, 2 * A])
    wu_raw = sb("wu_raw", [P, KD, A])
    ln_raw = sb("ln_raw", [X * KD, 2, P])
    b1_raw = sb("b1_raw", [X * HC, P])
    bdn = sb("bdn", [A, 1])
    bt_raw = sb("bt_raw", [1, A])
    wdT = sb("wdT", [P, KD, A])
    wtd = sb("wtd", [P, 4, A])
    bt8 = sb("bt8", [1, GT, A])
    lnT = sb("lnT", [P, 2, X * KD])
    b1T = sb("b1T", [P, X * HC])
    attr = [sb(f"attr{i}", [P, GT * FE]) for i in range(2)]
    attrT = sb("attrT", [P, 2, P])
    tf = [sb(f"tf{i}", [P, GT, AC]) for i in range(2)]
    same = [sb(f"same{i}", [P, 4, P]) for i in range(2)]
    rank = [sb(f"rank{i}", [P, GT]) for i in range(2)]
    away = [sb(f"away{i}", [P, GT]) for i in range(2)]
    idx = [sb(f"idx{i}", [P, GT], I32) for i in range(2)]
    pay = [sb(f"pay{i}", [P, GT, AC]) for i in range(2)]
    xt = sb("xt", [P, D])
    xn = sb("xn", [P, D])
    st = sb("st", [P, D])
    xnT = sb("xnT", [P, KD, P])
    stats = sb("stats", [P, 6])
    mv = sb("mv", [P, 2])
    std = sb("std", [P, 1])
    rstd = sb("rstd", [P, 1])
    stage = sb("stage", [P, 2 * H])

    between = sem("between")
    small_loaded = sem("small_loaded")
    init_stored = sem("init_stored")
    zeroed = sem("zeroed")
    filled = sem("filled")
    ready = sem("ready")
    prep_psum = sem("prep_psum")
    prep_done = sem("prep_done")
    src_loaded = sem("src_loaded")
    src_float = sem("src_float")
    added, parts_stored = g["added"], g["parts_stored"]
    tab_done = [sem(f"tab_done{k}") for k in range(TABLES)]

    with nc.Block() as block:
        small = [
            (wd_raw[:, :], g["W_down"]), (wf_raw[:, :], g["W_fusion"]),
            (wu_raw[:, :, :], g["W_up"].rearrange("(k p) a -> p k a", p=P)),
            (ln_raw[:, 0, :], g["ln_g"].rearrange("e (k p) -> (e k) p", p=P)),
            (ln_raw[:, 1, :], g["ln_b"].rearrange("e (k p) -> (e k) p", p=P)),
            (b1_raw[:, :], g["b1"].rearrange("e (c p) -> (e c) p", p=P)),
            (bdn[:, :], g["b_down"].rearrange("(a o) -> a o", o=1)),
            (bfu[:, :], g["b_fusion"].rearrange("(a o) -> a o", o=1)),
            (bt_raw[:, :], g["b_time"].rearrange("(o a) -> o a", o=1)),
            (wup[A:A + 1, :], g["b_up"].rearrange("(o d) -> o d", o=1)),
            (wr[:, :, :], g["Wr"].rearrange("(k p) e -> p k e", p=P)),
            (brb[:, :], g["br"].rearrange("(o e) -> o e", o=1).to_broadcast([P, X])),
        ] + [(wt_raw[:, i, :], g["W_time"]) for i in range(4)]

        @block.sync
        def _(sp):
            sp.dma_start(srci[:, :], src.rearrange("(p j) -> p j", p=P)).then_inc(src_loaded, 16)
            for dst, s in small:
                sp.dma_start(dst, s).then_inc(small_loaded, 16)
            sp.wait_ge(filled, 1)
            sp.dma_start(rowmap[0:P * MT, :].rearrange("(p i) c -> p (i c)", p=P),
                         preset[:, :, :].rearrange("p i c -> p (i c)")).then_inc(init_stored, 16)
            sp.wait_ge(small_loaded, 16 * len(small))
            sp.wait_ge(init_stored, 16)

        @block.gpsimd
        def _(pool):
            pool.memset(zero[:, :], 0.0).then_inc(zeroed, 1)
            pool.wait_ge(zeroed, 1)
            for k in range(TABLES):
                rows = ROWS // P * AC
                pool.dma_start(
                    tables[k].rearrange("(p r) a -> p (r a)", p=P).rearrange("p (u v) -> p u v", v=650),
                    zero[:, :].rearrange("p (o v) -> p o v", o=1).to_broadcast([P, rows // 650, 650]),
                ).then_inc(tab_done[k], 16)
            for h in range(2):
                pool.dma_start(out[NPAD + h * A:NPAD + (h + 1) * A, :], zero[h * A:(h + 1) * A, 0:D]).then_inc(added, 16)
            pool.dma_start(xtab[NPAD:ROWS, :], zero[:, 0:D].bitcast(BF16)).then_inc(parts_stored, 16)
            pool.memset(ident[:, :], 0.0).then_inc(ready, 1)
            pool.memset(upto[:, :], 1.0).then_inc(ready, 1)
            pool.memset(before[:, :], 1.0).then_inc(ready, 1)
            pool.memset(ones[:, :], 1.0).then_inc(ready, 1)
            pool.memset(preset[:, :, :], 0).then_inc(ready, 1)
            pool.memset(eps[:, :], EPS).then_inc(ready, 1)
            pool.memset(eps2[:, :], EPS * EPS).then_inc(ready, 1)
            pool.iota(trash[:, :], pattern=[[0, 1]], base=NPAD, channel_multiplier=1,
                      allow_small_or_imprecise_dtypes=True).then_inc(ready, 1)
            pool.wait_ge(ready, 8)
            pool.iota(preset[:, :, 0], pattern=[[0, MT]], base=NPAD, channel_multiplier=1).then_inc(filled, 1)
            pool.affine_select(out=ident[:, :], in_=ident[:, :], compare_op=ALU.not_equal, fill=1.0,
                               base=0, pattern=[[-1, P]], channel_multiplier=1).then_inc(ready, 1)
            pool.affine_select(out=upto[:, :], in_=upto[:, :], compare_op=ALU.is_ge, fill=0.0,
                               base=0, pattern=[[-1, P]], channel_multiplier=1).then_inc(ready, 1)
            pool.affine_select(out=before[:, :], in_=before[:, :], compare_op=ALU.is_ge, fill=0.0,
                               base=-1, pattern=[[1, P]], channel_multiplier=-1).then_inc(ready, 1)

        @block.tensor
        def _(pe):
            pe.wait_ge(ready, 11)
            pe.wait_ge(small_loaded, 16 * len(small))
            for k in range(KD):
                pe.transpose(bank[0][:, k * A:(k + 1) * A], wd_raw[:, k * P:(k + 1) * P], ident[0:A, 0:A])
            pe.transpose(bank[0][:, 128:128 + A], wt_raw[:, :, :].rearrange("a i f -> a (i f)"),
                         ident[0:A, 0:A]).then_inc(prep_psum, 1)
            for i in range(2):
                pe.transpose(bank[1][0:A, i * A:(i + 1) * A], wf_raw[:, i * A:(i + 1) * A], ident[0:A, 0:A])
            for k in range(KD):
                mm = pe.transpose(bank[1][0:A, 128 + k * P:128 + (k + 1) * P], wu_raw[:, k, :], ident[:, :])
            mm.then_inc(prep_psum, 1)
            for i in range(2):
                pe.transpose(bank[2][:, i * X * KD:(i + 1) * X * KD], ln_raw[:, i, :],
                             ident[0:X * KD, 0:X * KD])
            pe.transpose(bank[2][:, 64:64 + X * HC], b1_raw[:, :], ident[0:X * HC, 0:X * HC]).then_inc(prep_psum, 1)

        @block.vector
        def _(dve):
            dve.memset(wtd[:, :, :], 0.0).then_inc(prep_done, 1)
            dve.memset(wfa[:, :], 0.0).then_inc(prep_done, 1)
            dve.memset(wfb[:, :], 0.0).then_inc(prep_done, 1)
            for b in range(2):
                dve.memset(tf[b][:, :, A:AC], 1.0).then_inc(prep_done, 1)
            dve.wait_ge(prep_done, 5)
            dve.wait_ge(src_loaded, 16)
            dve.tensor_copy(srcf[:, :], srci[:, :]).then_inc(src_float, 1)
            dve.wait_ge(ready, 11)
            dve.tensor_copy(identb[:, :], ident[:, :]).then_inc(prep_done, 1)
            dve.wait_ge(prep_psum, 1)
            dve.tensor_copy(wdT[:, :, :].rearrange("p k a -> p (k a)"), bank[0][:, 0:KD * A]).then_inc(prep_done, 1)
            for i in range(4):
                dve.tensor_copy(wtd[i * FE:(i + 1) * FE, i, :],
                                bank[0][i * FE:(i + 1) * FE, 128:128 + A]).then_inc(prep_done, 1)
            dve.wait_ge(small_loaded, 16 * len(small))
            dve.tensor_copy(bt8[:, :, :], bt_raw[:, :].rearrange("o (u a) -> o u a", u=1).to_broadcast([1, GT, A])).then_inc(prep_done, 1)
            dve.wait_ge(prep_psum, 2)
            dve.tensor_copy(wfa[:, 0:A], bank[1][0:A, 0:A]).then_inc(prep_done, 1)
            dve.tensor_copy(wfb[:, 0:A], bank[1][0:A, A:2 * A]).then_inc(prep_done, 1)
            dve.tensor_copy(wup[0:A, :], bank[1][0:A, 128:128 + D]).then_inc(prep_done, 1)
            dve.wait_ge(prep_psum, 3)
            dve.tensor_copy(lnT[:, :, :].rearrange("p i c -> p (i c)"), bank[2][:, 0:2 * X * KD]).then_inc(prep_done, 1)
            dve.tensor_copy(b1T[:, :], bank[2][:, 64:64 + X * HC]).then_inc(prep_done, 1)

    attr_loaded = [sem(f"attr_loaded{b}") for b in range(2)]
    attr_free = [sem(f"attr_free{b}") for b in range(2)]
    src_group = sem("src_group")
    attrT_psum = sem("attrT_psum")
    attrT_ready = sem("attrT_ready")
    tf_psum = sem("tf_psum")
    tf_ready = sem("tf_ready")
    srcT_psum = sem("srcT_psum")
    same_ready = sem("same_ready")
    idx_ready = sem("idx_ready")
    pay_psum = sem("pay_psum")
    pay_ready = sem("pay_ready")
    pay_free = sem("pay_free")
    x_loaded = sem("x_loaded")
    x_free = sem("x_free")
    mv_ready = sem("mv_ready")
    std_ready = sem("std_ready")
    xn_ready = sem("xn_ready")
    skip_ready = sem("skip_ready")
    skip_stored = sem("skip_stored")
    xnT_psum = sem("xnT_psum")
    xnT_ready = sem("xnT_ready")
    node_psum = sem("node_psum")
    node_ready = sem("node_ready")
    w_loaded = sem("w_loaded")
    w_cut = sem("w_cut")
    w_bias_psum = sem("w_bias_psum")
    w_free = sem("w_free")
    dve_step = sem("dve_step")

    NODES, W1_UNIT, W2_UNIT = 1, 2, 4
    segments = [(0, X, NODES | W1_UNIT), (X, 2 * X, NODES | W2_UNIT), (2 * X, TPP, NODES), (TPP, ITERS, 0)]
    edge_v = edge.rearrange("(p j) f -> p (j f)", p=P)
    x_v = x.rearrange("(p t) d -> p t d", p=P)
    skip_v = skip.rearrange("(p t) d -> p t d", p=P)
    w1_v = g["W1"].rearrange("e (k p) h -> p e k h", p=P)
    w2_v = g["W2"].rearrange("e (c p) d -> p e c d", p=P)
    bankA, bankB, bankN, bankW = bank[0], bank[1], bank[6], bank[7]
    bankC, bankD = bank[2:4], bank[4:6]

    with nc.Block() as block:

        @block.sync
        def _(sp):
            for first, end, kind in segments:
                with sp.Fori(first, end) as it:
                    for b in range(2):
                        sp.wait_ge(attr_free[b], it + 1)
                        sp.dma_start(attr[b][:, :], edge_v[:, bass.ds(it * (2 * GT * FE) + b * GT * FE, GT * FE)]
                                     ).then_inc(attr_loaded[b], 16)
                    if kind & NODES:
                        sp.wait_ge(x_free, it + 1)
                        sp.dma_start(xt[:, :], x_v[:, bass.ds(it, 1), :].rearrange("p o d -> p (o d)")).then_inc(x_loaded, 16)
                    if kind & W1_UNIT:
                        sp.wait_ge(w_free, it + 1)
                        sp.dma_start(stage[:, :].rearrange("p (k h) -> p k h", k=KD),
                                     w1_v[:, bass.ds(it, 1), :, :].rearrange("p o k h -> p (o k) h")).then_inc(w_loaded, 16)
                    if kind & W2_UNIT:
                        sp.wait_ge(w_free, it + 1)
                        sp.dma_start(stage[:, :].rearrange("p (c d) -> p c d", c=HC),
                                     w2_v[:, bass.ds(it - X, 1), :, :].rearrange("p o c d -> p (o c) d")).then_inc(w_loaded, 16)
                    if kind & NODES:
                        sp.wait_ge(skip_ready, it + 1)
                        sp.dma_start(skip_v[:, bass.ds(it, 1), :].rearrange("p o d -> p (o d)"), st[:, :]).then_inc(skip_stored, 16)
            sp.wait_ge(skip_stored, 16 * (TPP + 1))

        @block.gpsimd
        def _(pool):
            pool.sem_inc(pay_free, 3 * 4)
            with pool.Fori(0, ITERS) as it:
                for b in range(2):
                    pool.wait_ge(idx_ready, it * 2 + (b + 1))
                    for q in range(2):
                        quad = it * 4 + (2 * b + q)
                        pool.wait_ge(pay_ready, quad + 3)
                        for s in range(4):
                            pool.wait_ge(tab_done[s], quad * 16 + 16)
                            pool.sem_inc(pay_free, 1)
                            col = 4 * q + s
                            pool.indirect_dma_start(
                                tables[s], bass.IndirectOffsetOnAxis(ap=idx[b][:, col:col + 1], axis=0),
                                pay[b][:, col, :], None, compute_op=ALU.add).then_inc(tab_done[s], 16)
            for s in range(TABLES):
                pool.wait_ge(tab_done[s], 16 * (1 + 4 * ITERS))

        @block.tensor
        def _(pe):
            for b in range(2):
                pe.sem_inc(attr_free[b], 1)

            def turn_attr(it, b):
                pe.wait_ge(attr_loaded[b], it * 16 + 16)
                for q in range(2):
                    mm = pe.transpose(bankA[:, q * P:(q + 1) * P], attr[b][:, q * P:(q + 1) * P], ident[:, :])
                mm.then_inc(attrT_psum, 1)

            def features(it, b):
                pe.wait_ge(attrT_ready, it * 2 + (b + 1))
                pe.sem_inc(attr_free[b], 1)
                for q in range(2):
                    o = bankB[:, q * 4 * A:(q + 1) * 4 * A]
                    pe.matmul(o, attrT[:, q, :], wtd[:, :, :].rearrange("p i a -> p (i a)"), start=True, stop=False)
                    mm = pe.matmul(o, ones[0:1, :], bt8[:, 0:4, :].rearrange("o i a -> o (i a)"), start=False, stop=True)
                mm.then_inc(tf_psum, 1)

            def turn_src(it, n):
                if n == 0:
                    pe.wait_ge(src_group, it + 1)
                for s in range(4):
                    mm = pe.transpose(bankC[n % 2][:, s * P:(s + 1) * P],
                                      srcg[:, 4 * n + s:4 * n + s + 1].to_broadcast([P, P]), ident[:, :])
                mm.then_inc(srcT_psum, 1)

            def add_same(it, n):
                b, q = n // 2, n % 2
                pe.wait_ge(same_ready, it * 4 + (n + 1))
                if q == 0:
                    pe.wait_ge(tf_ready, it * 2 + (b + 1))
                pe.wait_ge(pay_ready, it * 4 + (n + 1))
                for s in range(4):
                    mm = pe.matmul(bankD[n % 2][:, s * AC:(s + 1) * AC], same[n % 2][:, s, :],
                                   tf[b][:, 4 * q + s, :], start=True, stop=True)
                mm.then_inc(pay_psum, 1)

            def node(it):
                pe.wait_ge(xn_ready, it + 1)
                for k in range(KD):
                    mm = pe.transpose(bankN[:, k * P:(k + 1) * P], xn[:, k * P:(k + 1) * P], ident[:, :])
                mm.then_inc(xnT_psum, 1)
                pe.wait_ge(xnT_ready, it + 1)
                for k in range(KD):
                    mm = pe.matmul(bankN[0:A, 0:P], wdT[:, k, :], xnT[:, k, :], start=(k == 0), stop=(k == KD - 1))
                mm.then_inc(node_psum, 1)

            def expert_bias(it):
                pe.wait_ge(w_loaded, it * 16 + 16)
                for c in range(HC):
                    for k in range(KD):
                        mm = pe.matmul(bankW[:, c:c + 1], stage[:, k * H + c * P:k * H + (c + 1) * P],
                                       lnT[:, 1, bass.ds(it * KD + k, 1)], start=(k == 0), stop=(k == KD - 1))
                mm.then_inc(w_bias_psum, 1)

            for first, end, kind in segments:
                with pe.Fori(first, end) as it:
                    turn_attr(it, 0)
                    turn_src(it, 0)
                    turn_src(it, 1)
                    features(it, 0)
                    turn_attr(it, 1)
                    add_same(it, 0)
                    turn_src(it, 2)
                    add_same(it, 1)
                    turn_src(it, 3)
                    features(it, 1)
                    add_same(it, 2)
                    add_same(it, 3)
                    if kind & NODES:
                        node(it)
                    if kind & W1_UNIT:
                        expert_bias(it)

        @block.scalar
        def _(act):
            act.sem_inc(pay_ready, 2)

            def take_attr(it, b):
                act.wait_ge(attrT_psum, it * 2 + (b + 1))
                nc.scalar.copy(attrT[:, :, :].rearrange("p q e -> p (q e)"), bankA[:, 0:2 * P]).then_inc(attrT_ready, 1)

            def take_features(it, b):
                act.wait_ge(tf_psum, it * 2 + (b + 1))
                nc.scalar.activation(tf[b][:, :, 0:A], bankB[:, :].rearrange("p (j a) -> p j a", a=A),
                                     ACT.Relu).then_inc(tf_ready, 1)

            def take_sums(it, n):
                b, q = n // 2, n % 2
                act.wait_ge(pay_psum, it * 4 + (n + 1))
                act.wait_ge(pay_free, it * 16 + (4 * n + 4))
                nc.scalar.copy(pay[b][:, 4 * q:4 * q + 4, :].rearrange("p s a -> p (s a)"),
                               bankD[n % 2][:, 0:4 * AC]).then_inc(pay_ready, 1)

            for first, end, kind in segments:
                with act.Fori(first, end) as it:
                    take_attr(it, 0)
                    take_features(it, 0)
                    take_attr(it, 1)
                    take_sums(it, 0)
                    take_sums(it, 1)
                    take_features(it, 1)
                    if kind & NODES:
                        act.wait_ge(mv_ready, it * 2 + 2)
                        nc.scalar.activation(std[:, :], mv[:, 1:2], ACT.Sqrt, bias=eps[:, :]).then_inc(std_ready, 1)
                    take_sums(it, 2)
                    take_sums(it, 3)
                    if kind & NODES:
                        act.wait_ge(xnT_psum, it + 1)
                        nc.scalar.copy(xnT[:, :, :].rearrange("p k t -> p (k t)"), bankN[:, 0:D]).then_inc(xnT_ready, 1)
                        act.wait_ge(node_psum, it + 1)
                        nc.scalar.activation(nodeT[:, bass.ds(it * P, P)], bankN[0:A, 0:P], ACT.Relu,
                                             bias=bdn[:, :]).then_inc(node_ready, 1)

        @block.vector
        def _(dve):
            steps = Steps(dve, dve_step)
            dve.sem_inc(x_free, 1)
            dve.sem_inc(w_free, 1)
            dve.sem_inc(skip_stored, 16)

            def mark_same(it, n):
                b, q = n // 2, n % 2
                dve.wait_ge(srcT_psum, it * 4 + (n + 1))
                for s in range(4):
                    col = 4 * q + s
                    ins = dve.scalar_tensor_tensor(
                        out=same[n % 2][:, s, :], in0=bankC[n % 2][:, s * P:(s + 1) * P],
                        scalar=srcg[:, 4 * n + s:4 * n + s + 1], in1=upto[:, :], op0=ALU.is_equal, op1=ALU.mult,
                        accum_out=rank[b][:, col:col + 1])
                ins.then_inc(same_ready, 1)

            def rows(it, b):
                dve.wait_ge(same_ready, it * 4 + (2 * b + 2))
                steps.step(dve.tensor_scalar(away[b][:, :], srcg[:, b * GT:(b + 1) * GT], trash[:, :], None, ALU.subtract))
                steps.settle()
                steps.step(dve.scalar_tensor_tensor(out=away[b][:, :], in0=rank[b][:, :], scalar=1.0, in1=away[b][:, :],
                                                    op0=ALU.is_equal, op1=ALU.mult))
                steps.settle()
                dve.wait_ge(pay_free, it * 16 + (8 * b + 8))
                dve.tensor_scalar(idx[b][:, :], away[b][:, :], trash[:, :], None, ALU.add).then_inc(idx_ready, 1)

            for first, end, kind in segments:
                start = steps.n
                count = 4 + (3 if kind & NODES else 0) + (KD if kind & W1_UNIT else 0) + (1 if kind & W2_UNIT else 0)
                with dve.Fori(first, end) as it:
                    steps.n = (it - first) * count + start
                    dve.tensor_copy(srcg[:, :], srcf[:, bass.ds(it * (2 * GT), 2 * GT)]).then_inc(src_group, 1)
                    dve.wait_ge(src_group, it + 1)
                    mark_same(it, 0)
                    mark_same(it, 1)
                    rows(it, 0)
                    if kind & NODES:
                        dve.wait_ge(x_loaded, it * 16 + 16)
                        dve.bn_stats(stats[:, :], xt[:, :]).then_inc(mv_ready, 1)
                        dve.wait_ge(mv_ready, it * 2 + 1)
                        dve.sem_inc(between, 1)
                        dve.bn_aggr(mv[:, :], stats[:, :]).then_inc(mv_ready, 1)
                    mark_same(it, 2)
                    mark_same(it, 3)
                    rows(it, 1)
                    if kind & NODES:
                        dve.wait_ge(std_ready, it + 1)
                        steps.step(dve.reciprocal(rstd[:, :], std[:, :]))
                        steps.settle()
                        steps.step(dve.tensor_scalar(xt[:, :], xt[:, :], mv[:, 0:1], None, ALU.subtract))
                        steps.settle()
                        dve.tensor_scalar(xn[:, :], xt[:, :], rstd[:, :], None, ALU.mult).then_inc(xn_ready, 1)
                        dve.wait_ge(xn_ready, it + 1)
                        steps.step(dve.tensor_scalar(xt[:, :], xt[:, :], mv[:, 0:1], None, ALU.add))
                        steps.settle()
                        dve.wait_ge(skip_stored, it * 16 + 16)
                        dve.tensor_tensor(st[:, :], xt[:, :], xn[:, :], ALU.add).then_inc(skip_ready, 1)
                        dve.wait_ge(skip_ready, it + 1)
                        dve.sem_inc(x_free, 1)
                    if kind & W1_UNIT:
                        dve.wait_ge(w_loaded, it * 16 + 16)
                        for k in range(KD):
                            gain = lnT[:, 0, bass.ds(it * KD + k, 1)]
                            hi = w1s[:, bass.ds(it, 1), k, 0, :].rearrange("p o h -> p (o h)")
                            steps.step(dve.tensor_scalar(hi, stage[:, k * H:(k + 1) * H], gain, None, ALU.mult))
                            steps.settle()
                            lo = w1s[:, bass.ds(it, 1), k, 1, :].rearrange("p o h -> p (o h)")
                            ins = dve.scalar_tensor_tensor(out=lo, in0=stage[:, k * H:(k + 1) * H], scalar=gain, in1=hi,
                                                           op0=ALU.mult, op1=ALU.subtract).then_inc(w_cut, 1)
                        dve.wait_ge(w_cut, it * KD + KD)
                        dve.wait_ge(w_bias_psum, it + 1)
                        dve.tensor_tensor(b1p[:, bass.ds(it * HC, HC)], bankW[:, 0:HC],
                                          b1T[:, bass.ds(it * HC, HC)], ALU.add).then_inc(w_free, 1)
                    if kind & W2_UNIT:
                        dve.wait_ge(w_loaded, it * 16 + 16)
                        e = it - X
                        hi = w2s[:, bass.ds(e, 1), :, 0, :].rearrange("p o c d -> p (o c) d")
                        lo = w2s[:, bass.ds(e, 1), :, 1, :].rearrange("p o c d -> p (o c) d")
                        whole = stage[:, :].rearrange("p (c d) -> p c d", c=HC)
                        steps.step(dve.tensor_copy(hi, whole))
                        steps.settle()
                        dve.tensor_tensor(lo, whole, hi, ALU.subtract).then_inc(w_free, 1)
                steps.n = start + (end - first) * count


def node_update(nc, sb_, sem_, bank, env):
    g = env
    with ExitStack() as ctx:
        def sb(name, shape, dt=F32):
            return sb_(name, shape, dt, ctx)
        def sem(name):
            return sem_(name, ctx)
        tables, xtab, skip, out, ident, nodeT, parts_stored = (
            g[k] for k in ("tables", "xtab", "skip", "out", "ident", "nodeT", "parts_stored"))
        eps, eps2, wfa, wfb, wup, wr, brb, bfu, logits = (g[k] for k in ("eps", "eps2", "wfa", "wfb", "wup", "wr", "brb", "bfu", "logits"))
        tab = sb("tab", [P, TABLES, BATCH, AC])
        mean = sb("mean", [P, BATCH, A])
        cnt = sb("cnt", [P, BATCH])
        meanT = sb("meanT", [A, BATCH * P])
        fused = sb("fused", [A + 1, BATCH * P])
        x1 = [sb(f"x1_{i}", [P, BATCH, D]) for i in range(2)]
        xn2 = sb("xn2", [P, BATCH, D])
        parts = sb("parts", [P, BATCH, 2, D], BF16)
        xn2T = sb("xn2T", [P, 2, 2 * D])
        stats = sb("stats2", [P, BATCH, 6])
        mv = sb("mv2", [P, BATCH, 2])
        sd = sb("sd2", [P, 2, BATCH])
        rs = sb("rs2", [P, 2, BATCH])

        between = sem("between2")
        tab_loaded = sem("tab_loaded")
        tab_free = sem("tab_free")
        skip_loaded = [sem(f"skip_loaded{b}") for b in range(2)]
        x1_stored = sem("x1_stored")
        mean_ready = sem("mean_ready")
        meanT_psum = sem("meanT_psum")
        meanT_ready = sem("meanT_ready")
        fused_psum = sem("fused_psum")
        fused_ready = sem("fused_ready")
        up_psum = sem("up_psum")
        x1_ready = sem("x1_ready")
        mv_ready = sem("mv2_ready")
        sd_ready = sem("sd2_ready")
        xn2_ready = sem("xn2_ready")
        hi_ready = sem("hi_ready")
        parts_ready = sem("parts_ready")
        xn2T_psum = sem("xn2T_psum")
        xn2T_ready = sem("xn2T_ready")
        logit_psum = sem("logit_psum")
        logit_ready = sem("logit_ready")
        dve_step = sem("dve_step2")
        ones_ready = sem("ones_ready")
        x1_free = sem("x1_free")

        halves = [(0, 4), (4, BATCH)]
        pairs = [(j, min(j + 2, BATCH)) for j in range(0, BATCH, 2)]
        NPAIR = len(pairs)
        tab_v = [t[0:NPAD, :].rearrange("(p t) a -> p (t a)", p=P) for t in tables]
        skip_v = skip.rearrange("(p t) d -> p (t d)", p=P)
        out_v = out[0:NPAD, :].rearrange("(p t) d -> p (t d)", p=P)
        xtab_v = xtab[0:NPAD, :].rearrange("(p t) d -> p (t d)", p=P)

        with nc.Block() as block:

            def batches(eng, body):
                with eng.Fori(0, NB // 2) as it:
                    body(it * 2, 0, it)
                    body(it * 2 + 1, 1, it)
                body(NB - 1, 0, NB // 2)

            @block.sync
            def _(sp):
                def body(bt, b, it):
                    sp.wait_ge(tab_free, bt + 1)
                    for k in range(TABLES):
                        sp.dma_start(tab[:, k, :, :].rearrange("p t a -> p (t a)"),
                                     tab_v[k][:, bass.ds(bt * (BATCH * AC), BATCH * AC)]).then_inc(tab_loaded, 16)
                    sp.wait_ge(x1_free, bt + 1)
                    sp.dma_start(x1[b][:, :, :].rearrange("p t d -> p (t d)"),
                                 skip_v[:, bass.ds(bt * (BATCH * D), BATCH * D)]).then_inc(skip_loaded[b], 16)

                batches(sp, body)

            @block.gpsimd
            def _(pool):
                pool.sem_inc(tab_free, 1)
                pool.sem_inc(x1_free, 2)

                def body(bt, b, it):
                    pool.wait_ge(x1_ready, bt * NPAIR + NPAIR)
                    pool.dma_start(out_v[:, bass.ds(bt * (BATCH * D), BATCH * D)],
                                   x1[b][:, :, :].rearrange("p t d -> p (t d)")).then_inc(x1_stored, 16)
                    pool.wait_ge(parts_ready, bt + 1)
                    pool.dma_start(xtab_v[:, bass.ds(bt * (BATCH * 2 * D), BATCH * 2 * D)],
                                   parts[:, :, :, :].rearrange("p t i d -> p (t i d)")).then_inc(parts_stored, 16)
                    pool.wait_ge(x1_stored, bt * 16 + 16)
                    pool.wait_ge(xn2_ready, bt + 1)
                    pool.sem_inc(x1_free, 1)

                batches(pool, body)
                pool.wait_ge(parts_stored, 16 * (NB + 1))

            @block.tensor
            def _(pe):
                pe.wait_ge(ones_ready, 1)

                def body(bt, b, it):
                    pe.wait_ge(mean_ready, bt + 1)
                    pe.wait_ge(logit_ready, bt + 1)
                    pe.sem_inc(between, 1)
                    for h, (lo, hi) in enumerate(halves):
                        for j in range(lo, hi):
                            mm = pe.transpose(bank[h][0:A, (j - lo) * P:(j - lo + 1) * P], mean[:, j, :], ident[:, :])
                        mm.then_inc(meanT_psum, 1)
                    for h, (lo, hi) in enumerate(halves):
                        pe.wait_ge(meanT_ready, bt * 2 + (h + 1))
                        w = (hi - lo) * P
                        pe.matmul(bank[h][:, 0:w], wfa[:, :], nodeT[:, bass.ds(bt * (BATCH * P) + lo * P, w)],
                                  start=True, stop=False)
                        pe.matmul(bank[h][:, 0:w], wfb[:, :], meanT[:, lo * P:hi * P], start=False,
                                  stop=True).then_inc(fused_psum, 1)
                    for n, (lo, hi) in enumerate(pairs):
                        pe.wait_ge(fused_ready, bt * 2 + (1 if hi <= 4 else 2))
                        for j in range(lo, hi):
                            mm = pe.matmul(bank[2 + n][:, (j - lo) * D:(j - lo + 1) * D], fused[:, j * P:(j + 1) * P],
                                           wup[:, :], start=True, stop=True)
                        mm.then_inc(up_psum, 1)
                    pe.wait_ge(xn2_ready, bt + 1)
                    for n, (lo, hi) in enumerate(pairs):
                        if n >= 2:
                            pe.wait_ge(xn2T_ready, bt * NPAIR + (n - 1))
                        for j in range(lo, hi):
                            for k in range(KD):
                                o = (j - lo) * D + k * P
                                mm = pe.transpose(bank[6 + n % 2][:, o:o + P], xn2[:, j, k * P:(k + 1) * P], ident[:, :])
                        mm.then_inc(xn2T_psum, 1)
                        if n >= 1:
                            logit_pair(bt, n - 1)
                    logit_pair(bt, NPAIR - 1)

                def logit_pair(bt, n):
                    lo, hi = pairs[n]
                    pe.wait_ge(xn2T_ready, bt * NPAIR + (n + 1))
                    for j in range(lo, hi):
                        for k in range(KD):
                            o = (j - lo) * D + k * P
                            mm = pe.matmul(bank[0][:, j * X:(j + 1) * X], xn2T[:, n % 2, o:o + P], wr[:, k, :],
                                           start=(k == 0), stop=(k == KD - 1))
                    if n == NPAIR - 1:
                        mm.then_inc(logit_psum, 1)

                batches(pe, body)

            @block.scalar
            def _(act):
                def body(bt, b, it):
                    for h, (lo, hi) in enumerate(halves):
                        act.wait_ge(meanT_psum, bt * 2 + (h + 1))
                        nc.scalar.copy(meanT[:, lo * P:hi * P], bank[h][0:A, 0:(hi - lo) * P]).then_inc(meanT_ready, 1)
                    for h, (lo, hi) in enumerate(halves):
                        act.wait_ge(fused_psum, bt * 2 + (h + 1))
                        nc.scalar.activation(fused[0:A, lo * P:hi * P], bank[h][0:A, 0:(hi - lo) * P], ACT.Relu,
                                             bias=bfu[:, :]).then_inc(fused_ready, 1)
                    act.wait_ge(mv_ready, bt + 1)
                    nc.scalar.activation(sd[:, 0, :], mv[:, :, 1], ACT.Sqrt, bias=eps[:, :]).then_inc(sd_ready, 1)
                    nc.scalar.activation(sd[:, 1, :], mv[:, :, 1], ACT.Sqrt, bias=eps2[:, :],
                                         scale=1.0 + EPS).then_inc(sd_ready, 1)
                    act.wait_ge(xn2_ready, bt + 1)
                    for n, (lo, hi) in enumerate(pairs):
                        act.wait_ge(xn2T_psum, bt * NPAIR + (n + 1))
                        nc.scalar.copy(xn2T[:, n % 2, 0:(hi - lo) * D], bank[6 + n % 2][:, 0:(hi - lo) * D]).then_inc(xn2T_ready, 1)

                batches(act, body)

            @block.vector
            def _(dve):
                steps = Steps(dve, dve_step)
                dve.memset(fused[A:A + 1, :], 1.0).then_inc(ones_ready, 1)
                dve.sem_inc(logit_ready, 1)

                def body(bt, b, it):
                    dve.wait_ge(tab_loaded, bt * (16 * TABLES) + 16 * TABLES)
                    for k in range(1, TABLES):
                        steps.step(dve.tensor_tensor(tab[:, 0, :, :], tab[:, 0, :, :], tab[:, k, :, :], ALU.add))
                        steps.settle()
                    steps.step(dve.tensor_scalar(cnt[:, :], tab[:, 0, :, A], 1.0, None, ALU.max))
                    steps.settle()
                    steps.step(dve.reciprocal(cnt[:, :], cnt[:, :]))
                    steps.settle()
                    dve.tensor_tensor(mean[:, :, :], tab[:, 0, :, 0:A],
                                      cnt[:, :].rearrange("p (t o) -> p t o", o=1).to_broadcast([P, BATCH, A]),
                                      ALU.mult).then_inc(mean_ready, 1)
                    dve.wait_ge(mean_ready, bt + 1)
                    dve.sem_inc(tab_free, 1)
                    dve.wait_ge(skip_loaded[b], it * 16 + 16)
                    for n, (lo, hi) in enumerate(pairs):
                        dve.wait_ge(up_psum, bt * NPAIR + (n + 1))
                        dve.tensor_tensor(x1[b][:, lo:hi, :],
                                          bank[2 + n][:, 0:(hi - lo) * D].rearrange("p (t d) -> p t d", d=D),
                                          x1[b][:, lo:hi, :], ALU.add).then_inc(x1_ready, 1)
                    dve.wait_ge(x1_ready, bt * NPAIR + NPAIR)
                    for j in range(BATCH):
                        ins = dve.bn_stats(stats[:, j, :], x1[b][:, j, :])
                    steps.step(ins)
                    steps.settle()
                    dve.sem_inc(between, 1)
                    for j in range(BATCH):
                        ins = dve.bn_aggr(mv[:, j, :], stats[:, j, :])
                    ins.then_inc(mv_ready, 1)
                    dve.wait_ge(sd_ready, bt * 2 + 2)
                    steps.step(dve.reciprocal(rs[:, :, :], sd[:, :, :]))
                    steps.settle()
                    for j in range(BATCH):
                        ins = dve.tensor_scalar(xn2[:, j, :], x1[b][:, j, :], mv[:, j, 0:1], rs[:, 1, j:j + 1],
                                                ALU.subtract, ALU.mult)
                    ins.then_inc(xn2_ready, 1)
                    dve.wait_ge(xn2_ready, bt + 1)
                    steps.step(dve.tensor_tensor(rs[:, 0, :], rs[:, 0, :], sd[:, 1, :], ALU.mult))
                    dve.wait_ge(parts_stored, bt * 16 + 16)
                    steps.step(dve.tensor_copy(parts[:, :, 0, :], xn2[:, :, :]))
                    steps.settle()
                    dve.tensor_tensor(parts[:, :, 1, :], xn2[:, :, :], parts[:, :, 0, :], ALU.subtract).then_inc(parts_ready, 1)
                    dve.wait_ge(logit_psum, bt + 1)
                    steps.step(dve.tensor_tensor(stats_l[:, :, :], bank[0][:, 0:BATCH * X].rearrange("p (t e) -> p t e", e=X),
                                                 rs[:, 0, :].rearrange("p (t o) -> p t o", o=1).to_broadcast([P, BATCH, X]),
                                                 ALU.mult))
                    steps.settle()
                    dve.tensor_tensor(logits[:, bass.ds(bt * BATCH, BATCH), :], stats_l[:, :, :],
                                      brb[:, :].rearrange("p (o e) -> p o e", o=1).to_broadcast([P, BATCH, X]),
                                      ALU.add).then_inc(logit_ready, 1)

                count = (TABLES - 1) + 2 + 1 + 1 + 1 + 1 + 1
                stats_l = sb("scaled", [P, BATCH, X])
                with dve.Fori(0, NB // 2) as it:
                    for b in range(2):
                        steps.n = it * (2 * count) + b * count
                        body(it * 2 + b, b, it)
                steps.n = (NB - 1) * count
                body(NB - 1, 0, NB // 2)


def route_and_experts(nc, ctx, sb_, sem_, bank, env):
    g = env
    def sb(name, shape, dt=F32):
        return sb_(name, shape, dt, ctx)
    def sem(name):
        return sem_(name, ctx)
    rowmap, xtab, out, added, ones, before, logits, identb, w1s, w2s, b1p = (
        g[k] for k in ("rowmap", "xtab", "out", "added", "ones", "before", "logits", "identb", "w1s", "w2s", "b1p"))
    b2b = sb("b2b", [P, X, D])
    chosen = sb("chosen", [P, 2, TPP, X])
    both = sb("both", [P, TPP, X])
    tmp = sb("tmp_r", [P, TPP, X])
    tmp2 = sb("tmp_r2", [P, TPP, X])
    pos = sb("pos", [P, TPP, X])
    seq8 = sb("seq8", [P, TPP, X])
    top = sb("top", [P, 2, TPP])
    first = sb("first", [P, TPP])
    valid = sb("valid", [P, TPP])
    weight = sb("weight", [P, 2, TPP])
    where = sb("where", [P, 2, TPP])
    wherei = sb("wherei", [P, 2, 2, TPP], I32)
    wheref = sb("wheref", [P, 2, 2, TPP])
    away = sb("away_r", [P, 2, TPP])
    rowi = sb("rowi", [P, 2, TPP], I32)
    record = sb("record", [P, TPP, 2, 2], I32)
    ntile = sb("ntile", [P, 3, X])
    ntilei = sb("ntilei", [P, X], I32)
    tileno = sb("tileno", [1, MT, X])
    cover = sb("cover", [1, MT, X])
    exf = sb("exf", [1, MT])
    exi = sb("exi", [1, MT], I32)
    mp = sb("mp", [P, MT, 2], I32)

    between = sem("between3")
    made = sem("made")
    steps_sem = sem("dve_step3")
    rank_in = sem("rank_in")
    rank_psum = sem("rank_psum")
    tot_psum = sem("tot_psum")
    gap_ready = sem("gap_ready")
    exp_ready = sem("exp_ready")
    rows_ready = sem("rows_ready")
    scattered = sem("scattered")
    map_loaded = sem("map_loaded")
    b2_loaded = sem("b2_loaded")

    flat = lambda t: t[:, :, :].rearrange("p t e -> p (t e)")
    per_tok = lambda t: t.rearrange("p (t o) -> p t o", o=1).to_broadcast([P, TPP, X])

    with nc.Block() as block:

        @block.sync
        def _(sp):
            sp.dma_start(b2b[:, :, :].rearrange("p e d -> p (e d)"),
                         g["b2"].rearrange("(o e) d -> o (e d)", o=1).to_broadcast([P, X * D])).then_inc(b2_loaded, 16)
            sp.wait_ge(b2_loaded, 16)

        @block.gpsimd
        def _(pool):
            pool.iota(seq8[:, :, :], pattern=[[0, TPP], [1, X]], base=-X, channel_multiplier=0,
                      allow_small_or_imprecise_dtypes=True).then_inc(made, 1)
            pool.memset(valid[:, :], 1.0).then_inc(made, 1)
            for s in range(2):
                pool.iota(record[:, :, s, 0], pattern=[[1, TPP]], base=0, channel_multiplier=TPP).then_inc(made, 1)
                pool.iota(away[:, s, :], pattern=[[1, TPP]], base=P * MT + s * TPP, channel_multiplier=0,
                          allow_small_or_imprecise_dtypes=True).then_inc(made, 1)
            pool.iota(tileno[:, :, :], pattern=[[1, MT], [0, X]], base=0, channel_multiplier=0,
                      allow_small_or_imprecise_dtypes=True).then_inc(made, 1)
            pool.wait_ge(made, 7)
            pool.affine_select(out=valid[:, :], in_=valid[:, :], compare_op=ALU.is_ge, fill=0.0, base=N - 1,
                               pattern=[[-1, TPP]], channel_multiplier=-TPP).then_inc(made, 1)
            pool.wait_ge(rows_ready, 2)
            for t in range(TPP):
                for s in range(2):
                    pool.indirect_dma_start(rowmap, bass.IndirectOffsetOnAxis(ap=rowi[:, s, t:t + 1], axis=0),
                                            record[:, t, s, :], None).then_inc(scattered, 16)
            pool.wait_ge(scattered, 16 * 2 * TPP)
            pool.dma_start(mp[:, :, :].rearrange("p i c -> p (i c)"),
                           rowmap[0:P * MT, :].rearrange("(p i) c -> p (i c)", p=P)).then_inc(map_loaded, 16)
            pool.wait_ge(map_loaded, 16)

        @block.tensor
        def _(pe):
            pe.wait_ge(rank_in, 1)
            pe.matmul(bank[0][:, 0:TPP * X], before[:, :], flat(both), start=True, stop=True).then_inc(rank_psum, 1)
            pe.matmul(bank[1][:, 0:TPP * X], ones[:, :], flat(both), start=True, stop=True).then_inc(tot_psum, 1)

        @block.scalar
        def _(act):
            act.wait_ge(gap_ready, 1)
            nc.scalar.activation(weight[:, 1, :], weight[:, 0, :], ACT.Exp).then_inc(exp_ready, 1)

        @block.vector
        def _(dve):
            steps = Steps(dve, steps_sem)

            def do(ins):
                steps.step(ins)
                steps.settle()

            dve.wait_ge(made, 8)
            for s in range(2):
                do(dve.tensor_reduce(top[:, s, :], logits[:, :, :], AX_X, ALU.max))
                do(dve.tensor_tensor(tmp[:, :, :], logits[:, :, :], per_tok(top[:, s, :]), ALU.is_equal))
                do(dve.tensor_tensor(tmp[:, :, :], tmp[:, :, :], seq8[:, :, :], ALU.mult))
                do(dve.tensor_reduce(first[:, :], tmp[:, :, :], AX_X, ALU.min))
                do(dve.tensor_tensor(chosen[:, s, :, :], seq8[:, :, :], per_tok(first[:, :]), ALU.is_equal))
                if s == 0:
                    do(dve.scalar_tensor_tensor(out=flat(logits), in0=chosen[:, 0, :, :].rearrange("p t e -> p (t e)"),
                                                scalar=-BIG, in1=flat(logits), op0=ALU.mult, op1=ALU.add))
            do(dve.tensor_tensor(both[:, :, :], chosen[:, 0, :, :], chosen[:, 1, :, :], ALU.add))
            dve.tensor_tensor(both[:, :, :], both[:, :, :], per_tok(valid[:, :]), ALU.mult).then_inc(rank_in, 1)
            dve.tensor_tensor(weight[:, 0, :], top[:, 1, :], top[:, 0, :], ALU.subtract).then_inc(gap_ready, 1)
            dve.wait_ge(exp_ready, 1)
            do(dve.tensor_scalar(first[:, :], weight[:, 1, :], 1.0, None, ALU.add))
            do(dve.reciprocal(weight[:, 0, :], first[:, :]))
            do(dve.tensor_tensor(weight[:, 1, :], weight[:, 1, :], weight[:, 0, :], ALU.mult))
            for s in range(2):
                do(dve.tensor_copy(record[:, :, s, 1].bitcast(F32), weight[:, s, :]))
            dve.wait_ge(tot_psum, 1)
            do(dve.memset(tmp[:, 0:1, :], 0.0))
            do(dve.tensor_copy(tmp[:, 1:TPP, :], bank[1][:, 0:(TPP - 1) * X].rearrange("p (t e) -> p t e", e=X)))
            a, b = tmp, tmp2
            d = 1
            while d < TPP:
                do(dve.tensor_copy(b[:, 0:d, :], a[:, 0:d, :]))
                do(dve.tensor_tensor(b[:, d:TPP, :], a[:, d:TPP, :], a[:, 0:TPP - d, :], ALU.add))
                a, b = b, a
                d *= 2
            do(dve.tensor_tensor(pos[:, :, :], a[:, :, :], bank[0][:, 0:TPP * X].rearrange("p (t e) -> p t e", e=X), ALU.add))
            do(dve.tensor_tensor(ntile[:, 0, :], a[:, TPP - 1, :], bank[1][:, (TPP - 1) * X:TPP * X], ALU.add))
            do(dve.tensor_scalar(ntilei[:, :], ntile[:, 0, :], float(P - 1), None, ALU.add))
            do(dve.tensor_scalar(ntilei[:, :], ntilei[:, :], 7, None, ALU.arith_shift_right))
            do(dve.tensor_copy(ntile[:, 0, :], ntilei[:, :]))
            u, v = 0, 1
            d = 1
            while d < X:
                do(dve.tensor_copy(ntile[:, v, 0:d], ntile[:, u, 0:d]))
                do(dve.tensor_tensor(ntile[:, v, d:X], ntile[:, u, d:X], ntile[:, u, 0:X - d], ALU.add))
                u, v = v, u
                d *= 2
            do(dve.tensor_copy(ntile[:, 2, :], ntilei[:, :]))
            do(dve.tensor_tensor(ntile[:, v, :], ntile[:, u, :], ntile[:, 2, :], ALU.subtract))
            do(dve.tensor_scalar(ntile[:, v, :], ntile[:, v, :], float(P), None, ALU.mult))
            do(dve.tensor_tensor(pos[:, :, :], pos[:, :, :],
                                 ntile[:, v, :].rearrange("p (o e) -> p o e", o=1).to_broadcast([P, TPP, X]), ALU.add))
            do(dve.tensor_tensor(cover[:, :, :], tileno[:, :, :],
                                 ntile[0:1, u, :].rearrange("p (o e) -> p o e", o=1).to_broadcast([1, MT, X]), ALU.is_ge))
            do(dve.tensor_reduce(exf[:, :], cover[:, :, :], AX_X, ALU.add))
            do(dve.tensor_scalar(exi[:, :], exf[:, :], float(X - 1), None, ALU.min))
            for s in range(2):
                do(dve.tensor_tensor(tmp[:, :, :], pos[:, :, :], chosen[:, s, :, :], ALU.mult))
                do(dve.tensor_reduce(where[:, s, :], tmp[:, :, :], AX_X, ALU.add))
            do(dve.tensor_copy(rowi[:, :, :], where[:, :, :]))
            do(dve.tensor_scalar(wherei[:, 0, :, :], rowi[:, :, :], P - 1, None, ALU.bitwise_and))
            do(dve.tensor_scalar(wherei[:, 1, :, :], rowi[:, :, :], 7, None, ALU.arith_shift_right))
            do(dve.tensor_copy(wheref[:, :, :, :], wherei[:, :, :, :]))
            fl = lambda t: t.rearrange("p s t -> p (s t)")
            do(dve.scalar_tensor_tensor(out=fl(where[:, :, :]), in0=fl(wheref[:, 0, :, :]), scalar=float(MT),
                                        in1=fl(wheref[:, 1, :, :]), op0=ALU.mult, op1=ALU.add))
            do(dve.tensor_tensor(where[:, :, :], where[:, :, :], away[:, :, :], ALU.subtract))
            for s in range(2):
                do(dve.tensor_tensor(where[:, s, :], where[:, s, :], valid[:, :], ALU.mult))
            do(dve.tensor_tensor(where[:, :, :], where[:, :, :], away[:, :, :], ALU.add))
            dve.tensor_copy(rowi[:, :, :], where[:, :, :]).then_inc(rows_ready, 2)

    gidx = [sb(f"gidx{i}", [P, 1], I32) for i in range(2)]
    sidx = [sb(f"sidx{i}", [P, 1], I32) for i in range(2)]
    xg = [sb(f"xg{i}", [P, 2 * KD, P], BF16) for i in range(2)]
    xT = [sb(f"xT{i}", [P, 2 * KD, P], BF16) for i in range(2)]
    hid = [sb(f"hid{i}", [P, H]) for i in range(2)]
    hs = [sb(f"hs{i}", [P, 2, H], BF16) for i in range(2)]
    yb = [sb(f"yb{i}", [P, D]) for i in range(2)]
    gidx_ready = sem("gidx_ready")
    gathered = [sem(f"gathered{b}") for b in range(2)]
    xT_psum = sem("xT_psum")
    xT_ready = sem("xT_ready")
    h_psum = sem("h_psum")
    h_ready = sem("h_ready")
    cut_hi = sem("cut_hi")
    cut_ready = sem("cut_ready")
    y_psum = sem("y_psum")
    y_sum = sem("y_sum")
    y_ready = sem("y_ready")
    bankH = [bank[0:2], bank[2:4]]
    bankX, bankY = bank[4:6], bank[6:8]
    mpf = mp[:, :, :].bitcast(F32)
    last = TILES - 1
    PAIRS = last // 2
    assert TILES % 2 == 1

    with nc.Block() as block:

        @block.gpsimd
        def _(pool):

            def gather(i, b, n):
                pool.wait_ge(gidx_ready, i + 1)
                pool.sem_inc(between, 1)
                pool.indirect_dma_start(xg[b][:, :, :].rearrange("p k d -> p (k d)"), None, xtab,
                                        bass.IndirectOffsetOnAxis(ap=gidx[b][:, :], axis=0)).then_inc(gathered[b], 16)

            def scatter(i, b):
                pool.wait_ge(y_ready, i + 3)
                pool.wait_ge(added, i * 16 + 32)
                pool.sem_inc(between, 1)
                pool.indirect_dma_start(out, bass.IndirectOffsetOnAxis(ap=sidx[b][:, :], axis=0),
                                        yb[b][:, :], None, compute_op=ALU.add).then_inc(added, 16)

            gather(0, 0, 0)
            gather(1, 1, 0)
            with pool.Fori(0, PAIRS) as it:
                for b in range(2):
                    i = it * 2 + b
                    pool.wait_ge(xT_psum, i + 1)
                    gather(i + 2, b, 0)
                    scatter(i, b)
            scatter(last, 0)
            pool.wait_ge(added, 16 * (TILES + 2))
            pool.wait_ge(gathered[0], 16 * (PAIRS + 1))
            pool.wait_ge(gathered[1], 16 * (PAIRS + 1))

        @block.tensor
        def _(pe):
            def layer1(i, b, n):
                pe.wait_ge(gathered[b], n * 16 + 16)
                for k in range(2 * KD):
                    mm = pe.transpose(bankX[b][:, 0:D].bitcast(BF16)[:, k * P:(k + 1) * P], xg[b][:, k, :], identb[:, :])
                mm.then_inc(xT_psum, 1)
                e = pe.value_load(exi[0:1, bass.ds(i, 1)], min_val=0, max_val=X - 1)
                pe.wait_ge(xT_ready, i + 1)
                for c in range(HC):
                    o = bankH[b][c // 4][:, (c % 4) * P:(c % 4 + 1) * P]
                    steps = [(k, w, v) for k in range(KD) for w, v in ((0, 0), (0, 1), (1, 0))]
                    for n_, (k, w, v) in enumerate(steps):
                        lhs = w1s[:, bass.ds(e, 1), k, w, c * P:(c + 1) * P].rearrange("p o h -> p (o h)")
                        mm = pe.matmul(o, lhs, xT[b][:, v * KD + k, :], start=(n_ == 0), stop=(n_ == len(steps) - 1))
                    if c % 4 == 3:
                        mm.then_inc(h_psum, 1)

            def layer2(i, b):
                e = pe.value_load(exi[0:1, bass.ds(i, 1)], min_val=0, max_val=X - 1)
                pe.wait_ge(y_ready, i + 1)
                for c in range(HC):
                    if c % 4 == 0:
                        pe.wait_ge(cut_ready, i * 2 + (c // 4 + 1))
                    for n_, (v, w) in enumerate(((0, 0), (0, 1), (1, 0))):
                        rhs = w2s[:, bass.ds(e, 1), c, w, :].rearrange("p o d -> p (o d)")
                        mm = pe.matmul(bankY[b][:, 0:D], hs[b][:, v, c * P:(c + 1) * P], rhs,
                                       start=(c == 0 and n_ == 0), stop=(c == HC - 1 and n_ == 2))
                mm.then_inc(y_psum, 1)

            layer1(0, 0, 0)
            with pe.Fori(0, PAIRS) as it:
                for b in range(2):
                    layer1(it * 2 + (b + 1), 1 - b, it + b)
                    layer2(it * 2 + b, b)
            layer2(last, 0)

        @block.scalar
        def _(act):
            def gelu(i, b):
                e = act.value_load(exi[0:1, bass.ds(i, 1)], min_val=0, max_val=X - 1)
                for c in range(HC):
                    if c % 4 == 0:
                        act.wait_ge(h_psum, i * 2 + (c // 4 + 1))
                    ins = nc.scalar.activation(hid[b][:, c * P:(c + 1) * P],
                                               bankH[b][c // 4][:, (c % 4) * P:(c % 4 + 1) * P], ACT.Gelu,
                                               bias=b1p[:, bass.ds(e * HC + c, 1)])
                    if c % 4 == 3:
                        ins.then_inc(h_ready, 1)

            gelu(0, 0)
            with act.Fori(0, PAIRS) as it:
                for b in range(2):
                    gelu(it * 2 + (b + 1), 1 - b)

        @block.vector
        def _(dve):
            dve.sem_inc(y_ready, 2)

            def gather_rows(i, b):
                dve.tensor_copy(gidx[b][:, :], mp[:, bass.ds(i, 1), 0]).then_inc(gidx_ready, 1)

            def take_x(i, b):
                dve.wait_ge(xT_psum, i + 1)
                dve.tensor_copy(xT[b][:, :, :].rearrange("p k t -> p (k t)"),
                                bankX[b][:, 0:D].bitcast(BF16)).then_inc(xT_ready, 1)

            def cut(i, b):
                for h in range(2):
                    cols = slice(h * 512, h * 512 + 512)
                    dve.wait_ge(h_ready, i * 2 + (h + 1))
                    dve.tensor_copy(hs[b][:, 0, cols], hid[b][:, cols]).then_inc(cut_hi, 1)
                    dve.wait_ge(cut_hi, i * 2 + (h + 1))
                    dve.tensor_tensor(hs[b][:, 1, cols], hid[b][:, cols], hs[b][:, 0, cols],
                                      ALU.subtract).then_inc(cut_ready, 1)

            def finish(i, b):
                dve.wait_ge(added, i * 16 + 16)
                e = dve.value_load(exi[0:1, bass.ds(i, 1)], min_val=0, max_val=X - 1)
                dve.tensor_copy(sidx[b][:, :], mp[:, bass.ds(i, 1), 0]).then_inc(y_sum, 1)
                dve.wait_ge(y_psum, i + 1)
                dve.tensor_tensor(yb[b][:, :], bankY[b][:, 0:D],
                                  b2b[:, bass.ds(e, 1), :].rearrange("p o d -> p (o d)"), ALU.add).then_inc(y_sum, 1)
                dve.wait_ge(y_sum, i * 2 + 2)
                dve.tensor_scalar(yb[b][:, :], yb[b][:, :], mpf[:, bass.ds(i, 1), 1], None, ALU.mult).then_inc(y_ready, 1)

            gather_rows(0, 0)
            gather_rows(1, 1)
            take_x(0, 0)
            gather_rows(2, 0)
            cut(0, 0)
            with dve.Fori(0, PAIRS) as it:
                for b in range(2):
                    i = it * 2 + b
                    take_x(i + 1, 1 - b)
                    if b == 0:
                        gather_rows(i + 3, 1)
                    else:
                        gather_rows(i + 3, 0)
                    cut(i + 1, 1 - b)
                    finish(i, b)
            finish(last, 0)


_NAMES = {"x": "x", "src": "src", "edge": "edge_attr_32"} | {
    k: f"L0_gnn_{k}" for k in ("W_down", "b_down", "W_time", "b_time", "W_fusion", "b_fusion", "W_up", "b_up")} | {
    k: f"L0_ffn_{k}" for k in ("Wr", "br", "ln_g", "ln_b", "W1", "b1", "W2", "b2")}


def kernel(**inputs):
    import numpy as _np
    import concourse.bacc as _bacc
    from concourse import mybir as _mybir
    from concourse.bass_utils import run_bass_kernel_spmd as _run

    arrays = {k: _np.ascontiguousarray(inputs[name]) for k, name in _NAMES.items()}
    for k, rows, fill in (("x", NPAD, 0), ("edge", EPAD, 0), ("src", EPAD, N)):
        a = arrays[k]
        padded = _np.full((rows,) + a.shape[1:], fill, a.dtype)
        padded[:a.shape[0]] = a
        arrays[k] = padded
    nc = _bacc.Bacc("TRN2", target_bir_lowering=False, num_devices=1)
    args = {k: nc.dram_tensor(f"in_{k}", a.shape, _mybir.dt.from_np(a.dtype), kind="ExternalInput").ap()
            for k, a in arrays.items()}
    res = nc.dram_tensor("out_0_dram", (ROWS, D), F32, kind="ExternalOutput").ap()
    program(nc, **args, out=res)
    r = _run(nc, [{f"in_{k}": a for k, a in arrays.items()}], core_ids=[0])
    return r.results[0]["out_0_dram"][:N]
```

```python
from contextlib import ExitStack

import concourse.bass as bass
from concourse import mybir

P = 128
F32 = mybir.dt.float32
F16 = mybir.dt.float16
I32 = mybir.dt.int32
ALU = mybir.AluOpType
ACT = mybir.ActivationFunctionType
AX_X = mybir.AxisListType.X
EPS = 1e-5


def ceil_div(a, b):
    return -(-a // b)


N = 6250
D = 256
TPP = ceil_div(N, P)
NPAD = TPP * P
KD = D // P
E = 106250
FE = 32
GT = 8
EPP = ceil_div(ceil_div(E, P), 2 * GT) * 2 * GT
EPAD = EPP * P
ITERS = EPP // (2 * GT)
A = 64
AC = A + 1
X = 8
H = 1024
HC = H // P
SUB = 2
BR = SUB * P
BLOCKS = (2 * N + X * (BR - 1)) // BR
CAPB = ceil_div(N, BR)
CAP = CAPB * BR
MAP_BLOCKS = X * CAPB + BLOCKS
MAP_PP = MAP_BLOCKS * BR // P
MAP_ROWS = MAP_BLOCKS * BR + 2 * TPP
ROWS = NPAD + BR
TAB_ROWS = NPAD + P
TABLES = 4
BATCH = 7
NB = TPP // BATCH
BIG = 3.0e38
XS = 1024.0
TOP = 32768.0
XMAX = 16.0
TINY = 1e-30
assert XMAX * XMAX == D and XMAX * XS < TOP


class Steps:

    def __init__(self, eng, sem):
        self.eng, self.sem, self.n, self.taken = eng, sem, 0, 0

    def step(self, ins):
        ins.then_inc(self.sem, 1)
        self.n = self.n + 1
        self.taken += 1

    def settle(self):
        self.eng.wait_ge(self.sem, self.n)


def program(nc, x, src, edge, W_down, b_down, W_time, b_time, W_fusion, b_fusion, W_up, b_up,
            Wr, br, ln_g, ln_b, W1, b1, W2, b2, out):
    tables = [nc.dram_tensor(f"sums_{k}", [TAB_ROWS, AC], F32).ap() for k in range(TABLES)]
    xtab = nc.dram_tensor("xn_parts", [ROWS, 2 * D], F16).ap()
    skip = nc.dram_tensor("x_plus_xn", [NPAD, D], F32).ap()
    rowmap = nc.dram_tensor("row_map", [MAP_ROWS, 2], I32).ap()

    ctx = ExitStack()
    with ctx:
        def sb(name, shape, dt=F32, scope=ctx):
            return scope.enter_context(nc.sbuf_tensor(name, shape, dt))

        def sem(name, scope=ctx):
            return scope.enter_context(nc.semaphore(name))

        bank = [ctx.enter_context(nc.psum_tensor(f"bank{i}", [P, 512], F32)) for i in range(8)]

        w1s = sb("w1s", [P, X, KD, 2, H], F16)
        w2s = sb("w2s", [P, X, HC, 2, D], F16)
        b1p = sb("b1p", [P, X * HC])
        wsum = sb("wsum", [P, 2 * X])
        ident = sb("ident", [P, P])
        identb = sb("identb", [P, P], F16)
        ones = sb("ones", [P, P])
        before = sb("before", [P, P])
        trash = sb("trash", [P, 1])
        eps = sb("eps", [P, 1])
        eps2 = sb("eps2", [P, 1])
        wfT = sb("wfT", [2 * A, A])
        wup = sb("wup", [A + 1, D])
        wr = sb("wr", [P, KD, X])
        brb = sb("brb", [P, X])
        bfu = sb("bfu", [A, 1])
        count = sb("count", [P, X])
        added = sem("added")

        with ExitStack() as gnn:
            nodeT = sb("nodeT", [2 * A, TPP * P], F32, gnn)
            with ExitStack() as one:
                edges_and_nodes(nc, one, sb, sem, bank, locals())
            node_update(nc, sb, sem, bank, locals())
        with ExitStack() as moe:
            experts(nc, moe, sb, sem, bank, locals())


def edges_and_nodes(nc, ctx, sb_, sem_, bank, env):
    g = env
    def sb(name, shape, dt=F32):
        return sb_(name, shape, dt, ctx)
    def sem(name):
        return sem_(name, ctx)
    x, src, edge, tables, xtab, skip, rowmap, out = (g[k] for k in ("x", "src", "edge", "tables", "xtab", "skip", "rowmap", "out"))
    w1s, w2s, b1p, wsum, ident, identb, ones, before, trash = (
        g[k] for k in ("w1s", "w2s", "b1p", "wsum", "ident", "identb", "ones", "before", "trash"))
    eps, eps2, wfT, wup, wr, brb, bfu, nodeT = (g[k] for k in ("eps", "eps2", "wfT", "wup", "wr", "brb", "bfu", "nodeT"))

    upto = sb("upto", [P, P])
    srci = sb("srci", [P, EPP], I32)
    srcf = sb("srcf", [P, EPP])
    srcg = sb("srcg", [P, 2 * GT])
    wd_raw = sb("wd_raw", [A, D])
    wt_raw = sb("wt_raw", [A, 4, FE])
    wf_raw = sb("wf_raw", [A, 2 * A])
    wu_raw = sb("wu_raw", [P, KD, A])
    ln_raw = sb("ln_raw", [X * KD, 2, P])
    b1_raw = sb("b1_raw", [X * HC, P])
    bdn = sb("bdn", [A, 1])
    bt_raw = sb("bt_raw", [1, A])
    wdT = sb("wdT", [P, KD, A])
    wtd = sb("wtd", [P, 4, A])
    bt8 = sb("bt8", [1, GT, A])
    lnT = sb("lnT", [P, 2, X * KD])
    b1T = sb("b1T", [P, X * HC])
    attr = [sb(f"attr{i}", [P, GT * FE]) for i in range(2)]
    attrT = sb("attrT", [P, 2, P])
    tf = [sb(f"tf{i}", [P, GT, AC]) for i in range(2)]
    same = [sb(f"same{i}", [P, 4, P]) for i in range(2)]
    rank = [sb(f"rank{i}", [P, GT]) for i in range(2)]
    away = [sb(f"away{i}", [P, GT]) for i in range(2)]
    idx = [sb(f"idx{i}", [P, GT], I32) for i in range(4)]
    pay = [sb(f"pay{i}", [P, GT, AC]) for i in range(4)]
    rowmax = sb("rowmax", [P, KD])
    wscale = sb("wscale", [P, 1])
    gains = sb("gains", [P, KD])
    xt = sb("xt", [P, D])
    xn = sb("xn", [P, D])
    st = sb("st", [P, D])
    xnT = sb("xnT", [P, KD, P])
    stats = sb("stats", [P, 6])
    mv = sb("mv", [P, 2])
    std = sb("std", [P, 1])
    rstd = sb("rstd", [P, 1])
    stage = sb("stage", [P, KD, H])
    zero = stage[:, 0, 0:650]
    preset = stage[:, 1, 0:2 * MAP_PP].bitcast(I32).rearrange("p (i c) -> p i c", c=2)

    between = sem("between")
    small_loaded = sem("small_loaded")
    init_stored = sem("init_stored")
    zeroed = sem("zeroed")
    trash_stored = sem("trash_stored")
    filled = sem("filled")
    ready = sem("ready")
    prep_psum = sem("prep_psum")
    prep_done = sem("prep_done")
    src_loaded = sem("src_loaded")
    src_float = sem("src_float")
    added = g["added"]
    tab_done = [sem(f"tab_done{k}") for k in range(TABLES)]

    with nc.Block() as block:
        small = [
            (wd_raw[:, :], g["W_down"]), (wf_raw[:, :], g["W_fusion"]),
            (wu_raw[:, :, :], g["W_up"].rearrange("(k p) a -> p k a", p=P)),
            (ln_raw[:, 0, :], g["ln_g"].rearrange("e (k p) -> (e k) p", p=P)),
            (ln_raw[:, 1, :], g["ln_b"].rearrange("e (k p) -> (e k) p", p=P)),
            (b1_raw[:, :], g["b1"].rearrange("e (c p) -> (e c) p", p=P)),
            (bdn[:, :], g["b_down"].rearrange("(a o) -> a o", o=1)),
            (bfu[:, :], g["b_fusion"].rearrange("(a o) -> a o", o=1)),
            (bt_raw[:, :], g["b_time"].rearrange("(o a) -> o a", o=1)),
            (wup[A:A + 1, :], g["b_up"].rearrange("(o d) -> o d", o=1)),
            (wr[:, :, :], g["Wr"].rearrange("(k p) e -> p k e", p=P)),
            (brb[:, :], g["br"].rearrange("(o e) -> o e", o=1).to_broadcast([P, X])),
        ] + [(wt_raw[:, i, :], g["W_time"]) for i in range(4)]

        @block.sync
        def _(sp):
            sp.dma_start(srci[:, :], src.rearrange("(p j) -> p j", p=P)).then_inc(src_loaded, 16)
            for dst, s in small:
                sp.dma_start(dst, s).then_inc(small_loaded, 16)
            sp.wait_ge(filled, 1)
            sp.dma_start(rowmap[0:MAP_BLOCKS * BR, :].rearrange("(p i) c -> p (i c)", p=P),
                         preset[:, :, :].rearrange("p i c -> p (i c)")).then_inc(init_stored, 16)
            sp.wait_ge(small_loaded, 16 * len(small))
            sp.wait_ge(init_stored, 16)

        @block.gpsimd
        def _(pool):
            pool.memset(zero[:, :], 0.0).then_inc(zeroed, 1)
            pool.wait_ge(zeroed, 1)
            for k in range(TABLES):
                rows = TAB_ROWS // P * AC
                pool.dma_start(
                    tables[k].rearrange("(p r) a -> p (r a)", p=P).rearrange("p (u v) -> p u v", v=650),
                    zero[:, :].rearrange("p (o v) -> p o v", o=1).to_broadcast([P, rows // 650, 650]),
                ).then_inc(tab_done[k], 16)
            for first, rows in ((NPAD, P), (NPAD + P, A), (NPAD + P + A, A)):
                pool.dma_start(out[first:first + rows, :], zero[0:rows, 0:D]).then_inc(added, 16)
            pool.dma_start(xtab[NPAD:ROWS, :].rearrange("(p u) d -> p (u d)", p=P),
                           zero[:, 0:SUB * D].bitcast(F16)).then_inc(trash_stored, 16)
            pool.wait_ge(trash_stored, 16)
            pool.memset(ident[:, :], 0.0).then_inc(ready, 1)
            pool.memset(upto[:, :], 1.0).then_inc(ready, 1)
            pool.memset(before[:, :], 1.0).then_inc(ready, 1)
            pool.memset(ones[:, :], 1.0).then_inc(ready, 1)
            pool.memset(preset[:, :, :], 0).then_inc(ready, 1)
            pool.memset(eps[:, :], EPS).then_inc(ready, 1)
            pool.memset(eps2[:, :], EPS * EPS).then_inc(ready, 1)
            pool.iota(trash[:, :], pattern=[[0, 1]], base=NPAD, channel_multiplier=1,
                      allow_small_or_imprecise_dtypes=True).then_inc(ready, 1)
            pool.wait_ge(ready, 8)
            pool.iota(preset[:, :, 0], pattern=[[1, MAP_PP]], base=0, channel_multiplier=MAP_PP).then_inc(ready, 1)
            pool.affine_select(out=ident[:, :], in_=ident[:, :], compare_op=ALU.not_equal, fill=1.0,
                               base=0, pattern=[[-1, P]], channel_multiplier=1).then_inc(ready, 1)
            pool.affine_select(out=upto[:, :], in_=upto[:, :], compare_op=ALU.is_ge, fill=0.0,
                               base=0, pattern=[[-1, P]], channel_multiplier=1).then_inc(ready, 1)
            pool.affine_select(out=before[:, :], in_=before[:, :], compare_op=ALU.is_ge, fill=0.0,
                               base=-1, pattern=[[1, P]], channel_multiplier=-1).then_inc(ready, 1)

        @block.tensor
        def _(pe):
            pe.wait_ge(ready, 12)
            pe.wait_ge(small_loaded, 16 * len(small))
            for k in range(KD):
                pe.transpose(bank[0][:, k * A:(k + 1) * A], wd_raw[:, k * P:(k + 1) * P], ident[0:A, 0:A])
            pe.transpose(bank[0][:, 128:128 + A], wt_raw[:, :, :].rearrange("a i f -> a (i f)"),
                         ident[0:A, 0:A]).then_inc(prep_psum, 1)
            pe.transpose(bank[1][:, 0:A], wf_raw[:, :], ident[0:A, 0:A])
            for k in range(KD):
                mm = pe.transpose(bank[1][0:A, 128 + k * P:128 + (k + 1) * P], wu_raw[:, k, :], ident[:, :])
            mm.then_inc(prep_psum, 1)
            for i in range(2):
                pe.transpose(bank[2][:, i * X * KD:(i + 1) * X * KD], ln_raw[:, i, :],
                             ident[0:X * KD, 0:X * KD])
            pe.transpose(bank[2][:, 64:64 + X * HC], b1_raw[:, :], ident[0:X * HC, 0:X * HC]).then_inc(prep_psum, 1)

        @block.vector
        def _(dve):
            dve.memset(wtd[:, :, :], 0.0).then_inc(prep_done, 1)
            for b in range(2):
                dve.memset(tf[b][:, :, A:AC], 1.0).then_inc(prep_done, 1)
            dve.wait_ge(prep_done, 3)
            dve.wait_ge(src_loaded, 16)
            dve.tensor_copy(srcf[:, :], srci[:, :]).then_inc(src_float, 1)
            dve.wait_ge(ready, 12)
            dve.tensor_copy(identb[:, :], ident[:, :]).then_inc(prep_done, 1)
            dve.tensor_scalar(preset[:, :, 0], preset[:, :, 0], BR - 1, None, ALU.bitwise_and).then_inc(prep_done, 1)
            dve.wait_ge(prep_done, 5)
            dve.tensor_scalar(preset[:, :, 0], preset[:, :, 0], NPAD, None, ALU.add).then_inc(filled, 1)
            dve.wait_ge(prep_psum, 1)
            dve.tensor_copy(wdT[:, :, :].rearrange("p k a -> p (k a)"), bank[0][:, 0:KD * A]).then_inc(prep_done, 1)
            for i in range(4):
                dve.tensor_copy(wtd[i * FE:(i + 1) * FE, i, :],
                                bank[0][i * FE:(i + 1) * FE, 128:128 + A]).then_inc(prep_done, 1)
            dve.wait_ge(small_loaded, 16 * len(small))
            dve.tensor_copy(bt8[:, :, :], bt_raw[:, :].rearrange("o (u a) -> o u a", u=1).to_broadcast([1, GT, A])).then_inc(prep_done, 1)
            dve.wait_ge(prep_psum, 2)
            dve.tensor_copy(wfT[:, :], bank[1][:, 0:A]).then_inc(prep_done, 1)
            dve.tensor_copy(wup[0:A, :], bank[1][0:A, 128:128 + D]).then_inc(prep_done, 1)
            dve.wait_ge(prep_psum, 3)
            dve.tensor_copy(lnT[:, :, :].rearrange("p i c -> p (i c)"), bank[2][:, 0:2 * X * KD]).then_inc(prep_done, 1)
            dve.tensor_copy(b1T[:, :], bank[2][:, 64:64 + X * HC]).then_inc(prep_done, 1)

    attr_loaded = [sem(f"attr_loaded{b}") for b in range(2)]
    attr_free = [sem(f"attr_free{b}") for b in range(2)]
    src_group = sem("src_group")
    attrT_psum = sem("attrT_psum")
    attrT_ready = sem("attrT_ready")
    tf_psum = sem("tf_psum")
    tf_ready = sem("tf_ready")
    srcT_psum = sem("srcT_psum")
    same_ready = sem("same_ready")
    idx_ready = sem("idx_ready")
    pay_psum = sem("pay_psum")
    pay_ready = sem("pay_ready")
    pay_free = sem("pay_free")
    x_loaded = sem("x_loaded")
    x_free = sem("x_free")
    mv_ready = sem("mv_ready")
    std_ready = sem("std_ready")
    xn_ready = sem("xn_ready")
    skip_ready = sem("skip_ready")
    skip_stored = sem("skip_stored")
    xnT_psum = sem("xnT_psum")
    xnT_ready = sem("xnT_ready")
    node_psum = sem("node_psum")
    node_ready = sem("node_ready")
    w_loaded = sem("w_loaded")
    w_cut = sem("w_cut")
    w_bias_psum = sem("w_bias_psum")
    w_free = sem("w_free")
    rowmax_ready = sem("rowmax_ready")
    dve_step = sem("dve_step")

    NODES, W1_UNIT, W2_UNIT = 1, 2, 4
    segments = [(0, X, NODES | W1_UNIT), (X, 2 * X, NODES | W2_UNIT), (2 * X, TPP - 1, NODES), (TPP - 1, TPP, NODES)] + [
        (i, i + 1, 0) for i in range(TPP, ITERS)]
    assert X % 2 == 0 and TPP % 2 == 1

    def iterations(eng, body):
        for first, end, kind in segments:
            if end - first == 1:
                body(first, first % 2, kind)
            else:
                with eng.Fori(0, (end - first) // 2) as turn:
                    for u in range(2):
                        body(turn * 2 + (first + u), (first + u) % 2, kind)
    edge_v = edge.rearrange("(p j) f -> p (j f)", p=P)
    x_v = x.rearrange("(p t) d -> p t d", p=P)
    skip_v = skip.rearrange("(p t) d -> p t d", p=P)
    w1_v = g["W1"].rearrange("e (k p) h -> p e k h", p=P)
    w2_v = g["W2"].rearrange("e (c p) d -> p e c d", p=P)
    bankA, bankB, bankN, bankW = bank[0], bank[1], bank[6], bank[7]
    bankC, bankD = bank[2:4], bank[4:6]
    GROUPS = len(pay)
    QUADS = 2 * GROUPS

    with nc.Block() as block:

        @block.sync
        def _(sp):
            def body(it, u, kind):
                for b in range(2):
                    sp.wait_ge(attr_free[b], it + 1)
                    sp.dma_start(attr[b][:, :], edge_v[:, bass.ds(it * (2 * GT * FE) + b * GT * FE, GT * FE)]
                                 ).then_inc(attr_loaded[b], 16)
                if kind & NODES:
                    sp.wait_ge(x_free, it + 1)
                    sp.dma_start(xt[:, :], x_v[:, bass.ds(it, 1), :].rearrange("p o d -> p (o d)")).then_inc(x_loaded, 16)
                if kind & W1_UNIT:
                    sp.wait_ge(w_free, it + 1)
                    sp.dma_start(stage[:, :, :], w1_v[:, bass.ds(it, 1), :, :].rearrange("p o k h -> p (o k) h")
                                 ).then_inc(w_loaded, 16)
                if kind & W2_UNIT:
                    sp.wait_ge(w_free, it + 1)
                    sp.dma_start(stage[:, :, :].rearrange("p k (c d) -> p (k c) d", d=D),
                                 w2_v[:, bass.ds(it - X, 1), :, :].rearrange("p o c d -> p (o c) d")
                                 ).then_inc(w_loaded, 16)
                if kind & NODES:
                    sp.wait_ge(skip_ready, it + 1)
                    sp.dma_start(skip_v[:, bass.ds(it, 1), :].rearrange("p o d -> p (o d)"), st[:, :]).then_inc(skip_stored, 16)

            iterations(sp, body)
            sp.wait_ge(skip_stored, 16 * (TPP + 1))

        @block.gpsimd
        def _(pool):
            pool.sem_inc(pay_free, 4 * (QUADS - 1))

            def body(it, u):
                for b in range(2):
                    pool.wait_ge(idx_ready, it * 2 + (b + 1))
                    for q in range(2):
                        quad = it * 4 + (2 * b + q)
                        pool.wait_ge(pay_ready, quad + 3)
                        for s in range(4):
                            pool.wait_ge(tab_done[s], quad * 16 + 16)
                            pool.sem_inc(pay_free, 1)
                            col = 4 * q + s
                            pool.indirect_dma_start(
                                tables[s], bass.IndirectOffsetOnAxis(ap=idx[2 * u + b][:, col:col + 1], axis=0),
                                pay[2 * u + b][:, col, :], None, compute_op=ALU.add).then_inc(tab_done[s], 16)

            with pool.Fori(0, ITERS // 2) as turn:
                for u in range(2):
                    body(turn * 2 + u, u)
            for s in range(TABLES):
                pool.wait_ge(tab_done[s], 16 * (1 + 4 * ITERS))

        @block.tensor
        def _(pe):
            for b in range(2):
                pe.sem_inc(attr_free[b], 1)

            def turn_attr(it, b):
                pe.wait_ge(attr_loaded[b], it * 16 + 16)
                for q in range(2):
                    mm = pe.transpose(bankA[:, q * P:(q + 1) * P], attr[b][:, q * P:(q + 1) * P], ident[:, :])
                mm.then_inc(attrT_psum, 1)

            def features(it, b):
                pe.wait_ge(attrT_ready, it * 2 + (b + 1))
                pe.sem_inc(attr_free[b], 1)
                for q in range(2):
                    o = bankB[:, q * 4 * A:(q + 1) * 4 * A]
                    pe.matmul(o, attrT[:, q, :], wtd[:, :, :].rearrange("p i a -> p (i a)"), start=True, stop=False)
                    mm = pe.matmul(o, ones[0:1, :], bt8[:, 0:4, :].rearrange("o i a -> o (i a)"), start=False, stop=True)
                mm.then_inc(tf_psum, 1)

            def turn_src(it, n):
                if n == 0:
                    pe.wait_ge(src_group, it + 1)
                for s in range(4):
                    mm = pe.transpose(bankC[n % 2][:, s * P:(s + 1) * P],
                                      srcg[:, 4 * n + s:4 * n + s + 1].to_broadcast([P, P]), ident[:, :])
                mm.then_inc(srcT_psum, 1)

            def add_same(it, n):
                b, q = n // 2, n % 2
                pe.wait_ge(same_ready, it * 4 + (n + 1))
                if q == 0:
                    pe.wait_ge(tf_ready, it * 2 + (b + 1))
                pe.wait_ge(pay_ready, it * 4 + (n + 1))
                for s in range(4):
                    mm = pe.matmul(bankD[n % 2][:, s * AC:(s + 1) * AC], same[n % 2][:, s, :],
                                   tf[b][:, 4 * q + s, :], start=True, stop=True)
                mm.then_inc(pay_psum, 1)

            def node(it):
                pe.wait_ge(xn_ready, it + 1)
                for k in range(KD):
                    mm = pe.transpose(bankN[:, k * P:(k + 1) * P], xn[:, k * P:(k + 1) * P], ident[:, :])
                mm.then_inc(xnT_psum, 1)
                pe.wait_ge(xnT_ready, it + 1)
                for k in range(KD):
                    mm = pe.matmul(bankN[0:A, 0:P], wdT[:, k, :], xnT[:, k, :], start=(k == 0), stop=(k == KD - 1))
                mm.then_inc(node_psum, 1)

            def weight_sums(it, kind):
                pe.wait_ge(w_loaded, it * 16 + 16)
                if kind & W1_UNIT:
                    for c in range(HC):
                        for k in range(KD):
                            pe.matmul(bankW[:, c:c + 1], stage[:, k, c * P:(c + 1) * P],
                                      lnT[:, 1, bass.ds(it * KD + k, 1)], start=(k == 0), stop=(k == KD - 1))
                pe.wait_ge(rowmax_ready, it + 1)
                pe.matmul(bankW[:, HC:HC + KD], ones[:, :], rowmax[:, :], start=True, stop=True).then_inc(w_bias_psum, 1)

            def body(it, u, kind):
                turn_attr(it, 0)
                turn_src(it, 0)
                turn_src(it, 1)
                features(it, 0)
                turn_attr(it, 1)
                add_same(it, 0)
                turn_src(it, 2)
                add_same(it, 1)
                turn_src(it, 3)
                features(it, 1)
                if kind & (W1_UNIT | W2_UNIT):
                    weight_sums(it, kind)
                add_same(it, 2)
                add_same(it, 3)
                if kind & NODES:
                    node(it)

            iterations(pe, body)

        @block.scalar
        def _(act):
            act.sem_inc(pay_ready, 2)

            def take_attr(it, b):
                act.wait_ge(attrT_psum, it * 2 + (b + 1))
                nc.scalar.copy(attrT[:, :, :].rearrange("p q e -> p (q e)"), bankA[:, 0:2 * P]).then_inc(attrT_ready, 1)

            def take_features(it, b):
                act.wait_ge(tf_psum, it * 2 + (b + 1))
                nc.scalar.activation(tf[b][:, :, 0:A], bankB[:, :].rearrange("p (j a) -> p j a", a=A),
                                     ACT.Relu).then_inc(tf_ready, 1)

            def take_sums(it, u, n):
                b, q = n // 2, n % 2
                act.wait_ge(pay_psum, it * 4 + (n + 1))
                act.wait_ge(pay_free, it * 16 + (4 * n + 4))
                nc.scalar.copy(pay[2 * u + b][:, 4 * q:4 * q + 4, :].rearrange("p s a -> p (s a)"),
                               bankD[n % 2][:, 0:4 * AC]).then_inc(pay_ready, 1)

            def body(it, u, kind):
                take_attr(it, 0)
                take_features(it, 0)
                take_attr(it, 1)
                take_sums(it, u, 0)
                take_sums(it, u, 1)
                take_features(it, 1)
                if kind & NODES:
                    act.wait_ge(mv_ready, it * 2 + 2)
                    nc.scalar.activation(std[:, :], mv[:, 1:2], ACT.Sqrt, bias=eps[:, :]).then_inc(std_ready, 1)
                take_sums(it, u, 2)
                take_sums(it, u, 3)
                if kind & NODES:
                    act.wait_ge(xnT_psum, it + 1)
                    nc.scalar.copy(xnT[:, :, :].rearrange("p k t -> p (k t)"), bankN[:, 0:D]).then_inc(xnT_ready, 1)
                    act.wait_ge(node_psum, it + 1)
                    nc.scalar.activation(nodeT[0:A, bass.ds(it * P, P)], bankN[0:A, 0:P], ACT.Relu,
                                         bias=bdn[:, :]).then_inc(node_ready, 1)

            iterations(act, body)

        @block.vector
        def _(dve):
            steps = Steps(dve, dve_step)

            def do(ins):
                steps.step(ins)
                steps.settle()

            dve.sem_inc(x_free, 1)
            dve.sem_inc(w_free, 1)
            dve.sem_inc(skip_stored, 16)

            def mark_same(it, n):
                b, q = n // 2, n % 2
                dve.wait_ge(srcT_psum, it * 4 + (n + 1))
                for s in range(4):
                    col = 4 * q + s
                    ins = dve.scalar_tensor_tensor(
                        out=same[n % 2][:, s, :], in0=bankC[n % 2][:, s * P:(s + 1) * P],
                        scalar=srcg[:, 4 * n + s:4 * n + s + 1], in1=upto[:, :], op0=ALU.is_equal, op1=ALU.mult,
                        accum_out=rank[b][:, col:col + 1])
                ins.then_inc(same_ready, 1)

            def rows(it, u, b):
                dve.wait_ge(same_ready, it * 4 + (2 * b + 2))
                do(dve.tensor_scalar(away[b][:, :], srcg[:, b * GT:(b + 1) * GT], trash[:, :], None, ALU.subtract))
                do(dve.scalar_tensor_tensor(out=away[b][:, :], in0=rank[b][:, :], scalar=1.0, in1=away[b][:, :],
                                            op0=ALU.is_equal, op1=ALU.mult))
                dve.wait_ge(pay_free, it * 16 + (8 * b + 8))
                dve.tensor_scalar(idx[2 * u + b][:, :], away[b][:, :], trash[:, :], None, ALU.add).then_inc(idx_ready, 1)

            def greatest_weights(it, kind):
                dve.wait_ge(w_loaded, it * 16 + 16)
                do(dve.tensor_reduce(gains[:, :], stage[:, :, :], AX_X, ALU.max, apply_absolute_value=True))
                if kind & W1_UNIT:
                    do(dve.tensor_tensor(gains[:, :], gains[:, :], lnT[:, 0, bass.ds(it * KD, KD)], ALU.mult))
                dve.scalar_tensor_tensor(out=rowmax[:, :], in0=gains[:, :], scalar=-1.0, in1=gains[:, :],
                                         op0=ALU.mult, op1=ALU.max).then_inc(rowmax_ready, 1)

            def scale_and_cut(it, kind):
                dve.wait_ge(w_bias_psum, it + 1)
                do(dve.tensor_reduce(wscale[:, :], bankW[:, HC:HC + KD], AX_X, ALU.add))
                do(dve.tensor_scalar(wscale[:, :], wscale[:, :], TINY, None, ALU.max))
                do(dve.tensor_copy(wsum[:, bass.ds(it, 1)], wscale[:, :]))
                do(dve.reciprocal(wscale[:, :], wscale[:, :]))
                do(dve.tensor_scalar(wscale[:, :], wscale[:, :], TOP, None, ALU.mult))
                if kind & W1_UNIT:
                    do(dve.tensor_scalar(gains[:, :], lnT[:, 0, bass.ds(it * KD, KD)], wscale[:, :], None, ALU.mult))
                for k in range(KD):
                    if kind & W1_UNIT:
                        gain, tab, at = gains[:, k:k + 1], w1s[:, bass.ds(it, 1), k, :, :].rearrange("p o i h -> p (o i) h"), it
                        hi, lo, whole = tab[:, 0, :], tab[:, 1, :], stage[:, k, :]
                    else:
                        half = slice(k * HC // KD, (k + 1) * HC // KD)
                        tab = w2s[:, bass.ds(it - X, 1), half, :, :].rearrange("p o c i d -> p (o c) i d")
                        gain, hi, lo = wscale[:, :], tab[:, :, 0, :], tab[:, :, 1, :]
                        whole = stage[:, k, :].rearrange("p (c d) -> p c d", d=D)
                    do(dve.tensor_scalar(hi, whole, gain, None, ALU.mult))
                    do(dve.scalar_tensor_tensor(out=lo, in0=whole, scalar=gain, in1=hi, op0=ALU.mult, op1=ALU.subtract))
                if kind & W1_UNIT:
                    do(dve.tensor_tensor(b1p[:, bass.ds(it * HC, HC)], bankW[:, 0:HC],
                                         b1T[:, bass.ds(it * HC, HC)], ALU.add))
                dve.sem_inc(w_free, 1)

            def take_node(it):
                dve.wait_ge(x_loaded, it * 16 + 16)
                dve.bn_stats(stats[:, :], xt[:, :]).then_inc(mv_ready, 1)
                dve.wait_ge(mv_ready, it * 2 + 1)
                dve.sem_inc(between, 1)
                dve.bn_aggr(mv[:, :], stats[:, :]).then_inc(mv_ready, 1)

            def norm_node(it):
                dve.wait_ge(std_ready, it + 1)
                do(dve.reciprocal(rstd[:, :], std[:, :]))
                do(dve.tensor_scalar(xt[:, :], xt[:, :], mv[:, 0:1], None, ALU.subtract))
                dve.tensor_scalar(xn[:, :], xt[:, :], rstd[:, :], None, ALU.mult).then_inc(xn_ready, 1)
                dve.wait_ge(xn_ready, it + 1)
                do(dve.tensor_scalar(xt[:, :], xt[:, :], mv[:, 0:1], None, ALU.add))
                dve.wait_ge(skip_stored, it * 16 + 16)
                dve.tensor_tensor(st[:, :], xt[:, :], xn[:, :], ALU.add).then_inc(skip_ready, 1)
                dve.wait_ge(skip_ready, it + 1)
                dve.sem_inc(x_free, 1)

            def taken(kind):
                w1, w2 = bool(kind & W1_UNIT), bool(kind & W2_UNIT)
                return 4 + (3 if kind & NODES else 0) + 13 * w1 + 10 * w2

            def body(it, u, kind):
                first = next(s[0] for s in segments if s[2] == kind and (not isinstance(it, int) or s[0] == it))
                earlier = sum((s[1] - s[0]) * taken(s[2]) for s in segments if s[0] < first)
                steps.n = (it - first) * taken(kind) + earlier
                was = steps.taken
                dve.tensor_copy(srcg[:, :], srcf[:, bass.ds(it * (2 * GT), 2 * GT)]).then_inc(src_group, 1)
                dve.wait_ge(src_group, it + 1)
                mark_same(it, 0)
                mark_same(it, 1)
                rows(it, u, 0)
                if kind & (W1_UNIT | W2_UNIT):
                    greatest_weights(it, kind)
                if kind & NODES:
                    take_node(it)
                mark_same(it, 2)
                mark_same(it, 3)
                rows(it, u, 1)
                if kind & NODES:
                    norm_node(it)
                if kind & (W1_UNIT | W2_UNIT):
                    scale_and_cut(it, kind)
                assert steps.taken - was == taken(kind), (kind, steps.taken - was)

            iterations(dve, body)


def node_update(nc, sb_, sem_, bank, env):
    g = env
    with ExitStack() as ctx:
        def sb(name, shape, dt=F32):
            return sb_(name, shape, dt, ctx)
        def sem(name):
            return sem_(name, ctx)
        tables, xtab, skip, out, rowmap, ident, nodeT, ones, before, count = (
            g[k] for k in ("tables", "xtab", "skip", "out", "rowmap", "ident", "nodeT", "ones", "before", "count"))
        eps, eps2, wfT, wup, wr, brb, bfu = (g[k] for k in ("eps", "eps2", "wfT", "wup", "wr", "brb", "bfu"))
        tab = sb("tab", [P, TABLES, BATCH, AC])
        mean = sb("mean", [P, BATCH, 2 * A])
        cnt = sb("cnt", [P, BATCH])
        fused = sb("fused", [A + 1, BATCH * P])
        x1 = [sb(f"x1_{i}", [P, BATCH, D]) for i in range(2)]
        xn2 = sb("xn2", [P, BATCH, D])
        parts = sb("parts", [P, BATCH, 2, D], F16)
        xn2T = sb("xn2T", [P, 2, 2 * D])
        stats = sb("stats2", [P, BATCH, 6])
        mv = sb("mv2", [P, BATCH, 2])
        sd = sb("sd2", [P, 2, BATCH])
        rs = sb("rs2", [P, 2, BATCH])
        lg = sb("lg", [P, BATCH, X])
        seq8 = sb("seq8", [P, BATCH, X])
        chosen = sb("chosen", [P, 2, BATCH * X])
        tmp = sb("tmp_r", [P, 2, BATCH * X])
        both = tmp[:, 1, :]
        pos = lg[:, :, :].rearrange("p t e -> p (t e)")
        cum = sb("cum", [P, BATCH + 1, X])
        top = sb("top", [P, 2, BATCH])
        first = sb("first", [P, BATCH])
        weight = sb("weight", [P, 2, BATCH])
        where = sb("where", [P, 2, BATCH])
        mask = sb("mask", [P, 2, BATCH])
        valid = sb("valid", [P, TPP])
        away = sb("away_r", [P, 2, TPP])
        ids = sb("ids", [P, TPP], I32)
        rowi = [sb(f"rowi{i}", [P, 2, BATCH], I32) for i in range(2)]
        record = [sb(f"record{i}", [P, 2, BATCH, 2], I32) for i in range(2)]

        between = sem("between2")
        made = sem("made")
        tab_loaded = sem("tab_loaded")
        skip_loaded = [sem(f"skip_loaded{b}") for b in range(2)]
        x1_stored = sem("x1_stored")
        mean_ready = sem("mean_ready")
        meanT_psum = sem("meanT_psum")
        meanT_ready = sem("meanT_ready")
        fused_psum = sem("fused_psum")
        fused_ready = sem("fused_ready")
        up_psum = sem("up_psum")
        x1_ready = sem("x1_ready")
        mv_ready = sem("mv2_ready")
        sd_ready = sem("sd2_ready")
        xn2_ready = sem("xn2_ready")
        hi_ready = sem("hi_ready")
        parts_ready = sem("parts_ready")
        parts_stored = sem("parts_stored")
        xn2T_psum = sem("xn2T_psum")
        xn2T_ready = sem("xn2T_ready")
        logit_psum = sem("logit_psum")
        both_ready = sem("both_ready")
        rank_psum = sem("rank_psum")
        placed = sem("placed")
        gap_ready = sem("gap_ready")
        exp_ready = sem("exp_ready")
        rows_ready = sem("rows_ready")
        scattered = sem("scattered")
        record_free = sem("record_free")
        dve_step = sem("dve_step2")
        ones_ready = sem("ones_ready")

        halves = [(0, 4), (4, BATCH)]
        pairs = [(j, min(j + 2, BATCH)) for j in range(0, BATCH, 2)]
        NPAIR = len(pairs)
        LOG, PRE, TOT = (slice(i * BATCH * X, (i + 1) * BATCH * X) for i in range(3))
        tab_v = [t[0:NPAD, :].rearrange("(p t) a -> p (t a)", p=P) for t in tables]
        skip_v = skip.rearrange("(p t) d -> p (t d)", p=P)
        out_v = out[0:NPAD, :].rearrange("(p t) d -> p (t d)", p=P)
        xtab_v = xtab[0:NPAD, :].rearrange("(p t) d -> p (t d)", p=P)
        assert NB % 2 == 1 and NPAIR % 2 == 0

        with nc.Block() as block:

            def batches(eng, body):
                with eng.Fori(0, (NB - 3) // 2) as it:
                    for b in range(2):
                        body(it * 2 + b, b, it)
                for bt in range(NB - 3, NB):
                    body(bt, bt % 2, bt // 2)

            def is_batch(bt):
                return not isinstance(bt, int) or bt < NB

            @block.sync
            def _(sp):
                def load_skip(bt, b):
                    sp.dma_start(x1[b][:, :, :].rearrange("p t d -> p (t d)"),
                                 skip_v[:, bass.ds(bt * (BATCH * D), BATCH * D)]).then_inc(skip_loaded[b], 16)

                def load_tables(bt):
                    if not isinstance(bt, int) or bt > 0:
                        sp.wait_ge(mean_ready, bt)
                    for k in range(TABLES):
                        sp.dma_start(tab[:, k, :, :].rearrange("p t a -> p (t a)"),
                                     tab_v[k][:, bass.ds(bt * (BATCH * AC), BATCH * AC)]).then_inc(tab_loaded, 16)

                def body(bt, b, n):
                    if is_batch(bt + 2):
                        load_tables(bt + 2)
                    sp.wait_ge(x1_ready, bt * NPAIR + 2 * NPAIR)
                    sp.dma_start(out_v[:, bass.ds(bt * (BATCH * D), BATCH * D)],
                                 x1[b][:, :, :].rearrange("p t d -> p (t d)")).then_inc(x1_stored, 16)
                    sp.wait_ge(parts_ready, bt + 1)
                    sp.dma_start(xtab_v[:, bass.ds(bt * (BATCH * 2 * D), BATCH * 2 * D)],
                                 parts[:, :, :, :].rearrange("p t i d -> p (t i d)")).then_inc(parts_stored, 16)
                    if is_batch(bt + 2):
                        sp.wait_ge(x1_stored, bt * 16 + 16)
                        sp.wait_ge(xn2_ready, bt + 1)
                        load_skip(bt + 2, b)

                load_tables(0)
                load_skip(0, 0)
                load_skip(1, 1)
                load_tables(1)
                batches(sp, body)
                sp.wait_ge(x1_stored, 16 * NB)
                sp.wait_ge(parts_stored, 16 * (NB + 1))

            @block.gpsimd
            def _(pool):
                pool.sem_inc(record_free, 2)
                pool.iota(seq8[:, :, :], pattern=[[0, BATCH], [1, X]], base=-X, channel_multiplier=0,
                          allow_small_or_imprecise_dtypes=True).then_inc(made, 1)
                pool.iota(cum[:, 0, :], pattern=[[CAP, X]], base=0, channel_multiplier=0,
                          allow_small_or_imprecise_dtypes=True).then_inc(made, 1)
                pool.memset(valid[:, :], 1.0).then_inc(made, 1)
                pool.iota(ids[:, :], pattern=[[1, TPP]], base=0, channel_multiplier=TPP).then_inc(made, 1)
                pool.iota(away[:, :, :], pattern=[[TPP, 2], [1, TPP]], base=MAP_BLOCKS * BR, channel_multiplier=0,
                          allow_small_or_imprecise_dtypes=True).then_inc(made, 1)
                pool.wait_ge(made, 5)
                pool.affine_select(out=valid[:, :], in_=valid[:, :], compare_op=ALU.is_ge, fill=0.0,
                                   base=N - 1, pattern=[[-1, TPP]], channel_multiplier=-TPP).then_inc(made, 1)
                for s in range(2):
                    pool.affine_select(out=away[:, s, :], in_=away[:, s, :], compare_op=ALU.is_ge, fill=0.0,
                                       base=-N, pattern=[[1, TPP]], channel_multiplier=TPP).then_inc(made, 1)

                def scatter(bt, b, n):
                    pool.wait_ge(rows_ready, bt + 1)
                    pool.sem_inc(between, 1)
                    for j in range(BATCH):
                        for s in range(2):
                            pool.indirect_dma_start(rowmap, bass.IndirectOffsetOnAxis(ap=rowi[b][:, s, j:j + 1], axis=0),
                                                    record[b][:, s, j, :], None).then_inc(scattered, 16)
                    pool.wait_ge(scattered, bt * (32 * BATCH) + 32 * BATCH)
                    pool.sem_inc(record_free, 1)

                batches(pool, scatter)

            @block.tensor
            def _(pe):
                pe.wait_ge(ones_ready, 2)

                def turn_means(bt):
                    pe.wait_ge(mean_ready, bt + 1)
                    for h, (lo, hi) in enumerate(halves):
                        for j in range(lo, hi):
                            mm = pe.transpose(bank[h][:, (j - lo) * P:(j - lo + 1) * P], mean[:, j, :], ident[:, :])
                        mm.then_inc(meanT_psum, 1)

                def update(bt):
                    for h, (lo, hi) in enumerate(halves):
                        pe.wait_ge(meanT_ready, bt * 2 + (h + 1))
                        w = (hi - lo) * P
                        pe.matmul(bank[h][0:A, 0:w], wfT[:, :], nodeT[:, bass.ds(bt * (BATCH * P) + lo * P, w)],
                                  start=True, stop=True).then_inc(fused_psum, 1)
                    for n, (lo, hi) in enumerate(pairs):
                        pe.wait_ge(fused_ready, bt * 2 + (1 if hi <= 4 else 2))
                        pe.wait_ge(x1_ready, bt * NPAIR + (n + 1))
                        for j in range(lo, hi):
                            mm = pe.matmul(bank[2 + n][:, (j - lo) * D:(j - lo + 1) * D], fused[:, j * P:(j + 1) * P],
                                           wup[:, :], start=True, stop=True)
                        mm.then_inc(up_psum, 1)

                def turn_pair(n):
                    lo, hi = pairs[n]
                    for j in range(lo, hi):
                        for k in range(KD):
                            o = (j - lo) * D + k * P
                            mm = pe.transpose(bank[6][:, o:o + P], xn2[:, j, k * P:(k + 1) * P], ident[:, :])
                    mm.then_inc(xn2T_psum, 1)

                def logit_pair(n):
                    lo, hi = pairs[n]
                    for j in range(lo, hi):
                        for k in range(KD):
                            o = (j - lo) * D + k * P
                            mm = pe.matmul(bank[7][:, j * X:(j + 1) * X], xn2T[:, n % 2, o:o + P], wr[:, k, :],
                                           start=(k == 0), stop=(k == KD - 1))
                    if n == NPAIR - 1:
                        mm.then_inc(logit_psum, 1)

                def router(bt):
                    pe.wait_ge(xn2_ready, bt + 1)
                    turn_pair(0)
                    pe.wait_ge(placed, bt + 1)
                    for n in range(NPAIR):
                        pe.wait_ge(xn2T_ready, bt * NPAIR + (n + 1))
                        if n + 1 < NPAIR:
                            turn_pair(n + 1)
                        logit_pair(n)

                def places(bt):
                    pe.wait_ge(both_ready, bt + 1)
                    pe.matmul(bank[7][:, PRE], before[:, :], both, start=True, stop=True)
                    pe.matmul(bank[7][:, TOT], ones[:, :], both, start=True, stop=True).then_inc(rank_psum, 1)

                def body(bt, b, n):
                    router(bt)
                    if is_batch(bt + 2):
                        turn_means(bt + 2)
                    places(bt)
                    if is_batch(bt + 2):
                        update(bt + 2)

                for bt in range(2):
                    turn_means(bt)
                    update(bt)
                batches(pe, body)

            @block.scalar
            def _(act):
                def take_means(bt):
                    for h, (lo, hi) in enumerate(halves):
                        act.wait_ge(meanT_psum, bt * 2 + (h + 1))
                        nc.scalar.copy(nodeT[A:2 * A, bass.ds(bt * (BATCH * P) + lo * P, (hi - lo) * P)],
                                       bank[h][A:2 * A, 0:(hi - lo) * P]).then_inc(meanT_ready, 1)

                def fuse(bt):
                    for h, (lo, hi) in enumerate(halves):
                        act.wait_ge(fused_psum, bt * 2 + (h + 1))
                        nc.scalar.activation(fused[0:A, lo * P:hi * P], bank[h][0:A, 0:(hi - lo) * P], ACT.Relu,
                                             bias=bfu[:, :]).then_inc(fused_ready, 1)

                def deviation(bt):
                    act.wait_ge(mv_ready, bt + 1)
                    nc.scalar.activation(sd[:, 0, :], mv[:, :, 1], ACT.Sqrt, bias=eps[:, :]).then_inc(sd_ready, 1)
                    nc.scalar.activation(sd[:, 1, :], mv[:, :, 1], ACT.Sqrt, bias=eps2[:, :],
                                         scale=1.0 + EPS).then_inc(sd_ready, 1)

                def body(bt, b, n):
                    for n_, (lo, hi) in enumerate(pairs):
                        act.wait_ge(xn2T_psum, bt * NPAIR + (n_ + 1))
                        nc.scalar.copy(xn2T[:, n_ % 2, 0:(hi - lo) * D], bank[6][:, 0:(hi - lo) * D]).then_inc(xn2T_ready, 1)
                        if n_ == 0:
                            act.wait_ge(parts_stored, bt * 16 + 16)
                            nc.scalar.activation(parts[:, :, 0, :], xn2[:, :, :], ACT.Copy, scale=XS).then_inc(hi_ready, 1)
                    if is_batch(bt + 2):
                        take_means(bt + 2)
                    act.wait_ge(gap_ready, bt + 1)
                    nc.scalar.activation(weight[:, 1, :], weight[:, 0, :], ACT.Exp).then_inc(exp_ready, 1)
                    if is_batch(bt + 2):
                        fuse(bt + 2)
                    if is_batch(bt + 1):
                        deviation(bt + 1)

                for bt in range(2):
                    take_means(bt)
                    fuse(bt)
                deviation(0)
                batches(act, body)

            @block.vector
            def _(dve):
                steps = Steps(dve, dve_step)

                def do(ins):
                    steps.step(ins)
                    steps.settle()

                MEAN_STEPS, STAT_STEPS, NORM_STEPS, ROUTE_STEPS = TABLES + 1, 1, 2, 30
                BATCH_STEPS = MEAN_STEPS + STAT_STEPS + NORM_STEPS + ROUTE_STEPS

                dve.memset(fused[A:A + 1, :], 1.0).then_inc(ones_ready, 1)
                dve.memset(mean[:, :, 0:A], 0.0).then_inc(ones_ready, 1)
                dve.sem_inc(placed, 1)
                dve.sem_inc(x1_ready, NPAIR)
                dve.sem_inc(parts_stored, 16)

                def means(bt):
                    dve.wait_ge(tab_loaded, bt * (16 * TABLES) + 16 * TABLES)
                    for k in range(1, TABLES):
                        do(dve.tensor_tensor(tab[:, 0, :, :], tab[:, 0, :, :], tab[:, k, :, :], ALU.add))
                    do(dve.tensor_scalar(cnt[:, :], tab[:, 0, :, A], 1.0, None, ALU.max))
                    do(dve.reciprocal(cnt[:, :], cnt[:, :]))
                    if not isinstance(bt, int) or bt > 0:
                        dve.wait_ge(meanT_psum, bt * 2)
                    dve.tensor_tensor(mean[:, :, A:2 * A], tab[:, 0, :, 0:A],
                                      cnt[:, :].rearrange("p (t o) -> p t o", o=1).to_broadcast([P, BATCH, A]),
                                      ALU.mult).then_inc(mean_ready, 1)

                def add_update(bt, b, n_):
                    dve.wait_ge(skip_loaded[b], n_ * 16 + 16)
                    for n, (lo, hi) in enumerate(pairs):
                        dve.wait_ge(up_psum, bt * NPAIR + (n + 1))
                        dve.tensor_tensor(x1[b][:, lo:hi, :],
                                          bank[2 + n][:, 0:(hi - lo) * D].rearrange("p (t d) -> p t d", d=D),
                                          x1[b][:, lo:hi, :], ALU.add).then_inc(x1_ready, 1)

                def statistics(bt, b):
                    dve.wait_ge(x1_ready, bt * NPAIR + 2 * NPAIR)
                    for j in range(BATCH):
                        ins = dve.bn_stats(stats[:, j, :], x1[b][:, j, :])
                    do(ins)
                    dve.sem_inc(between, 1)
                    for j in range(BATCH):
                        ins = dve.bn_aggr(mv[:, j, :], stats[:, j, :])
                    ins.then_inc(mv_ready, 1)

                def norm(bt, b):
                    dve.wait_ge(sd_ready, bt * 2 + 2)
                    do(dve.reciprocal(rs[:, :, :], sd[:, :, :]))
                    for j in range(BATCH):
                        ins = dve.tensor_scalar(xn2[:, j, :], x1[b][:, j, :], mv[:, j, 0:1], rs[:, 1, j:j + 1],
                                                ALU.subtract, ALU.mult)
                    ins.then_inc(xn2_ready, 1)
                    dve.wait_ge(xn2_ready, bt + 1)
                    do(dve.tensor_tensor(rs[:, 0, :], rs[:, 0, :], sd[:, 1, :], ALU.mult))

                def low_parts(bt):
                    dve.wait_ge(hi_ready, bt + 1)
                    dve.scalar_tensor_tensor(out=parts[:, :, 1, :], in0=xn2[:, :, :], scalar=XS, in1=parts[:, :, 0, :],
                                             op0=ALU.mult, op1=ALU.subtract).then_inc(parts_ready, 1)

                def route(bt, b):
                    col = lambda t: t.rearrange("p (t e) -> p t e", e=X)
                    per_tok = lambda t: t.rearrange("p (t o) -> p t o", o=1).to_broadcast([P, BATCH, X])
                    toks = bass.ds(bt * BATCH, BATCH)
                    per_choice = lambda t: t.rearrange("p (o t) -> p o t", o=1).to_broadcast([P, 2, BATCH])
                    dve.wait_ge(record_free, bt + 1)
                    do(dve.tensor_copy(record[b][:, :, :, 0], per_choice(ids[:, toks])))
                    do(dve.tensor_copy(mask[:, :, :], per_choice(valid[:, toks])))
                    dve.wait_ge(logit_psum, bt + 1)
                    do(dve.tensor_tensor(lg[:, :, :], col(bank[7][:, LOG]), per_tok(rs[:, 0, :]), ALU.mult))
                    do(dve.tensor_tensor(lg[:, :, :], lg[:, :, :],
                                         brb[:, :].rearrange("p (o e) -> p o e", o=1).to_broadcast([P, BATCH, X]), ALU.add))
                    for s in range(2):
                        do(dve.tensor_reduce(top[:, s, :], lg[:, :, :], AX_X, ALU.max))
                        do(dve.tensor_tensor(col(tmp[:, 0, :]), lg[:, :, :], per_tok(top[:, s, :]), ALU.is_equal))
                        do(dve.tensor_tensor(col(tmp[:, 0, :]), col(tmp[:, 0, :]), seq8[:, :, :], ALU.mult))
                        do(dve.tensor_reduce(first[:, :], col(tmp[:, 0, :]), AX_X, ALU.min))
                        do(dve.tensor_tensor(col(chosen[:, s, :]), seq8[:, :, :], per_tok(first[:, :]), ALU.is_equal))
                        if s == 0:
                            do(dve.scalar_tensor_tensor(out=lg[:, :, :], in0=col(chosen[:, 0, :]), scalar=-BIG,
                                                        in1=lg[:, :, :], op0=ALU.mult, op1=ALU.add))
                    do(dve.tensor_tensor(chosen[:, :, :].rearrange("p s (t e) -> p (s t) e", e=X),
                                         chosen[:, :, :].rearrange("p s (t e) -> p (s t) e", e=X),
                                         mask[:, :, :].rearrange("p s (t o) -> p (s t) o", o=1).to_broadcast([P, 2 * BATCH, X]),
                                         ALU.mult))
                    dve.tensor_tensor(both, chosen[:, 0, :], chosen[:, 1, :], ALU.add).then_inc(both_ready, 1)
                    dve.tensor_tensor(weight[:, 0, :], top[:, 1, :], top[:, 0, :], ALU.subtract).then_inc(gap_ready, 1)
                    dve.wait_ge(rank_psum, bt + 1)
                    for j in range(BATCH):
                        do(dve.tensor_tensor(cum[:, j + 1, :], cum[:, j, :], col(bank[7][:, TOT])[:, j, :], ALU.add))
                    dve.tensor_tensor(col(pos[:, :]), cum[:, 0:BATCH, :], col(bank[7][:, PRE]), ALU.add).then_inc(placed, 1)
                    dve.wait_ge(placed, bt + 2)
                    steps.step(dve.tensor_copy(cum[:, 0, :], cum[:, BATCH, :]))
                    do(dve.tensor_tensor(tmp[:, :, :], chosen[:, :, :],
                                         pos[:, :].rearrange("p (o c) -> p o c", o=1).to_broadcast([P, 2, BATCH * X]), ALU.mult))
                    do(dve.tensor_reduce(where[:, :, :].rearrange("p s t -> p (s t)"),
                                         tmp[:, :, :].rearrange("p s (t e) -> p (s t) e", e=X), AX_X, ALU.add))
                    steps.step(dve.tensor_tensor(rowi[b][:, :, :], where[:, :, :], away[:, :, toks], ALU.add))
                    dve.wait_ge(exp_ready, bt + 1)
                    do(dve.tensor_scalar(first[:, :], weight[:, 1, :], 1.0, None, ALU.add))
                    do(dve.reciprocal(weight[:, 0, :], first[:, :]))
                    do(dve.tensor_tensor(weight[:, 1, :], weight[:, 1, :], weight[:, 0, :], ALU.mult))
                    dve.tensor_copy(record[b][:, :, :, 1].bitcast(F32), weight[:, :, :]).then_inc(rows_ready, 1)

                def norm_all(bt, b, n):
                    add_update(bt, b, n)
                    statistics(bt, b)
                    norm(bt, b)

                def body(bt, b, n):
                    was = steps.taken
                    steps.n = bt * BATCH_STEPS + before_loop
                    if is_batch(bt + 2):
                        means(bt + 2)
                    else:
                        steps.n = steps.n + MEAN_STEPS
                        dve.sem_inc(dve_step, MEAN_STEPS)
                    low_parts(bt)
                    route(bt, b)
                    if is_batch(bt + 1):
                        norm_all(bt + 1, 1 - b, n + b)
                        assert not is_batch(bt + 2) or steps.taken - was == BATCH_STEPS, steps.taken - was

                for bt in range(2):
                    means(bt)
                norm_all(0, 0, 0)
                before_loop = steps.n
                dve.wait_ge(made, 8)
                batches(dve, body)
                dve.tensor_copy(count[:, :], cum[:, 0, :])


def experts(nc, ctx, sb_, sem_, bank, env):
    g = env
    def sb(name, shape, dt=F32):
        return sb_(name, shape, dt, ctx)
    def sem(name):
        return sem_(name, ctx)
    rowmap, xtab, out, added, ones, count, identb, w1s, w2s, b1p, wsum = (
        g[k] for k in ("rowmap", "xtab", "out", "added", "ones", "count", "identb", "w1s", "w2s", "b1p", "wsum"))
    b2b = sb("b2b", [P, X, D])
    nblk = sb("nblk", [P, 4, X])
    nblki = sb("nblki", [P, X], I32)
    blockno = sb("blockno", [1, BLOCKS])
    cover = sb("cover", [1, BLOCKS, X - 1])
    skipped = sb("skipped", [1, BLOCKS, X - 1])
    exf = sb("exf", [1, BLOCKS])
    exi = sb("exi", [1, BLOCKS], I32)
    blki = sb("blki", [1, BLOCKS], I32)
    bmax = sb("bmax", [P, X])
    hbound = sb("hbound", [P, X])
    hscale = sb("hscale", [P, X])
    hcut = sb("hcut", [P, X])
    yscale = sb("yscale", [P, X])

    between = sem("between3")
    made = sem("made3")
    steps_sem = sem("dve_step3")
    bmax_ready = sem("bmax_ready")
    bsum_psum = sem("bsum_psum")
    b2_loaded = sem("b2_loaded")

    with nc.Block() as block:

        @block.sync
        def _(sp):
            sp.dma_start(b2b[:, :, :].rearrange("p e d -> p (e d)"),
                         g["b2"].rearrange("(o e) d -> o (e d)", o=1).to_broadcast([P, X * D])).then_inc(b2_loaded, 16)
            sp.wait_ge(b2_loaded, 16)

        @block.gpsimd
        def _(pool):
            pool.iota(blockno[:, :], pattern=[[1, BLOCKS]], base=0, channel_multiplier=0,
                      allow_small_or_imprecise_dtypes=True).then_inc(made, 1)
            pool.iota(nblk[:, 2, :], pattern=[[CAP, X]], base=0, channel_multiplier=0,
                      allow_small_or_imprecise_dtypes=True).then_inc(made, 1)

        @block.tensor
        def _(pe):
            pe.wait_ge(bmax_ready, 1)
            pe.matmul(bank[0][:, 0:X], ones[:, :], bmax[:, :], start=True, stop=True).then_inc(bsum_psum, 1)

        @block.vector
        def _(dve):
            steps = Steps(dve, steps_sem)

            def do(ins):
                steps.step(ins)
                steps.settle()

            dve.tensor_reduce(bmax[:, :], b1p[:, :].rearrange("p (e c) -> p e c", c=HC), AX_X, ALU.max,
                              apply_absolute_value=True).then_inc(bmax_ready, 1)
            dve.wait_ge(made, 2)
            do(dve.tensor_tensor(nblk[:, 0, :], count[:, :], nblk[:, 2, :], ALU.subtract))
            do(dve.tensor_scalar(nblki[:, :], nblk[:, 0, :], float(BR - 1), None, ALU.add))
            do(dve.tensor_scalar(nblki[:, :], nblki[:, :], BR.bit_length() - 1, None, ALU.arith_shift_right))
            do(dve.tensor_copy(nblk[:, 0, :], nblki[:, :]))
            do(dve.tensor_scalar(nblk[:, 3, :], nblk[:, 0, :], -1.0, float(CAPB), ALU.mult, ALU.add))
            u, v = 0, 1
            d = 1
            while d < X:
                do(dve.tensor_copy(nblk[:, v, 0:d], nblk[:, u, 0:d]))
                do(dve.tensor_tensor(nblk[:, v, d:X], nblk[:, u, d:X], nblk[:, u, 0:X - d], ALU.add))
                u, v = v, u
                d *= 2
            per_block = lambda t: t.rearrange("p (o e) -> p o e", o=1).to_broadcast([1, BLOCKS, X - 1])
            do(dve.tensor_tensor(cover[:, :, :], blockno[:, :].rearrange("p (i o) -> p i o", o=1).to_broadcast([1, BLOCKS, X - 1]),
                                 per_block(nblk[0:1, u, 0:X - 1]), ALU.is_ge))
            do(dve.tensor_reduce(exf[:, :], cover[:, :, :], AX_X, ALU.add))
            do(dve.tensor_copy(exi[:, :], exf[:, :]))
            do(dve.tensor_tensor(skipped[:, :, :], cover[:, :, :], per_block(nblk[0:1, 3, 0:X - 1]), ALU.mult))
            do(dve.tensor_reduce(exf[:, :], skipped[:, :, :], AX_X, ALU.add))
            do(dve.tensor_tensor(exf[:, :], exf[:, :], blockno[:, :], ALU.add))
            do(dve.tensor_copy(blki[:, :], exf[:, :]))
            dve.wait_ge(bsum_psum, 1)
            do(dve.scalar_tensor_tensor(out=hbound[:, :], in0=wsum[:, 0:X], scalar=XMAX, in1=bank[0][:, 0:X],
                                        op0=ALU.mult, op1=ALU.add))
            do(dve.reciprocal(hcut[:, :], hbound[:, :]))
            do(dve.tensor_scalar(hcut[:, :], hcut[:, :], TOP, None, ALU.mult))
            do(dve.tensor_scalar(hscale[:, :], wsum[:, 0:X], 1.0 / (TOP * XS), None, ALU.mult))
            do(dve.tensor_scalar(yscale[:, :], wsum[:, X:2 * X], 1.0 / TOP, None, ALU.mult))
            do(dve.tensor_tensor(yscale[:, :], yscale[:, :], hbound[:, :], ALU.mult))
            do(dve.tensor_scalar(yscale[:, :], yscale[:, :], 1.0 / TOP, None, ALU.mult))

    RING = 4
    QUARTERS = 4
    QC = HC // QUARTERS
    rec = [sb(f"rec{i}", [P, SUB, 2], I32) for i in range(RING)]
    xg = [sb(f"xg{i}", [P, SUB, 2 * D], F16) for i in range(2)]
    xT = [sb(f"xT{i}", [P, 2 * KD, BR], F16) for i in range(2)]
    hid = [sb(f"hid{i}", [P, HC, BR]) for i in range(2)]
    hs = [sb(f"hs{i}", [P, 2, HC, BR], F16) for i in range(2)]
    yb = [sb(f"yb{i}", [P, SUB, D]) for i in range(2)]
    rec_loaded = [sem(f"rec_loaded{r}") for r in range(RING)]
    gathered = [sem(f"gathered{b}") for b in range(2)]
    xT_psum = sem("xT_psum")
    xT_ready = sem("xT_ready")
    h_psum = sem("h_psum")
    h_ready = sem("h_ready")
    cut_hi = sem("cut_hi")
    cut_ready = sem("cut_ready")
    y_psum = sem("y_psum")
    y_sum = sem("y_sum")
    y_ready = sem("y_ready")
    bankH, bankX, bankY = bank[0:4], bank[4:6], bank[6:8]
    rowmap_v = rowmap[0:MAP_BLOCKS * BR, :].rearrange("(i p s) c -> p i (s c)", p=P, s=SUB)
    FIRST, EACH = 3 * 16, SUB * 16
    LOOPED = (BLOCKS - RING) // RING * RING
    assert BLOCKS % RING == 0 and RING % 2 == 0

    def blocks(eng, body):
        with eng.Fori(0, LOOPED // RING) as n:
            for r in range(RING):
                body(n * RING + r, n, r)
        for i in range(LOOPED, BLOCKS):
            body(i, i // RING, i % RING)

    def is_block(i):
        return not isinstance(i, int) or i < BLOCKS

    def expert_of(eng, i):
        return eng.value_load(exi[0:1, bass.ds(i, 1)], min_val=0, max_val=X - 1)

    with nc.Block() as block:

        @block.sync
        def _(sp):
            def load_record(i, r):
                at = sp.value_load(blki[0:1, bass.ds(i, 1)], min_val=0, max_val=MAP_BLOCKS - 1)
                sp.dma_start(rec[r][:, :, :].rearrange("p s c -> p (s c)"),
                             rowmap_v[:, bass.ds(at, 1), :].rearrange("p o c -> p (o c)")).then_inc(rec_loaded[r], 16)

            for i in range(RING):
                load_record(i, i)

            def body(i, n, r):
                if is_block(i + RING) and not (isinstance(i, int) and i + RING >= BLOCKS):
                    sp.wait_ge(added, i * EACH + (FIRST + EACH))
                    load_record(i + RING, r)

            blocks(sp, body)

        @block.gpsimd
        def _(pool):
            def gather(i, n, r):
                b = r % 2
                pool.wait_ge(rec_loaded[r], n * 16 + 16)
                pool.sem_inc(between, 1)
                if not isinstance(i, int) or i >= 2:
                    pool.wait_ge(xT_psum, i - 1)
                    pool.sem_inc(between, 1)
                for s in range(SUB):
                    pool.indirect_dma_start(xg[b][:, s, :], None, xtab,
                                            bass.IndirectOffsetOnAxis(ap=rec[r][:, s, 0:1], axis=0)).then_inc(gathered[b], 16)

            def body(i, n, r):
                if is_block(i + 3):
                    gather(i + 3, n + (1 if r + 3 >= RING else 0), (r + 3) % RING)
                b = r % 2
                pool.wait_ge(y_ready, i + 3)
                pool.wait_ge(added, i * EACH + FIRST)
                pool.sem_inc(between, 1)
                for s in range(SUB):
                    pool.indirect_dma_start(out, bass.IndirectOffsetOnAxis(ap=rec[r][:, s, 0:1], axis=0),
                                            yb[b][:, s, :], None, compute_op=ALU.add).then_inc(added, 16)

            for i in range(3):
                gather(i, 0, i)
            blocks(pool, body)
            pool.wait_ge(added, FIRST + EACH * BLOCKS)

        @block.tensor
        def _(pe):
            def turn(i, n2, b):
                pe.wait_ge(gathered[b], n2 * (16 * SUB) + 16 * SUB)
                for s in range(SUB):
                    for k in range(2 * KD):
                        mm = pe.transpose(bankX[b][:, :].bitcast(F16)[:, k * BR + s * P:k * BR + (s + 1) * P],
                                          xg[b][:, s, k * P:(k + 1) * P], identb[:, :])
                mm.then_inc(xT_psum, 1)

            def layer1(i, b):
                e = expert_of(pe, i)
                pe.wait_ge(xT_ready, i + 1)
                for c in range(HC):
                    if c % QC == 0:
                        pe.wait_ge(h_ready, i * QUARTERS + (c // QC + 1))
                    o = bankH[c // QC][:, (c % QC) * BR:(c % QC + 1) * BR]
                    passes = [(k, w, v) for k in range(KD) for w, v in ((0, 0), (0, 1), (1, 0))]
                    for m, (k, w, v) in enumerate(passes):
                        lhs = w1s[:, bass.ds(e, 1), k, w, c * P:(c + 1) * P].rearrange("p o h -> p (o h)")
                        mm = pe.matmul(o, lhs, xT[b][:, v * KD + k, :], start=(m == 0), stop=(m == len(passes) - 1))
                    if c % QC == QC - 1:
                        mm.then_inc(h_psum, 1)

            def layer2(i, b):
                e = expert_of(pe, i)
                pe.wait_ge(y_ready, i + 1)
                for s in range(SUB):
                    for c in range(HC):
                        if s == 0 and c % QC == 0:
                            pe.wait_ge(cut_ready, i * QUARTERS + (c // QC + 1))
                        for m, (v, w) in enumerate(((0, 0), (0, 1), (1, 0))):
                            rhs = w2s[:, bass.ds(e, 1), c, w, :].rearrange("p o d -> p (o d)")
                            mm = pe.matmul(bankY[b][:, s * D:(s + 1) * D], hs[b][:, v, c, s * P:(s + 1) * P], rhs,
                                           start=(c == 0 and m == 0), stop=(c == HC - 1 and m == 2))
                mm.then_inc(y_psum, 1)

            def body(i, n, r):
                b = r % 2
                if is_block(i + 1):
                    layer1(i + 1, 1 - b)
                if is_block(i + 2):
                    turn(i + 2, n * (RING // 2) + (r // 2 + 1), b)
                layer2(i, b)

            turn(0, 0, 0)
            layer1(0, 0)
            turn(1, 0, 1)
            blocks(pe, body)

        @block.scalar
        def _(act):
            act.sem_inc(h_ready, QUARTERS)

            def gelu(i, b):
                e = expert_of(act, i)
                for c in range(HC):
                    if c % QC == 0:
                        act.wait_ge(h_psum, i * QUARTERS + (c // QC + 1))
                    ins = nc.scalar.activation(hid[b][:, c, :], bankH[c // QC][:, (c % QC) * BR:(c % QC + 1) * BR],
                                               ACT.Gelu, bias=b1p[:, bass.ds(e * HC + c, 1)],
                                               scale=hscale[:, bass.ds(e, 1)])
                    if c % QC == QC - 1:
                        ins.then_inc(h_ready, 1)

            def body(i, n, r):
                if is_block(i + 1):
                    gelu(i + 1, 1 - r % 2)

            gelu(0, 0)
            blocks(act, body)

        @block.vector
        def _(dve):
            dve.sem_inc(y_ready, 2)

            def take_x(i, b):
                dve.wait_ge(xT_psum, i + 1)
                dve.tensor_copy(xT[b][:, :, :].rearrange("p k t -> p (k t)"),
                                bankX[b][:, :].bitcast(F16)).then_inc(xT_ready, 1)

            def cut(i, b):
                e = expert_of(dve, i)
                to_cut = hcut[:, bass.ds(e, 1)]
                for q in range(QUARTERS):
                    hi, lo = (hs[b][:, v, q * QC:(q + 1) * QC, :].rearrange("p c t -> p (c t)") for v in range(2))
                    whole = hid[b][:, q * QC:(q + 1) * QC, :].rearrange("p c t -> p (c t)")
                    dve.wait_ge(h_ready, i * QUARTERS + (q + 1 + QUARTERS))
                    dve.tensor_scalar(hi, whole, to_cut, None, ALU.mult).then_inc(cut_hi, 1)
                    dve.wait_ge(cut_hi, i * QUARTERS + (q + 1))
                    dve.scalar_tensor_tensor(out=lo, in0=whole, scalar=to_cut, in1=hi, op0=ALU.mult,
                                             op1=ALU.subtract).then_inc(cut_ready, 1)

            def finish(i, r):
                b = r % 2
                e = expert_of(dve, i)
                dve.wait_ge(y_psum, i + 1)
                dve.wait_ge(added, i * EACH + (FIRST - EACH))
                for s in range(SUB):
                    dve.scalar_tensor_tensor(out=yb[b][:, s, :], in0=bankY[b][:, s * D:(s + 1) * D],
                                             scalar=yscale[:, bass.ds(e, 1)],
                                             in1=b2b[:, bass.ds(e, 1), :].rearrange("p o d -> p (o d)"),
                                             op0=ALU.mult, op1=ALU.add).then_inc(y_sum, 1)
                dve.wait_ge(y_sum, i * SUB + SUB)
                for s in range(SUB):
                    ins = dve.tensor_scalar(yb[b][:, s, :], yb[b][:, s, :], rec[r][:, s, 1:2].bitcast(F32), None, ALU.mult)
                ins.then_inc(y_ready, 1)

            def body(i, n, r):
                b = r % 2
                if is_block(i + 1):
                    cut(i + 1, 1 - b)
                if is_block(i + 2):
                    take_x(i + 2, b)
                finish(i, r)

            take_x(0, 0)
            cut(0, 0)
            take_x(1, 1)
            blocks(dve, body)


_NAMES = {"x": "x", "src": "src", "edge": "edge_attr_32"} | {
    k: f"L0_gnn_{k}" for k in ("W_down", "b_down", "W_time", "b_time", "W_fusion", "b_fusion", "W_up", "b_up")} | {
    k: f"L0_ffn_{k}" for k in ("Wr", "br", "ln_g", "ln_b", "W1", "b1", "W2", "b2")}


def kernel(**inputs):
    import numpy as _np
    import concourse.bacc as _bacc
    from concourse import mybir as _mybir
    from concourse.bass_utils import run_bass_kernel_spmd as _run

    arrays = {k: _np.ascontiguousarray(inputs[name]) for k, name in _NAMES.items()}
    for k, rows, fill in (("x", NPAD, 0), ("edge", EPAD, 0), ("src", EPAD, N)):
        a = arrays[k]
        padded = _np.full((rows,) + a.shape[1:], fill, a.dtype)
        padded[:a.shape[0]] = a
        arrays[k] = padded
    nc = _bacc.Bacc("TRN2", target_bir_lowering=False, num_devices=1)
    args = {k: nc.dram_tensor(f"in_{k}", a.shape, _mybir.dt.from_np(a.dtype), kind="ExternalInput").ap()
            for k, a in arrays.items()}
    res = nc.dram_tensor("out_0_dram", (ROWS, D), F32, kind="ExternalOutput").ap()
    program(nc, **args, out=res)
    r = _run(nc, [{f"in_{k}": a for k, a in arrays.items()}], core_ids=[0])
    return r.results[0]["out_0_dram"][:N]
```

```python
from contextlib import ExitStack

import concourse.bass as bass
from concourse import mybir

P = 128
F32 = mybir.dt.float32
F16 = mybir.dt.float16
BF16 = mybir.dt.bfloat16
I32 = mybir.dt.int32
ALU = mybir.AluOpType
ACT = mybir.ActivationFunctionType
AX_X = mybir.AxisListType.X
EPS = 1e-5


def ceil_div(a, b):
    return -(-a // b)


N = 6250
D = 256
TPP = ceil_div(N, P)
NPAD = TPP * P
KD = D // P
E = 106250
FE = 32
GT = 8
EPP = ceil_div(ceil_div(E, P), 2 * GT) * 2 * GT
EPAD = EPP * P
ITERS = EPP // (2 * GT)
A = 64
AC = A + 1
X = 8
H = 1024
HC = H // P
SUB = 2
BR = SUB * P
BLOCKS = (2 * N + X * (BR - 1)) // BR
CAPB = ceil_div(N, BR)
CAP = CAPB * BR
MAP_BLOCKS = X * CAPB + BLOCKS
MAP_PP = MAP_BLOCKS * BR // P
MAP_ROWS = MAP_BLOCKS * BR + 2 * TPP
ROWS = NPAD + BR
TAB_ROWS = NPAD + P
TABLES = 4
BATCH = 7
NB = TPP // BATCH
BIG = 3.0e38
XS = 1024.0
TOP = 32768.0
XMAX = 16.0
TINY = 1e-30
assert XMAX * XMAX == D and XMAX * XS < TOP


class Steps:

    def __init__(self, eng, sem):
        self.eng, self.sem, self.n, self.taken = eng, sem, 0, 0

    def step(self, ins):
        ins.then_inc(self.sem, 1)
        self.n = self.n + 1
        self.taken += 1

    def settle(self):
        self.eng.wait_ge(self.sem, self.n)


def program(nc, x, src, edge, W_down, b_down, W_time, b_time, W_fusion, b_fusion, W_up, b_up,
            Wr, br, ln_g, ln_b, W1, b1, W2, b2, out):
    tables = [nc.dram_tensor(f"sums_{k}", [TAB_ROWS, AC], F32).ap() for k in range(TABLES)]
    xtab = nc.dram_tensor("normed_rows", [ROWS, D], F32).ap()
    skip = nc.dram_tensor("x_plus_xn", [NPAD, D], F32).ap()
    rowmap = nc.dram_tensor("row_map", [MAP_ROWS, 2], I32).ap()

    ctx = ExitStack()
    with ctx:
        def sb(name, shape, dt=F32, scope=ctx):
            return scope.enter_context(nc.sbuf_tensor(name, shape, dt))

        def sem(name, scope=ctx):
            return scope.enter_context(nc.semaphore(name))

        bank = [ctx.enter_context(nc.psum_tensor(f"bank{i}", [P, 512], F32)) for i in range(8)]

        w1s = sb("w1s", [P, X, KD, 2, H], F16)
        w2s = sb("w2s", [P, X, HC, 2, D], F16)
        b1p = sb("b1p", [P, X * HC])
        wsum = sb("wsum", [P, 2 * X])
        ident = sb("ident", [P, P])
        ident16 = sb("ident16", [P, P], F16)
        ones = sb("ones", [P, P])
        before = sb("before", [P, P])
        trash = sb("trash", [P, 1])
        eps = sb("eps", [P, 1])
        eps2 = sb("eps2", [P, 1])
        wfT = sb("wfT", [2 * A, A])
        wup = sb("wup", [A + 1, D])
        wr = sb("wr", [P, KD, X])
        brb = sb("brb", [P, X])
        bfu = sb("bfu", [A, 1])
        hscale = sb("hscale", [P, X])
        hcut = sb("hcut", [P, X])
        yscale = sb("yscale", [P, X])
        exi = sb("exi", [1, BLOCKS], I32)
        blki = sb("blki", [1, BLOCKS], I32)
        used = sb("used", [1, 1], I32)
        added = sem("added")

        with ExitStack() as gnn:
            nodeT = sb("nodeT", [2 * A, TPP * P], F32, gnn)
            with ExitStack() as one:
                edges_and_nodes(nc, one, sb, sem, bank, locals())
            node_update(nc, sb, sem, bank, locals())
        with ExitStack() as moe:
            experts(nc, moe, sb, sem, bank, locals())


def edges_and_nodes(nc, ctx, sb_, sem_, bank, env):
    g = env
    def sb(name, shape, dt=F32):
        return sb_(name, shape, dt, ctx)
    def sem(name):
        return sem_(name, ctx)
    x, src, edge, tables, xtab, skip, rowmap, out = (g[k] for k in ("x", "src", "edge", "tables", "xtab", "skip", "rowmap", "out"))
    w1s, w2s, b1p, wsum, ident, ident16, ones, before, trash = (
        g[k] for k in ("w1s", "w2s", "b1p", "wsum", "ident", "ident16", "ones", "before", "trash"))
    eps, eps2, wfT, wup, wr, brb, bfu, nodeT = (g[k] for k in ("eps", "eps2", "wfT", "wup", "wr", "brb", "bfu", "nodeT"))

    upto = sb("upto", [P, P])
    srci = sb("srci", [P, EPP], I32)
    srcf = sb("srcf", [P, EPP])
    srcg = [sb(f"srcg{i}", [P, 2 * GT]) for i in range(2)]
    zero = sb("zero", [P, 650])
    wd_raw = sb("wd_raw", [A, D])
    wt_raw = sb("wt_raw", [A, 4, FE])
    wf_raw = sb("wf_raw", [A, 2 * A])
    wu_raw = sb("wu_raw", [P, KD, A])
    ln_raw = sb("ln_raw", [X * KD, 2, P])
    b1_raw = sb("b1_raw", [X * HC, P])
    bdn = sb("bdn", [A, 1])
    bt_raw = sb("bt_raw", [1, A])
    wdT = sb("wdT", [P, KD, A])
    wtd = sb("wtd", [P, 4, A])
    bt_rest = sb("bt_rest", [1, 2, A])
    bt4 = sb("bt4", [1, 3, 4, A], BF16)
    onesb = sb("onesb", [1, P], BF16)
    lnT = sb("lnT", [P, 2, X * KD])
    b1T = sb("b1T", [P, X * HC])
    attr = [sb(f"attr{i}", [P, GT * FE]) for i in range(2)]
    attrT = sb("attrT", [P, 2, P])
    tf = [sb(f"tf{i}", [P, GT, AC]) for i in range(2)]
    same = [sb(f"same{i}", [P, 4, P]) for i in range(2)]
    rank = [sb(f"rank{i}", [P, GT]) for i in range(2)]
    away = [sb(f"away{i}", [P, GT]) for i in range(2)]
    idx = [sb(f"idx{i}", [P, GT], I32) for i in range(4)]
    pay = [sb(f"pay{i}", [P, GT, AC]) for i in range(4)]
    rowmax = sb("rowmax", [P, KD])
    wscale = sb("wscale", [P, 1])
    gains = sb("gains", [P, KD])
    xt = sb("xt", [P, D])
    xn = sb("xn", [P, D])
    st = sb("st", [P, D])
    xnT = sb("xnT", [P, KD, P])
    stats = sb("stats", [P, 6])
    mv = sb("mv", [P, 2])
    std = sb("std", [P, 1])
    rstd = sb("rstd", [P, 1])
    stage = sb("stage", [P, KD, H])
    preset = stage[:, 1, 0:2 * MAP_PP].bitcast(I32).rearrange("p (i c) -> p i c", c=2)

    between = sem("between")
    small_loaded = sem("small_loaded")
    init_stored = sem("init_stored")
    trash_stored = sem("trash_stored")
    filled = sem("filled")
    ready = sem("ready")
    prep_psum = sem("prep_psum")
    prep_done = sem("prep_done")
    bias_cut = sem("bias_cut")
    src_loaded = sem("src_loaded")
    src_float = sem("src_float")
    added = g["added"]
    tab_done = [sem(f"tab_done{k}") for k in range(TABLES)]

    with nc.Block() as block:
        small = [
            (wd_raw[:, :], g["W_down"]), (wf_raw[:, :], g["W_fusion"]),
            (wu_raw[:, :, :], g["W_up"].rearrange("(k p) a -> p k a", p=P)),
            (ln_raw[:, 0, :], g["ln_g"].rearrange("e (k p) -> (e k) p", p=P)),
            (ln_raw[:, 1, :], g["ln_b"].rearrange("e (k p) -> (e k) p", p=P)),
            (b1_raw[:, :], g["b1"].rearrange("e (c p) -> (e c) p", p=P)),
            (bdn[:, :], g["b_down"].rearrange("(a o) -> a o", o=1)),
            (bfu[:, :], g["b_fusion"].rearrange("(a o) -> a o", o=1)),
            (bt_raw[:, :], g["b_time"].rearrange("(o a) -> o a", o=1)),
            (wup[A:A + 1, :], g["b_up"].rearrange("(o d) -> o d", o=1)),
            (wr[:, :, :], g["Wr"].rearrange("(k p) e -> p k e", p=P)),
            (wt_raw[:, :, :], g["W_time"].rearrange("a (o f) -> a o f", o=1).to_broadcast([A, 4, FE])),
            (brb[:, :], g["br"].rearrange("(o e) -> o e", o=1).to_broadcast([P, X])),
        ]
        @block.sync
        def _(sp):
            sp.dma_start(srci[:, :], src.rearrange("(p j) -> p j", p=P)).then_inc(src_loaded, 16)
            for dst, s in small:
                sp.dma_start(dst, s).then_inc(small_loaded, 16)
            sp.wait_ge(filled, 1)
            sp.dma_start(rowmap[0:MAP_BLOCKS * BR, :].rearrange("(p i) c -> p (i c)", p=P),
                         preset[:, :, :].rearrange("p i c -> p (i c)")).then_inc(init_stored, 16)
            sp.wait_ge(small_loaded, 16 * len(small))
            sp.wait_ge(init_stored, 16)

        @block.gpsimd
        def _(pool):
            pool.memset(zero[:, :], 0.0)
            pool.memset(ident[:, :], 0.0).then_inc(ready, 1)
            pool.memset(upto[:, :], 1.0).then_inc(ready, 1)
            pool.memset(before[:, :], 1.0).then_inc(ready, 1)
            pool.memset(ones[:, :], 1.0).then_inc(ready, 1)
            pool.memset(preset[:, :, :], 0).then_inc(ready, 1)
            pool.memset(eps[:, :], EPS).then_inc(ready, 1)
            pool.memset(eps2[:, :], EPS * EPS).then_inc(ready, 1)
            pool.iota(trash[:, :], pattern=[[0, 1]], base=NPAD, channel_multiplier=1,
                      allow_small_or_imprecise_dtypes=True).then_inc(ready, 1)
            pool.wait_ge(ready, 8)
            pool.iota(preset[:, :, 0], pattern=[[1, MAP_PP]], base=0, channel_multiplier=MAP_PP).then_inc(ready, 1)
            pool.affine_select(out=ident[:, :], in_=ident[:, :], compare_op=ALU.not_equal, fill=1.0,
                               base=0, pattern=[[-1, P]], channel_multiplier=1).then_inc(ready, 1)
            pool.affine_select(out=upto[:, :], in_=upto[:, :], compare_op=ALU.is_ge, fill=0.0,
                               base=0, pattern=[[-1, P]], channel_multiplier=1).then_inc(ready, 1)
            pool.affine_select(out=before[:, :], in_=before[:, :], compare_op=ALU.is_ge, fill=0.0,
                               base=-1, pattern=[[1, P]], channel_multiplier=-1).then_inc(ready, 1)

        @block.tensor
        def _(pe):
            pe.wait_ge(ready, 12)
            pe.wait_ge(small_loaded, 16 * len(small))
            for k in range(KD):
                pe.transpose(bank[0][:, k * A:(k + 1) * A], wd_raw[:, k * P:(k + 1) * P], ident[0:A, 0:A])
            pe.transpose(bank[0][:, 128:128 + A], wt_raw[:, :, :].rearrange("a i f -> a (i f)"),
                         ident[0:A, 0:A]).then_inc(prep_psum, 1)
            pe.transpose(bank[1][:, 0:A], wf_raw[:, :], ident[0:A, 0:A])
            for k in range(KD):
                mm = pe.transpose(bank[1][0:A, 128 + k * P:128 + (k + 1) * P], wu_raw[:, k, :], ident[:, :])
            mm.then_inc(prep_psum, 1)
            for i in range(2):
                pe.transpose(bank[2][:, i * X * KD:(i + 1) * X * KD], ln_raw[:, i, :],
                             ident[0:X * KD, 0:X * KD])
            pe.transpose(bank[2][:, 64:64 + X * HC], b1_raw[:, :], ident[0:X * HC, 0:X * HC]).then_inc(prep_psum, 1)

        @block.vector
        def _(dve):
            dve.memset(wtd[:, :, :], 0.0).then_inc(prep_done, 1)
            for b in range(2):
                dve.memset(tf[b][:, :, A:AC], 1.0).then_inc(prep_done, 1)
            dve.wait_ge(prep_done, 3)
            dve.wait_ge(src_loaded, 16)
            dve.tensor_copy(srcf[:, :], srci[:, :]).then_inc(src_float, 1)
            dve.wait_ge(ready, 12)
            dve.tensor_copy(ident16[:, :], ident[:, :]).then_inc(prep_done, 1)
            dve.tensor_scalar(preset[:, :, 0], preset[:, :, 0], BR - 1, None, ALU.bitwise_and).then_inc(prep_done, 1)
            dve.wait_ge(prep_done, 5)
            dve.tensor_scalar(preset[:, :, 0], preset[:, :, 0], NPAD, None, ALU.add).then_inc(filled, 1)
            dve.wait_ge(prep_psum, 1)
            dve.tensor_copy(wdT[:, :, :].rearrange("p k a -> p (k a)"), bank[0][:, 0:KD * A]).then_inc(prep_done, 1)
            for i in range(4):
                dve.tensor_copy(wtd[i * FE:(i + 1) * FE, i, :],
                                bank[0][i * FE:(i + 1) * FE, 128:128 + A]).then_inc(prep_done, 1)
            dve.wait_ge(small_loaded, 16 * len(small))
            four = lambda t: t.rearrange("o (u a) -> o u a", u=1).to_broadcast([1, 4, A])
            rest = bt_raw[:, :]
            for i in range(3):
                dve.tensor_copy(bt4[:, i, :, :], four(rest)).then_inc(bias_cut, 1)
                if i < 2:
                    dve.wait_ge(bias_cut, 2 * i + 1)
                    dve.tensor_tensor(bt_rest[:, i, :], rest, bt4[:, i, 0, :], ALU.subtract).then_inc(bias_cut, 1)
                    dve.wait_ge(bias_cut, 2 * i + 2)
                    rest = bt_rest[:, i, :]
            dve.tensor_copy(onesb[:, :], ones[0:1, :]).then_inc(prep_done, 1)
            dve.wait_ge(prep_psum, 2)
            dve.tensor_copy(wfT[:, :], bank[1][:, 0:A]).then_inc(prep_done, 1)
            dve.tensor_copy(wup[0:A, :], bank[1][0:A, 128:128 + D]).then_inc(prep_done, 1)
            dve.wait_ge(prep_psum, 3)
            dve.tensor_copy(lnT[:, :, :].rearrange("p i c -> p (i c)"), bank[2][:, 0:2 * X * KD]).then_inc(prep_done, 1)
            dve.tensor_copy(b1T[:, :], bank[2][:, 64:64 + X * HC]).then_inc(prep_done, 1)

    attr_loaded = [sem(f"attr_loaded{b}") for b in range(2)]
    attr_free = [sem(f"attr_free{b}") for b in range(2)]
    src_group = sem("src_group")
    attrT_psum = sem("attrT_psum")
    attrT_ready = sem("attrT_ready")
    tf_psum = sem("tf_psum")
    tf_ready = sem("tf_ready")
    srcT_psum = sem("srcT_psum")
    same_ready = sem("same_ready")
    idx_ready = sem("idx_ready")
    pay_psum = sem("pay_psum")
    pay_ready = sem("pay_ready")
    pay_free = sem("pay_free")
    x_loaded = sem("x_loaded")
    x_free = sem("x_free")
    mv_ready = sem("mv_ready")
    std_ready = sem("std_ready")
    xn_ready = sem("xn_ready")
    skip_ready = sem("skip_ready")
    skip_stored = sem("skip_stored")
    xnT_psum = sem("xnT_psum")
    xnT_ready = sem("xnT_ready")
    node_psum = sem("node_psum")
    node_ready = sem("node_ready")
    w_loaded = sem("w_loaded")
    w_bias_psum = sem("w_bias_psum")
    w_free = sem("w_free")
    rowmax_ready = sem("rowmax_ready")
    dve_step = sem("dve_step")

    NODES, W1_UNIT, W2_UNIT = 1, 2, 4
    WEIGHTS = W1_UNIT | W2_UNIT
    segments = [(0, 2 * X, NODES | W1_UNIT), (2 * X, 4 * X, NODES | W2_UNIT), (4 * X, TPP - 1, NODES),
                (TPP - 1, TPP, NODES)] + [(i, i + 1, 0) for i in range(TPP, ITERS)]
    assert TPP % 2 == 1 and 4 * X < TPP < ITERS

    def iterations(eng, body):
        for first, end, kind in segments:
            if end - first == 1:
                body(first, first % 2, kind, 0, first)
            else:
                with eng.Fori(0, (end - first) // 2) as turn:
                    for u in range(2):
                        body(turn * 2 + (first + u), u, kind, turn, first)

    edge_v = edge.rearrange("(p j) f -> p (j f)", p=P)
    x_v = x.rearrange("(p t) d -> p t d", p=P)
    skip_v = skip.rearrange("(p t) d -> p t d", p=P)
    w1_v = g["W1"].rearrange("e (k p) h -> p e k h", p=P)
    w2_v = g["W2"].rearrange("e (c p) d -> p e c d", p=P)
    bankA, bankB, bankN, bankW = bank[0], bank[1], bank[6], bank[7]
    bankC, bankD = bank[2:4], bank[4:6]
    GROUPS = len(pay)
    QUADS = 2 * GROUPS

    with nc.Block() as block:

        @block.sync
        def _(sp):
            def body(it, u, kind, turn, first):
                for b in range(2):
                    sp.wait_ge(attr_free[b], it + 1)
                    sp.dma_start(attr[b][:, :], edge_v[:, bass.ds(it * (2 * GT * FE) + b * GT * FE, GT * FE)]
                                 ).then_inc(attr_loaded[b], 16)
                if kind & NODES:
                    sp.wait_ge(x_free, it + 1)
                    sp.dma_start(xt[:, :], x_v[:, bass.ds(it, 1), :].rearrange("p o d -> p (o d)")).then_inc(x_loaded, 16)
                unit = turn + first // 2
                if kind & WEIGHTS and u == 0:
                    sp.wait_ge(w_free, unit + 1)
                    sp.sem_inc(between, 1)
                if kind & W1_UNIT and u == 0:
                    sp.dma_start(stage[:, :, :], w1_v[:, bass.ds(unit, 1), :, :].rearrange("p o k h -> p (o k) h")
                                 ).then_inc(w_loaded, 16)
                if kind & W2_UNIT and u == 0:
                    sp.dma_start(stage[:, :, :].rearrange("p k (c d) -> p (k c) d", d=D),
                                 w2_v[:, bass.ds(unit - X, 1), :, :].rearrange("p o c d -> p (o c) d")
                                 ).then_inc(w_loaded, 16)
                if kind & NODES:
                    sp.wait_ge(skip_ready, it + 1)
                    sp.dma_start(skip_v[:, bass.ds(it, 1), :].rearrange("p o d -> p (o d)"), st[:, :]).then_inc(skip_stored, 16)

            iterations(sp, body)
            sp.wait_ge(skip_stored, 16 * (TPP + 1))

        @block.gpsimd
        def _(pool):
            for k in range(TABLES):
                rows = TAB_ROWS // P * AC
                pool.dma_start(
                    tables[k].rearrange("(p r) a -> p (r a)", p=P).rearrange("p (u v) -> p u v", v=650),
                    zero[:, :].rearrange("p (o v) -> p o v", o=1).to_broadcast([P, rows // 650, 650]),
                ).then_inc(tab_done[k], 16)
            for first, rows in ((NPAD, P), (NPAD + P, A), (NPAD + P + A, A)):
                pool.dma_start(out[first:first + rows, :], zero[0:rows, 0:D]).then_inc(added, 16)
            pool.dma_start(xtab[NPAD:ROWS, :].rearrange("(p u) d -> p (u d)", p=P),
                           zero[:, 0:SUB * D]).then_inc(trash_stored, 16)
            pool.sem_inc(pay_free, 4 * (QUADS - 1))

            def body(it, u):
                for b in range(2):
                    pool.wait_ge(idx_ready, it * 2 + (b + 1))
                    for q in range(2):
                        quad = it * 4 + (2 * b + q)
                        pool.wait_ge(pay_ready, quad + 3)
                        for s in range(4):
                            pool.wait_ge(tab_done[s], quad * 16 + 16)
                            pool.sem_inc(pay_free, 1)
                            col = 4 * q + s
                            pool.indirect_dma_start(
                                tables[s], bass.IndirectOffsetOnAxis(ap=idx[2 * u + b][:, col:col + 1], axis=0),
                                pay[2 * u + b][:, col, :], None, compute_op=ALU.add).then_inc(tab_done[s], 16)

            with pool.Fori(0, ITERS // 2) as turn:
                for u in range(2):
                    body(turn * 2 + u, u)
            for s in range(TABLES):
                pool.wait_ge(tab_done[s], 16 * (1 + 4 * ITERS))
            pool.wait_ge(trash_stored, 16)
            pool.wait_ge(added, 3 * 16)

        @block.tensor
        def _(pe):
            for b in range(2):
                pe.sem_inc(attr_free[b], 1)

            def turn_attr(it, b):
                pe.wait_ge(attr_loaded[b], it * 16 + 16)
                for q in range(2):
                    mm = pe.transpose(bankA[:, q * P:(q + 1) * P], attr[b][:, q * P:(q + 1) * P], ident[:, :])
                mm.then_inc(attrT_psum, 1)

            def features(it, b):
                pe.wait_ge(attrT_ready, it * 2 + (b + 1))
                pe.sem_inc(attr_free[b], 1)
                for q in range(2):
                    o = bankB[:, q * 4 * A:(q + 1) * 4 * A]
                    pe.matmul(o, attrT[:, q, :], wtd[:, :, :].rearrange("p i a -> p (i a)"), start=True, stop=False)
                    for i in range(3):
                        mm = pe.matmul(o, onesb[:, :], bt4[:, i, :, :].rearrange("o i a -> o (i a)"), start=False, stop=(i == 2))
                mm.then_inc(tf_psum, 1)

            def turn_src(it, u, n):
                if n == 0:
                    pe.wait_ge(src_group, it + 1)
                for s in range(4):
                    mm = pe.transpose(bankC[n % 2][:, s * P:(s + 1) * P],
                                      srcg[u][:, 4 * n + s:4 * n + s + 1].to_broadcast([P, P]), ident[:, :])
                mm.then_inc(srcT_psum, 1)

            def add_same(it, n):
                b, q = n // 2, n % 2
                pe.wait_ge(same_ready, it * 4 + (n + 1))
                if q == 0:
                    pe.wait_ge(tf_ready, it * 2 + (b + 1))
                pe.wait_ge(pay_ready, it * 4 + (n + 1))
                for s in range(4):
                    mm = pe.matmul(bankD[n % 2][:, s * AC:(s + 1) * AC], same[n % 2][:, s, :],
                                   tf[b][:, 4 * q + s, :], start=True, stop=True)
                mm.then_inc(pay_psum, 1)

            def node(it):
                pe.wait_ge(xn_ready, it + 1)
                for k in range(KD):
                    mm = pe.transpose(bankN[:, k * P:(k + 1) * P], xn[:, k * P:(k + 1) * P], ident[:, :])
                mm.then_inc(xnT_psum, 1)
                pe.wait_ge(xnT_ready, it + 1)
                for k in range(KD):
                    mm = pe.matmul(bankN[0:A, 0:P], wdT[:, k, :], xnT[:, k, :], start=(k == 0), stop=(k == KD - 1))
                mm.then_inc(node_psum, 1)

            def weight_sums(unit, kind):
                pe.wait_ge(w_loaded, unit * 16 + 16)
                if kind & W1_UNIT:
                    for c in range(HC):
                        for k in range(KD):
                            pe.matmul(bankW[:, c:c + 1], stage[:, k, c * P:(c + 1) * P],
                                      lnT[:, 1, bass.ds(unit * KD + k, 1)], start=(k == 0), stop=(k == KD - 1))
                pe.wait_ge(rowmax_ready, unit + 1)
                pe.matmul(bankW[:, HC:HC + KD], ones[:, :], rowmax[:, :], start=True, stop=True).then_inc(w_bias_psum, 1)

            def body(it, u, kind, turn, first):
                turn_attr(it, 0)
                turn_src(it, u, 0)
                turn_src(it, u, 1)
                features(it, 0)
                turn_attr(it, 1)
                add_same(it, 0)
                turn_src(it, u, 2)
                add_same(it, 1)
                turn_src(it, u, 3)
                features(it, 1)
                if kind & WEIGHTS and u == 1:
                    weight_sums(turn + first // 2, kind)
                add_same(it, 2)
                add_same(it, 3)
                if kind & NODES:
                    node(it)

            iterations(pe, body)

        @block.scalar
        def _(act):
            act.sem_inc(pay_ready, 2)

            def take_attr(it, b):
                act.wait_ge(attrT_psum, it * 2 + (b + 1))
                nc.scalar.copy(attrT[:, :, :].rearrange("p q e -> p (q e)"), bankA[:, 0:2 * P]).then_inc(attrT_ready, 1)

            def take_features(it, b):
                act.wait_ge(tf_psum, it * 2 + (b + 1))
                nc.scalar.activation(tf[b][:, :, 0:A], bankB[:, :].rearrange("p (j a) -> p j a", a=A),
                                     ACT.Relu).then_inc(tf_ready, 1)

            def take_sums(it, u, n):
                b, q = n // 2, n % 2
                act.wait_ge(pay_psum, it * 4 + (n + 1))
                act.wait_ge(pay_free, it * 16 + (4 * n + 4))
                nc.scalar.copy(pay[2 * u + b][:, 4 * q:4 * q + 4, :].rearrange("p s a -> p (s a)"),
                               bankD[n % 2][:, 0:4 * AC]).then_inc(pay_ready, 1)

            def body(it, u, kind, turn, first):
                take_attr(it, 0)
                take_features(it, 0)
                take_attr(it, 1)
                take_sums(it, u, 0)
                take_sums(it, u, 1)
                if kind & NODES:
                    act.wait_ge(mv_ready, it * 2 + 2)
                    nc.scalar.activation(std[:, :], mv[:, 1:2], ACT.Sqrt, bias=eps[:, :]).then_inc(std_ready, 1)
                take_features(it, 1)
                take_sums(it, u, 2)
                take_sums(it, u, 3)
                if kind & NODES:
                    act.wait_ge(xnT_psum, it + 1)
                    nc.scalar.copy(xnT[:, :, :].rearrange("p k t -> p (k t)"), bankN[:, 0:D]).then_inc(xnT_ready, 1)
                    act.wait_ge(node_psum, it + 1)
                    nc.scalar.activation(nodeT[0:A, bass.ds(it * P, P)], bankN[0:A, 0:P], ACT.Relu,
                                         bias=bdn[:, :]).then_inc(node_ready, 1)

            iterations(act, body)

        @block.vector
        def _(dve):
            steps = Steps(dve, dve_step)

            def do(ins):
                steps.step(ins)
                steps.settle()

            dve.sem_inc(x_free, 1)
            dve.sem_inc(w_free, 1)
            dve.sem_inc(skip_stored, 16)

            def mark_same(it, u, n):
                b, q = n // 2, n % 2
                dve.wait_ge(srcT_psum, it * 4 + (n + 1))
                for s in range(4):
                    col = 4 * q + s
                    ins = dve.scalar_tensor_tensor(
                        out=same[n % 2][:, s, :], in0=bankC[n % 2][:, s * P:(s + 1) * P],
                        scalar=srcg[u][:, 4 * n + s:4 * n + s + 1], in1=upto[:, :], op0=ALU.is_equal, op1=ALU.mult,
                        accum_out=rank[b][:, col:col + 1])
                ins.then_inc(same_ready, 1)

            def take_src(it, u):
                dve.tensor_copy(srcg[u][:, :], srcf[:, bass.ds(it * (2 * GT), 2 * GT)]).then_inc(src_group, 1)

            def rows(it, u, b):
                dve.wait_ge(same_ready, it * 4 + (2 * b + 2))
                do(dve.tensor_scalar(away[b][:, :], srcg[u][:, b * GT:(b + 1) * GT], trash[:, :], None, ALU.subtract))
                do(dve.scalar_tensor_tensor(out=away[b][:, :], in0=rank[b][:, :], scalar=1.0, in1=away[b][:, :],
                                            op0=ALU.is_equal, op1=ALU.mult))
                dve.wait_ge(pay_free, it * 16 + (8 * b + 8))
                dve.tensor_scalar(idx[2 * u + b][:, :], away[b][:, :], trash[:, :], None, ALU.add).then_inc(idx_ready, 1)

            def greatest_weights(unit, kind):
                dve.wait_ge(w_loaded, unit * 16 + 16)
                do(dve.tensor_reduce(gains[:, :], stage[:, :, :], AX_X, ALU.max, apply_absolute_value=True))
                if kind & W1_UNIT:
                    do(dve.tensor_tensor(gains[:, :], gains[:, :], lnT[:, 0, bass.ds(unit * KD, KD)], ALU.mult))
                dve.scalar_tensor_tensor(out=rowmax[:, :], in0=gains[:, :], scalar=-1.0, in1=gains[:, :],
                                         op0=ALU.mult, op1=ALU.max).then_inc(rowmax_ready, 1)

            def weight_scale(unit, kind):
                dve.wait_ge(w_bias_psum, unit + 1)
                do(dve.tensor_reduce(wscale[:, :], bankW[:, HC:HC + KD], AX_X, ALU.add))
                do(dve.tensor_scalar(wscale[:, :], wscale[:, :], TINY, None, ALU.max))
                do(dve.tensor_copy(wsum[:, bass.ds(unit, 1)], wscale[:, :]))
                do(dve.reciprocal(wscale[:, :], wscale[:, :]))
                do(dve.tensor_scalar(wscale[:, :], wscale[:, :], TOP, None, ALU.mult))
                if kind & W1_UNIT:
                    do(dve.tensor_scalar(gains[:, :], lnT[:, 0, bass.ds(unit * KD, KD)], wscale[:, :], None, ALU.mult))

            def cut_weights(unit, kind, k):
                if kind & W1_UNIT:
                    tab = w1s[:, bass.ds(unit, 1), k, :, :].rearrange("p o i h -> p (o i) h")
                    gain, hi, lo, whole = gains[:, k:k + 1], tab[:, 0, :], tab[:, 1, :], stage[:, k, :]
                else:
                    half = slice(k * HC // KD, (k + 1) * HC // KD)
                    tab = w2s[:, bass.ds(unit - X, 1), half, :, :].rearrange("p o c i d -> p (o c) i d")
                    gain, hi, lo = wscale[:, :], tab[:, :, 0, :], tab[:, :, 1, :]
                    whole = stage[:, k, :].rearrange("p (c d) -> p c d", d=D)
                do(dve.tensor_scalar(hi, whole, gain, None, ALU.mult))
                do(dve.scalar_tensor_tensor(out=lo, in0=whole, scalar=gain, in1=hi, op0=ALU.mult, op1=ALU.subtract))

            def end_unit(unit, kind):
                if kind & W1_UNIT:
                    do(dve.tensor_tensor(b1p[:, bass.ds(unit * HC, HC)], bankW[:, 0:HC],
                                         b1T[:, bass.ds(unit * HC, HC)], ALU.add))
                dve.sem_inc(w_free, 1)

            def take_node(it):
                dve.wait_ge(x_loaded, it * 16 + 16)
                dve.bn_stats(stats[:, :], xt[:, :]).then_inc(mv_ready, 1)
                dve.wait_ge(mv_ready, it * 2 + 1)
                dve.sem_inc(between, 1)
                dve.bn_aggr(mv[:, :], stats[:, :]).then_inc(mv_ready, 1)

            def norm_node(it):
                dve.wait_ge(std_ready, it + 1)
                do(dve.reciprocal(rstd[:, :], std[:, :]))
                do(dve.tensor_scalar(xt[:, :], xt[:, :], mv[:, 0:1], None, ALU.subtract))
                dve.tensor_scalar(xn[:, :], xt[:, :], rstd[:, :], None, ALU.mult).then_inc(xn_ready, 1)
                dve.wait_ge(xn_ready, it + 1)
                do(dve.tensor_scalar(xt[:, :], xt[:, :], mv[:, 0:1], None, ALU.add))
                dve.wait_ge(skip_stored, it * 16 + 16)
                dve.tensor_tensor(st[:, :], xt[:, :], xn[:, :], ALU.add).then_inc(skip_ready, 1)
                dve.wait_ge(skip_ready, it + 1)
                dve.sem_inc(x_free, 1)

            def taken(kind, u):
                weights = {0: (0, 0), W1_UNIT: (2, 11), W2_UNIT: (1, 9)}[kind & WEIGHTS]
                return 4 + (3 if kind & NODES else 0) + weights[u]

            def body(it, u, kind, turn, first):
                earlier = sum(taken(s[2], i % 2) for s in segments if s[0] < first for i in range(s[0], s[1]))
                steps.n = turn * (taken(kind, 0) + taken(kind, 1)) + (earlier + (taken(kind, 0) if u > first % 2 else 0))
                was = steps.taken
                unit = turn + first // 2
                dve.wait_ge(src_group, it + 1)
                mark_same(it, u, 0)
                mark_same(it, u, 1)
                rows(it, u, 0)
                if not isinstance(it, int) or it + 1 < ITERS:
                    take_src(it + 1, 1 - u)
                if kind & NODES:
                    take_node(it)
                mark_same(it, u, 2)
                if kind & NODES:
                    norm_node(it)
                mark_same(it, u, 3)
                rows(it, u, 1)
                if kind & WEIGHTS and u == 0:
                    greatest_weights(unit, kind)
                if kind & WEIGHTS and u == 1:
                    weight_scale(unit, kind)
                    for k in range(KD):
                        cut_weights(unit, kind, k)
                    end_unit(unit, kind)
                assert steps.taken - was == taken(kind, u), (kind, u, steps.taken - was)

            take_src(0, 0)
            iterations(dve, body)


def node_update(nc, sb_, sem_, bank, env):
    g = env
    with ExitStack() as ctx:
        def sb(name, shape, dt=F32):
            return sb_(name, shape, dt, ctx)
        def sem(name):
            return sem_(name, ctx)
        tables, xtab, skip, out, rowmap, ident, nodeT, ones, before = (
            g[k] for k in ("tables", "xtab", "skip", "out", "rowmap", "ident", "nodeT", "ones", "before"))
        b1p, wsum, hscale, hcut, yscale, exi, blki, used = (
            g[k] for k in ("b1p", "wsum", "hscale", "hcut", "yscale", "exi", "blki", "used"))
        eps, eps2, wfT, wup, wr, brb, bfu = (g[k] for k in ("eps", "eps2", "wfT", "wup", "wr", "brb", "bfu"))
        tab = sb("tab", [P, TABLES, BATCH, AC])
        mean = sb("mean", [P, BATCH, 2 * A])
        cnt = sb("cnt", [P, BATCH])
        fused = sb("fused", [A + 1, BATCH * P])
        x1 = [sb(f"x1_{i}", [P, BATCH, D]) for i in range(2)]
        xn2 = sb("xn2", [P, BATCH, D])
        xn2T = sb("xn2T", [P, 2, 2 * D])
        stats = sb("stats2", [P, BATCH, 6])
        mv = sb("mv2", [P, BATCH, 2])
        sd = sb("sd2", [P, 2, BATCH])
        rs = sb("rs2", [P, 2, BATCH])
        ratio = [sb(f"ratio{i}", [P, BATCH]) for i in range(2)]
        root = sb("root", [P, 1])
        root_ready = sem("root_ready")
        bmax = sb("bmax", [P, X])
        hbound = sb("hbound", [P, X])
        nblk = sb("nblk", [P, 4, X])
        nblki = sb("nblki", [P, X], I32)
        blockno = sb("blockno", [1, BLOCKS])
        exf = sb("exf", [1, BLOCKS])
        cover, skipped = (tab[0:1, k, :, :].rearrange("p t a -> p (t a)")[:, 0:BLOCKS * (X - 1)].rearrange(
            "p (i e) -> p i e", e=X - 1) for k in range(2))
        lg = sb("lg", [P, BATCH, X])
        seq8 = sb("seq8", [P, BATCH, X])
        chosen = sb("chosen", [P, 2, BATCH * X])
        tmp = sb("tmp_r", [P, 2, BATCH * X])
        both = tmp[:, 1, :]
        pos = lg[:, :, :].rearrange("p t e -> p (t e)")
        tot = sb("tot", [P, X, BATCH + 1])
        cum = sb("cum", [P, X, BATCH + 1])
        go_on = sb("go_on", [P, X, BATCH + 1])
        top = sb("top", [P, 2, BATCH])
        first = sb("first", [P, BATCH])
        weight = sb("weight", [P, 2, BATCH])
        where = sb("where", [P, 2, BATCH])
        mask = sb("mask", [P, 2, BATCH])
        valid = sb("valid", [P, TPP])
        away = sb("away_r", [P, 2, TPP])
        ids = sb("ids", [P, TPP], I32)
        rowi = [sb(f"rowi{i}", [P, 2, BATCH], I32) for i in range(2)]
        record = [sb(f"record{i}", [P, 2, BATCH, 2], I32) for i in range(2)]

        between = sem("between2")
        made = sem("made")
        tab_loaded = sem("tab_loaded")
        skip_loaded = [sem(f"skip_loaded{b}") for b in range(2)]
        x1_stored = sem("x1_stored")
        mean_ready = sem("mean_ready")
        meanT_psum = sem("meanT_psum")
        meanT_ready = sem("meanT_ready")
        fused_psum = sem("fused_psum")
        fused_ready = sem("fused_ready")
        up_psum = sem("up_psum")
        x1_ready = sem("x1_ready")
        mv_ready = sem("mv2_ready")
        sd_ready = sem("sd2_ready")
        xn2_ready = sem("xn2_ready")
        xn2_stored = sem("xn2_stored")
        xn2T_psum = sem("xn2T_psum")
        xn2T_ready = sem("xn2T_ready")
        logit_psum = sem("logit_psum")
        both_ready = sem("both_ready")
        rank_psum = sem("rank_psum")
        placed = sem("placed")
        gap_ready = sem("gap_ready")
        exp_ready = sem("exp_ready")
        rows_ready = sem("rows_ready")
        scattered = sem("scattered")
        record_free = sem("record_free")
        dve_step = sem("dve_step2")
        ones_ready = sem("ones_ready")
        bmax_ready = sem("bmax_ready")
        bsum_psum = sem("bsum_psum")
        logits_taken = sem("logits_taken")

        halves = [(0, 4), (4, BATCH)]
        pairs = [(j, min(j + 2, BATCH)) for j in range(0, BATCH, 2)]
        NPAIR = len(pairs)
        LOG, PRE, TOT = slice(0, BATCH * X), slice(0, BATCH * X), slice(BATCH * X, 2 * BATCH * X)
        tab_v = [t[0:NPAD, :].rearrange("(p t) a -> p (t a)", p=P) for t in tables]
        skip_v = skip.rearrange("(p t) d -> p (t d)", p=P)
        out_v = out[0:NPAD, :].rearrange("(p t) d -> p (t d)", p=P)
        xtab_v = xtab[0:NPAD, :].rearrange("(p t) d -> p (t d)", p=P)
        assert NB % 2 == 1 and NPAIR % 2 == 0

        with nc.Block() as block:

            def batches(eng, body):
                with eng.Fori(0, (NB - 3) // 2) as it:
                    for b in range(2):
                        body(it * 2 + b, b, it)
                for bt in range(NB - 3, NB):
                    body(bt, bt % 2, bt // 2)

            def is_batch(bt):
                return not isinstance(bt, int) or bt < NB

            @block.sync
            def _(sp):
                def load_skip(bt, b):
                    sp.dma_start(x1[b][:, :, :].rearrange("p t d -> p (t d)"),
                                 skip_v[:, bass.ds(bt * (BATCH * D), BATCH * D)]).then_inc(skip_loaded[b], 16)

                def load_tables(bt):
                    if not isinstance(bt, int) or bt > 0:
                        sp.wait_ge(mean_ready, bt)
                    for k in range(TABLES):
                        sp.dma_start(tab[:, k, :, :].rearrange("p t a -> p (t a)"),
                                     tab_v[k][:, bass.ds(bt * (BATCH * AC), BATCH * AC)]).then_inc(tab_loaded, 16)

                def body(bt, b, n):
                    sp.wait_ge(x1_ready, bt * NPAIR + 2 * NPAIR)
                    sp.dma_start(out_v[:, bass.ds(bt * (BATCH * D), BATCH * D)],
                                 x1[b][:, :, :].rearrange("p t d -> p (t d)")).then_inc(x1_stored, 16)
                    sp.wait_ge(xn2_ready, bt * NPAIR + NPAIR)
                    sp.dma_start(xtab_v[:, bass.ds(bt * (BATCH * D), BATCH * D)],
                                 xn2[:, :, :].rearrange("p t d -> p (t d)")).then_inc(xn2_stored, 16)
                    if is_batch(bt + 3):
                        load_tables(bt + 3)
                    if is_batch(bt + 2):
                        sp.wait_ge(x1_stored, bt * 16 + 16)
                        load_skip(bt + 2, b)

                load_tables(0)
                load_skip(0, 0)
                load_skip(1, 1)
                load_tables(1)
                load_tables(2)
                batches(sp, body)
                sp.wait_ge(x1_stored, 16 * NB)
                sp.wait_ge(xn2_stored, 16 * NB)

            @block.gpsimd
            def _(pool):
                pool.sem_inc(record_free, 2)
                pool.iota(seq8[:, :, :], pattern=[[0, BATCH], [1, X]], base=-X, channel_multiplier=0,
                          allow_small_or_imprecise_dtypes=True).then_inc(made, 1)
                pool.memset(go_on[:, :, :], 1.0).then_inc(made, 1)
                pool.iota(tot[:, :, 0], pattern=[[CAP, X]], base=0, channel_multiplier=0,
                          allow_small_or_imprecise_dtypes=True).then_inc(made, 1)
                pool.memset(valid[:, :], 1.0).then_inc(made, 1)
                pool.iota(ids[:, :], pattern=[[1, TPP]], base=0, channel_multiplier=TPP).then_inc(made, 1)
                pool.iota(away[:, :, :], pattern=[[TPP, 2], [1, TPP]], base=MAP_BLOCKS * BR, channel_multiplier=0,
                          allow_small_or_imprecise_dtypes=True).then_inc(made, 1)
                pool.iota(blockno[:, :], pattern=[[1, BLOCKS]], base=0, channel_multiplier=0,
                          allow_small_or_imprecise_dtypes=True).then_inc(made, 1)
                pool.iota(nblk[:, 2, :], pattern=[[CAP, X]], base=0, channel_multiplier=0,
                          allow_small_or_imprecise_dtypes=True).then_inc(made, 1)
                pool.wait_ge(made, 8)
                pool.memset(go_on[:, :, 0], 0.0).then_inc(made, 1)
                pool.affine_select(out=valid[:, :], in_=valid[:, :], compare_op=ALU.is_ge, fill=0.0,
                                   base=N - 1, pattern=[[-1, TPP]], channel_multiplier=-TPP).then_inc(made, 1)
                for s in range(2):
                    pool.affine_select(out=away[:, s, :], in_=away[:, s, :], compare_op=ALU.is_ge, fill=0.0,
                                       base=-N, pattern=[[1, TPP]], channel_multiplier=TPP).then_inc(made, 1)

                def scatter(bt, b, n):
                    pool.wait_ge(rows_ready, bt + 1)
                    pool.sem_inc(between, 1)
                    for j in range(BATCH):
                        for s in range(2):
                            pool.indirect_dma_start(rowmap, bass.IndirectOffsetOnAxis(ap=rowi[b][:, s, j:j + 1], axis=0),
                                                    record[b][:, s, j, :], None).then_inc(scattered, 16)
                    if is_batch(bt + 2):
                        pool.wait_ge(scattered, bt * (32 * BATCH) + 32 * BATCH)
                        pool.sem_inc(record_free, 1)

                batches(pool, scatter)
                pool.wait_ge(scattered, NB * 32 * BATCH)

            @block.tensor
            def _(pe):
                pe.wait_ge(ones_ready, 2)

                def turn_means(bt):
                    if not isinstance(bt, int) or bt >= 3:
                        pe.wait_ge(placed, bt - 2)
                    pe.wait_ge(mean_ready, bt + 1)
                    for h, (lo, hi) in enumerate(halves):
                        for j in range(lo, hi):
                            mm = pe.transpose(bank[h][:, (j - lo) * P:(j - lo + 1) * P], mean[:, j, :], ident[:, :])
                        mm.then_inc(meanT_psum, 1)

                def update(bt):
                    for h, (lo, hi) in enumerate(halves):
                        pe.wait_ge(meanT_ready, bt * 2 + (h + 1))
                        w = (hi - lo) * P
                        pe.matmul(bank[h][0:A, 0:w], wfT[:, :], nodeT[:, bass.ds(bt * (BATCH * P) + lo * P, w)],
                                  start=True, stop=True).then_inc(fused_psum, 1)
                    for n, (lo, hi) in enumerate(pairs):
                        pe.wait_ge(fused_ready, bt * 2 + (1 if hi <= 4 else 2))
                        pe.wait_ge(x1_ready, bt * NPAIR + (n + 1))
                        for j in range(lo, hi):
                            mm = pe.matmul(bank[2 + n][:, (j - lo) * D:(j - lo + 1) * D], fused[:, j * P:(j + 1) * P],
                                           wup[:, :], start=True, stop=True)
                        mm.then_inc(up_psum, 1)

                def turn_pair(bt, n):
                    pe.wait_ge(xn2_ready, bt * NPAIR + (n + 1))
                    lo, hi = pairs[n]
                    for j in range(lo, hi):
                        for k in range(KD):
                            o = (j - lo) * D + k * P
                            mm = pe.transpose(bank[6][:, o:o + P], xn2[:, j, k * P:(k + 1) * P], ident[:, :])
                    mm.then_inc(xn2T_psum, 1)

                def logit_pair(n):
                    lo, hi = pairs[n]
                    for j in range(lo, hi):
                        for k in range(KD):
                            o = (j - lo) * D + k * P
                            mm = pe.matmul(bank[7][:, j * X:(j + 1) * X], xn2T[:, n % 2, o:o + P], wr[:, k, :],
                                           start=(k == 0), stop=(k == KD - 1))
                    if n == NPAIR - 1:
                        mm.then_inc(logit_psum, 1)

                def places(bt):
                    pe.wait_ge(both_ready, bt + 1)
                    pe.matmul(bank[0][:, PRE], before[:, :], both, start=True, stop=True)
                    pe.matmul(bank[0][:, TOT], ones[:, :], both, start=True, stop=True).then_inc(rank_psum, 1)

                def router(bt):
                    later = not isinstance(bt, int) or bt > 0
                    turn_pair(bt, 0)
                    if later:
                        pe.wait_ge(logits_taken, bt)
                    for n in range(NPAIR):
                        pe.wait_ge(xn2T_ready, bt * NPAIR + (n + 1))
                        if n + 1 < NPAIR:
                            turn_pair(bt, n + 1)
                        logit_pair(n)
                        if n == 1 and later:
                            places(bt - 1)

                def body(bt, b, n):
                    if is_batch(bt + 1):
                        router(bt + 1)
                    else:
                        places(bt)
                    if is_batch(bt + 3):
                        turn_means(bt + 3)
                        update(bt + 3)

                pe.wait_ge(bmax_ready, 1)
                pe.matmul(bank[7][:, 0:X], ones[:, :], bmax[:, :], start=True, stop=True).then_inc(bsum_psum, 1)
                for bt in range(2):
                    turn_means(bt)
                    update(bt)
                router(0)
                turn_means(2)
                update(2)
                batches(pe, body)

            @block.scalar
            def _(act):
                def take_means(bt):
                    for h, (lo, hi) in enumerate(halves):
                        act.wait_ge(meanT_psum, bt * 2 + (h + 1))
                        nc.scalar.copy(nodeT[A:2 * A, bass.ds(bt * (BATCH * P) + lo * P, (hi - lo) * P)],
                                       bank[h][A:2 * A, 0:(hi - lo) * P]).then_inc(meanT_ready, 1)

                def fuse(bt):
                    for h, (lo, hi) in enumerate(halves):
                        act.wait_ge(fused_psum, bt * 2 + (h + 1))
                        nc.scalar.activation(fused[0:A, lo * P:hi * P], bank[h][0:A, 0:(hi - lo) * P], ACT.Relu,
                                             bias=bfu[:, :]).then_inc(fused_ready, 1)

                def deviation(bt):
                    act.wait_ge(mv_ready, bt + 1)
                    nc.scalar.activation(sd[:, 0, :], mv[:, :, 1], ACT.Sqrt, bias=eps[:, :]).then_inc(sd_ready, 1)
                    nc.scalar.activation(sd[:, 1, :], mv[:, :, 1], ACT.Sqrt, bias=eps2[:, :],
                                         scale=1.0 + EPS).then_inc(sd_ready, 1)

                def take_turned(bt):
                    for n_, (lo, hi) in enumerate(pairs):
                        act.wait_ge(xn2T_psum, bt * NPAIR + (n_ + 1))
                        nc.scalar.copy(xn2T[:, n_ % 2, 0:(hi - lo) * D], bank[6][:, 0:(hi - lo) * D]).then_inc(xn2T_ready, 1)
                    if not isinstance(bt, int) or bt > 0:
                        gaps(bt - 1)

                def gaps(bt):
                    act.wait_ge(gap_ready, bt + 1)
                    nc.scalar.activation(weight[:, 1, :], weight[:, 0, :], ACT.Exp).then_inc(exp_ready, 1)

                def body(bt, b, n):
                    if is_batch(bt + 1):
                        take_turned(bt + 1)
                    else:
                        gaps(bt)
                    if is_batch(bt + 2):
                        nc.scalar.activation(root[:, :], eps[:, :], ACT.Sqrt).then_inc(root_ready, 1)
                        act.wait_ge(root_ready, bt + 1)
                    if is_batch(bt + 3):
                        take_means(bt + 3)
                        fuse(bt + 3)
                    if is_batch(bt + 2):
                        deviation(bt + 2)

                for bt in range(2):
                    take_means(bt)
                    fuse(bt)
                deviation(0)
                take_turned(0)
                take_means(2)
                fuse(2)
                deviation(1)
                batches(act, body)

            @block.vector
            def _(dve):
                steps = Steps(dve, dve_step)

                def do(ins):
                    steps.step(ins)
                    steps.settle()

                MEAN_STEPS, STAT_STEPS, NORM_STEPS, ROUTE_STEPS = TABLES.bit_length() + 1, 1, 2, 24
                BATCH_STEPS = MEAN_STEPS + STAT_STEPS + NORM_STEPS + ROUTE_STEPS

                dve.memset(fused[A:A + 1, :], 1.0).then_inc(ones_ready, 1)
                dve.memset(mean[:, :, 0:A], 0.0).then_inc(ones_ready, 1)
                dve.sem_inc(x1_ready, NPAIR)

                def means(bt):
                    dve.wait_ge(tab_loaded, bt * (16 * TABLES) + 16 * TABLES)
                    k = TABLES // 2
                    while k:
                        do(dve.tensor_tensor(tab[:, 0:k, :, :].rearrange("p k t a -> p (k t a)"),
                                             tab[:, 0:k, :, :].rearrange("p k t a -> p (k t a)"),
                                             tab[:, k:2 * k, :, :].rearrange("p k t a -> p (k t a)"), ALU.add))
                        k //= 2
                    do(dve.tensor_scalar(cnt[:, :], tab[:, 0, :, A], 1.0, None, ALU.max))
                    do(dve.reciprocal(cnt[:, :], cnt[:, :]))
                    if not isinstance(bt, int) or bt > 0:
                        dve.wait_ge(meanT_psum, bt * 2)
                    dve.tensor_tensor(mean[:, :, A:2 * A], tab[:, 0, :, 0:A],
                                      cnt[:, :].rearrange("p (t o) -> p t o", o=1).to_broadcast([P, BATCH, A]),
                                      ALU.mult).then_inc(mean_ready, 1)

                def add_update(bt, b, n_):
                    dve.wait_ge(skip_loaded[b], n_ * 16 + 16)
                    for n, (lo, hi) in enumerate(pairs):
                        dve.wait_ge(up_psum, bt * NPAIR + (n + 1))
                        dve.tensor_tensor(x1[b][:, lo:hi, :],
                                          bank[2 + n][:, 0:(hi - lo) * D].rearrange("p (t d) -> p t d", d=D),
                                          x1[b][:, lo:hi, :], ALU.add).then_inc(x1_ready, 1)

                def statistics(bt, b):
                    dve.wait_ge(x1_ready, bt * NPAIR + 2 * NPAIR)
                    for j in range(BATCH):
                        ins = dve.bn_stats(stats[:, j, :], x1[b][:, j, :])
                    do(ins)
                    dve.sem_inc(between, 1)
                    for j in range(BATCH):
                        ins = dve.bn_aggr(mv[:, j, :], stats[:, j, :])
                    ins.then_inc(mv_ready, 1)

                def norm(bt, b):
                    dve.wait_ge(sd_ready, bt * 2 + 2)
                    do(dve.reciprocal(rs[:, :, :], sd[:, :, :]))
                    if not isinstance(bt, int) or bt > 0:
                        dve.wait_ge(xn2T_psum, bt * NPAIR)
                        dve.wait_ge(xn2_stored, bt * 16)
                    for lo, hi in pairs:
                        for j in range(lo, hi):
                            ins = dve.tensor_scalar(xn2[:, j, :], x1[b][:, j, :], mv[:, j, 0:1], rs[:, 1, j:j + 1],
                                                    ALU.subtract, ALU.mult)
                        ins.then_inc(xn2_ready, 1)
                    do(dve.tensor_tensor(ratio[b][:, :], rs[:, 0, :], sd[:, 1, :], ALU.mult))

                def route(bt, b):
                    col = lambda t: t.rearrange("p (t e) -> p t e", e=X)
                    per_tok = lambda t: t.rearrange("p (t o) -> p t o", o=1).to_broadcast([P, BATCH, X])
                    toks = bass.ds(bt * BATCH, BATCH)
                    per_choice = lambda t: t.rearrange("p (o t) -> p o t", o=1).to_broadcast([P, 2, BATCH])
                    dve.wait_ge(record_free, bt + 1)
                    steps.step(dve.tensor_copy(record[b][:, :, :, 0], per_choice(ids[:, toks])))
                    steps.step(dve.tensor_copy(mask[:, :, :], per_choice(valid[:, toks])))
                    dve.wait_ge(logit_psum, bt + 1)
                    dve.tensor_tensor(lg[:, :, :], col(bank[7][:, LOG]), per_tok(ratio[b][:, :]), ALU.mult).then_inc(logits_taken, 1)
                    dve.wait_ge(logits_taken, bt + 1)
                    do(dve.tensor_tensor(lg[:, :, :], lg[:, :, :],
                                         brb[:, :].rearrange("p (o e) -> p o e", o=1).to_broadcast([P, BATCH, X]), ALU.add))
                    for s in range(2):
                        do(dve.tensor_reduce(top[:, s, :], lg[:, :, :], AX_X, ALU.max))
                        do(dve.tensor_tensor(col(tmp[:, 0, :]), lg[:, :, :], per_tok(top[:, s, :]), ALU.is_equal))
                        do(dve.tensor_tensor(col(tmp[:, 0, :]), col(tmp[:, 0, :]), seq8[:, :, :], ALU.mult))
                        do(dve.tensor_reduce(first[:, :], col(tmp[:, 0, :]), AX_X, ALU.min))
                        do(dve.tensor_tensor(col(chosen[:, s, :]), seq8[:, :, :], per_tok(first[:, :]), ALU.is_equal))
                        if s == 0:
                            do(dve.scalar_tensor_tensor(out=lg[:, :, :], in0=col(chosen[:, 0, :]), scalar=-BIG,
                                                        in1=lg[:, :, :], op0=ALU.mult, op1=ALU.add))
                    do(dve.tensor_tensor(chosen[:, :, :].rearrange("p s (t e) -> p (s t) e", e=X),
                                         chosen[:, :, :].rearrange("p s (t e) -> p (s t) e", e=X),
                                         mask[:, :, :].rearrange("p s (t o) -> p (s t) o", o=1).to_broadcast([P, 2 * BATCH, X]),
                                         ALU.mult))
                    dve.tensor_tensor(both, chosen[:, 0, :], chosen[:, 1, :], ALU.add).then_inc(both_ready, 1)
                    dve.tensor_tensor(weight[:, 0, :], top[:, 1, :], top[:, 0, :], ALU.subtract).then_inc(gap_ready, 1)
                    dve.wait_ge(rank_psum, bt + 1)
                    do(dve.tensor_copy(tot[:, :, 1:BATCH + 1], col(bank[0][:, TOT]).rearrange("p t e -> p e t")))
                    run = lambda t: t[:, :, :].rearrange("p e t -> p (e t)")
                    do(dve.tensor_tensor_scan(run(cum), run(go_on), run(tot), 0.0, ALU.mult, ALU.add))
                    dve.tensor_tensor(col(pos[:, :]), cum[:, :, 0:BATCH].rearrange("p e t -> p t e"), col(bank[0][:, PRE]),
                                      ALU.add).then_inc(placed, 1)
                    steps.step(dve.tensor_copy(tot[:, :, 0], cum[:, :, BATCH]))
                    dve.wait_ge(placed, bt + 1)
                    do(dve.tensor_tensor(tmp[:, :, :], chosen[:, :, :],
                                         pos[:, :].rearrange("p (o c) -> p o c", o=1).to_broadcast([P, 2, BATCH * X]), ALU.mult))
                    do(dve.tensor_reduce(where[:, :, :].rearrange("p s t -> p (s t)"),
                                         tmp[:, :, :].rearrange("p s (t e) -> p (s t) e", e=X), AX_X, ALU.add))
                    steps.step(dve.tensor_tensor(rowi[b][:, :, :], where[:, :, :], away[:, :, toks], ALU.add))
                    dve.wait_ge(exp_ready, bt + 1)
                    do(dve.tensor_scalar(first[:, :], weight[:, 1, :], 1.0, None, ALU.add))
                    do(dve.reciprocal(weight[:, 0, :], first[:, :]))
                    do(dve.tensor_tensor(weight[:, 1, :], weight[:, 1, :], weight[:, 0, :], ALU.mult))
                    dve.tensor_copy(record[b][:, :, :, 1].bitcast(F32), weight[:, :, :]).then_inc(rows_ready, 1)

                def norm_all(bt, b, n):
                    add_update(bt, b, n)
                    statistics(bt, b)
                    norm(bt, b)

                def body(bt, b, n):
                    was = steps.taken
                    steps.n = bt * BATCH_STEPS + before_loop
                    route(bt, b)
                    if is_batch(bt + 3):
                        means(bt + 3)
                    else:
                        dve.sem_inc(dve_step, MEAN_STEPS)
                        steps.n = steps.n + MEAN_STEPS
                        steps.taken += MEAN_STEPS
                    if is_batch(bt + 2):
                        norm_all(bt + 2, b, n + 1)
                    else:
                        dve.sem_inc(dve_step, STAT_STEPS + NORM_STEPS)
                        steps.n = steps.n + STAT_STEPS + NORM_STEPS
                        steps.taken += STAT_STEPS + NORM_STEPS
                    assert steps.taken - was == BATCH_STEPS, steps.taken - was

                dve.tensor_reduce(bmax[:, :], b1p[:, :].rearrange("p (e c) -> p e c", c=HC), AX_X, ALU.max,
                                  apply_absolute_value=True).then_inc(bmax_ready, 1)
                dve.wait_ge(bsum_psum, 1)
                do(dve.scalar_tensor_tensor(out=hbound[:, :], in0=wsum[:, 0:X], scalar=XMAX, in1=bank[7][:, 0:X],
                                            op0=ALU.mult, op1=ALU.add))
                do(dve.reciprocal(hcut[:, :], hbound[:, :]))
                do(dve.tensor_scalar(hcut[:, :], hcut[:, :], TOP, None, ALU.mult))
                do(dve.tensor_scalar(hscale[:, :], wsum[:, 0:X], 1.0 / (TOP * XS), None, ALU.mult))
                do(dve.tensor_scalar(yscale[:, :], wsum[:, X:2 * X], 1.0 / TOP, None, ALU.mult))
                do(dve.tensor_tensor(yscale[:, :], yscale[:, :], hbound[:, :], ALU.mult))
                do(dve.tensor_scalar(yscale[:, :], yscale[:, :], 1.0 / TOP, None, ALU.mult))
                means(0)
                means(1)
                norm_all(0, 0, 0)
                means(2)
                norm_all(1, 1, 0)
                before_loop = steps.n
                dve.wait_ge(made, 12)
                batches(dve, body)
                do(dve.tensor_tensor(nblk[:, 0, :], tot[:, :, 0], nblk[:, 2, :], ALU.subtract))
                do(dve.tensor_scalar(nblki[:, :], nblk[:, 0, :], float(BR - 1), None, ALU.add))
                do(dve.tensor_scalar(nblki[:, :], nblki[:, :], BR.bit_length() - 1, None, ALU.arith_shift_right))
                do(dve.tensor_copy(nblk[:, 0, :], nblki[:, :]))
                do(dve.tensor_scalar(nblk[:, 3, :], nblk[:, 0, :], -1.0, float(CAPB), ALU.mult, ALU.add))
                u, v = 0, 1
                d = 1
                while d < X:
                    do(dve.tensor_copy(nblk[:, v, 0:d], nblk[:, u, 0:d]))
                    do(dve.tensor_tensor(nblk[:, v, d:X], nblk[:, u, d:X], nblk[:, u, 0:X - d], ALU.add))
                    u, v = v, u
                    d *= 2
                do(dve.tensor_copy(used[:, :], nblk[0:1, u, X - 1:X]))
                per_block = lambda t: t.rearrange("p (o e) -> p o e", o=1).to_broadcast([1, BLOCKS, X - 1])
                do(dve.tensor_tensor(cover[:, :, :], blockno[:, :].rearrange("p (i o) -> p i o", o=1).to_broadcast([1, BLOCKS, X - 1]),
                                     per_block(nblk[0:1, u, 0:X - 1]), ALU.is_ge))
                do(dve.tensor_reduce(exf[:, :], cover[:, :, :], AX_X, ALU.add))
                do(dve.tensor_copy(exi[:, :], exf[:, :]))
                do(dve.tensor_tensor(skipped[:, :, :], cover[:, :, :], per_block(nblk[0:1, 3, 0:X - 1]), ALU.mult))
                do(dve.tensor_reduce(exf[:, :], skipped[:, :, :], AX_X, ALU.add))
                do(dve.tensor_tensor(exf[:, :], exf[:, :], blockno[:, :], ALU.add))
                do(dve.tensor_copy(blki[:, :], exf[:, :]))


def experts(nc, ctx, sb_, sem_, bank, env):
    g = env
    def sb(name, shape, dt=F32):
        return sb_(name, shape, dt, ctx)
    def sem(name):
        return sem_(name, ctx)
    rowmap, xtab, out, added, ident16, w1s, w2s, b1p, hscale, hcut, yscale, exi, blki, used = (
        g[k] for k in ("rowmap", "xtab", "out", "added", "ident16", "w1s", "w2s", "b1p", "hscale", "hcut", "yscale",
                       "exi", "blki", "used"))
    b2b = sb("b2b", [P, X, D])
    between = sem("between3")
    b2_loaded = sem("b2_loaded")
    warm = sb("warm", [P, 1])
    warmed = sem("warmed")
    RING = 4
    QUARTERS = 4
    QC = HC // QUARTERS
    rec = [sb(f"rec{i}", [P, SUB, 2], I32) for i in range(RING)]
    xg = [sb(f"xg{i}", [P, SUB, D]) for i in range(2)]
    xs = [sb(f"xs{i}", [P, SUB, 2, D], F16) for i in range(2)]
    xT = [sb(f"xT{i}", [P, 2 * KD, BR], F16) for i in range(2)]
    hid = [sb(f"hid{i}", [P, HC, BR]) for i in range(2)]
    hs = [sb(f"hs{i}", [P, 2, HC, BR], F16) for i in range(2)]
    yb = [sb(f"yb{i}", [P, SUB, D]) for i in range(2)]
    rec_loaded = [sem(f"rec_loaded{r}") for r in range(RING)]
    gathered = [sem(f"gathered{b}") for b in range(2)]
    x_hi = sem("x_hi")
    x_cut = sem("x_cut")
    xT_psum = sem("xT_psum")
    xT_ready = sem("xT_ready")
    h_psum = sem("h_psum")
    h_ready = sem("h_ready")
    cut_hi = sem("cut_hi")
    cut_ready = sem("cut_ready")
    y_psum = sem("y_psum")
    y_sum = sem("y_sum")
    y_ready = sem("y_ready")
    bankH, bankX, bankY = bank[0:4], bank[4:6], bank[6:8]
    rowmap_v = rowmap[0:MAP_BLOCKS * BR, :].rearrange("(i p s) c -> p i (s c)", p=P, s=SUB)
    FIRST, EACH = 3 * 16, SUB * 16
    SURE = ceil_div(2 * N, BR)
    LOOPED = (SURE - 3) // RING * RING
    assert RING % 2 == 0

    def blocks(eng, body):
        with eng.Fori(0, LOOPED // RING) as n:
            for r in range(RING):
                body(n * RING + r, n, r)
        for i in range(LOOPED, BLOCKS):
            body(i, i // RING, i % RING)

    def if_block(eng, reach, i, work):
        if not isinstance(i, int) or i < SURE:
            work()
        elif i < BLOCKS:
            with eng.If(reach > i):
                work()

    def reach_of(eng):
        return eng.value_load(used[0:1, 0:1], min_val=SURE, max_val=BLOCKS)

    def expert_of(eng, i):
        return eng.value_load(exi[0:1, bass.ds(i, 1)], min_val=0, max_val=X - 1)

    with nc.Block() as block:

        @block.sync
        def _(sp):
            def load_record(i, r):
                at = sp.value_load(blki[0:1, bass.ds(i, 1)], min_val=0, max_val=MAP_BLOCKS - 1)
                sp.dma_start(rec[r][:, :, :].rearrange("p s c -> p (s c)"),
                             rowmap_v[:, bass.ds(at, 1), :].rearrange("p o c -> p (o c)")).then_inc(rec_loaded[r], 16)

            for i in range(RING):
                load_record(i, i)
            sp.dma_start(b2b[:, :, :].rearrange("p e d -> p (e d)"),
                         g["b2"].rearrange("(o e) d -> o (e d)", o=1).to_broadcast([P, X * D])).then_inc(b2_loaded, 16)

            def reload_record(i, r):
                sp.wait_ge(added, i * EACH + (FIRST + EACH - RING * EACH))
                load_record(i, r)

            reach = reach_of(sp)
            blocks(sp, lambda i, n, r: if_block(sp, reach, i + RING, lambda: reload_record(i + RING, r)))

        @block.gpsimd
        def _(pool):
            def gather(i, n, r):
                b = r % 2
                pool.wait_ge(rec_loaded[r], n * 16 + 16)
                pool.sem_inc(between, 1)
                if not isinstance(i, int) or i >= 2:
                    pool.wait_ge(x_cut, i - 1)
                    pool.sem_inc(between, 1)
                for s in range(SUB):
                    pool.indirect_dma_start(xg[b][:, s, :], None, xtab,
                                            bass.IndirectOffsetOnAxis(ap=rec[r][:, s, 0:1], axis=0)).then_inc(gathered[b], 16)

            def add(i, r):
                b = r % 2
                pool.wait_ge(y_ready, i + 3)
                pool.wait_ge(added, i * EACH + FIRST)
                pool.sem_inc(between, 1)
                for s in range(SUB):
                    pool.indirect_dma_start(out, bass.IndirectOffsetOnAxis(ap=rec[r][:, s, 0:1], axis=0),
                                            yb[b][:, s, :], None, compute_op=ALU.add).then_inc(added, 16)
                if isinstance(i, int) and i >= SURE - 1:
                    pool.wait_ge(added, FIRST + EACH * (i + 1))

            def body(i, n, r):
                if_block(pool, reach, i + 3, lambda: gather(i + 3, n + (1 if r + 3 >= RING else 0), (r + 3) % RING))
                if_block(pool, reach, i, lambda: add(i, r))

            reach = reach_of(pool)
            for i in range(3):
                gather(i, 0, i)
            blocks(pool, body)

        @block.tensor
        def _(pe):
            def turn(i, b):
                pe.wait_ge(x_cut, i + 1)
                for s in range(SUB):
                    for k in range(2 * KD):
                        mm = pe.transpose(bankX[b][:, :].bitcast(F16)[:, k * BR + s * P:k * BR + (s + 1) * P],
                                          xs[b][:, s, k // KD, k % KD * P:(k % KD + 1) * P], ident16[:, :])
                mm.then_inc(xT_psum, 1)

            def layer1(i, b):
                e = expert_of(pe, i)
                pe.wait_ge(xT_ready, i + 1)
                for c in range(HC):
                    if c % QC == 0:
                        pe.wait_ge(h_ready, i * QUARTERS + (c // QC + 1))
                    o = bankH[c // QC][:, (c % QC) * BR:(c % QC + 1) * BR]
                    passes = [(k, w, v) for k in range(KD) for w, v in ((0, 0), (0, 1), (1, 0))]
                    for m, (k, w, v) in enumerate(passes):
                        lhs = w1s[:, bass.ds(e, 1), k, w, c * P:(c + 1) * P].rearrange("p o h -> p (o h)")
                        mm = pe.matmul(o, lhs, xT[b][:, v * KD + k, :], start=(m == 0), stop=(m == len(passes) - 1))
                    if c % QC == QC - 1:
                        mm.then_inc(h_psum, 1)

            def layer2(i, b):
                e = expert_of(pe, i)
                pe.wait_ge(y_ready, i + 1)
                for s in range(SUB):
                    for c in range(HC):
                        if s == 0 and c % QC == 0:
                            pe.wait_ge(cut_ready, i * QUARTERS + (c // QC + 1))
                        for m, (v, w) in enumerate(((0, 0), (0, 1), (1, 0))):
                            rhs = w2s[:, bass.ds(e, 1), c, w, :].rearrange("p o d -> p (o d)")
                            mm = pe.matmul(bankY[b][:, s * D:(s + 1) * D], hs[b][:, v, c, s * P:(s + 1) * P], rhs,
                                           start=(c == 0 and m == 0), stop=(c == HC - 1 and m == 2))
                mm.then_inc(y_psum, 1)

            def body(i, n, r):
                b = r % 2
                if_block(pe, reach, i + 1, lambda: layer1(i + 1, 1 - b))
                if_block(pe, reach, i + 2, lambda: turn(i + 2, b))
                if_block(pe, reach, i, lambda: layer2(i, b))

            reach = reach_of(pe)
            turn(0, 0)
            turn(1, 1)
            layer1(0, 0)
            blocks(pe, body)

        @block.scalar
        def _(act):
            act.sem_inc(h_ready, QUARTERS)
            nc.scalar.activation(warm[:, :], hscale[:, 0:1], ACT.Gelu).then_inc(warmed, 1)
            act.wait_ge(warmed, 1)

            def gelu(i, b):
                e = expert_of(act, i)
                for c in range(HC):
                    if c % QC == 0:
                        act.wait_ge(h_psum, i * QUARTERS + (c // QC + 1))
                    ins = nc.scalar.activation(hid[b][:, c, :], bankH[c // QC][:, (c % QC) * BR:(c % QC + 1) * BR],
                                               ACT.Gelu, bias=b1p[:, bass.ds(e * HC + c, 1)],
                                               scale=hscale[:, bass.ds(e, 1)])
                    if c % QC == QC - 1:
                        ins.then_inc(h_ready, 1)

            reach = reach_of(act)
            gelu(0, 0)
            blocks(act, lambda i, n, r: if_block(act, reach, i + 1, lambda: gelu(i + 1, 1 - r % 2)))

        @block.vector
        def _(dve):
            dve.sem_inc(y_ready, 2)

            def cut_x(i, b, n2):
                dve.wait_ge(gathered[b], n2 * (16 * SUB) + 16 * SUB)
                dve.tensor_scalar(xs[b][:, :, 0, :], xg[b][:, :, :], XS, None, ALU.mult).then_inc(x_hi, 1)
                dve.wait_ge(x_hi, i + 1)
                dve.scalar_tensor_tensor(out=xs[b][:, :, 1, :], in0=xg[b][:, :, :], scalar=XS, in1=xs[b][:, :, 0, :],
                                         op0=ALU.mult, op1=ALU.subtract).then_inc(x_cut, 1)

            def take_x(i, b):
                dve.wait_ge(xT_psum, i + 1)
                dve.tensor_copy(xT[b][:, :, :].rearrange("p k t -> p (k t)"),
                                bankX[b][:, :].bitcast(F16)).then_inc(xT_ready, 1)

            def cut(i, b):
                e = expert_of(dve, i)
                to_cut = hcut[:, bass.ds(e, 1)]
                for q in range(QUARTERS):
                    hi, lo = (hs[b][:, v, q * QC:(q + 1) * QC, :].rearrange("p c t -> p (c t)") for v in range(2))
                    whole = hid[b][:, q * QC:(q + 1) * QC, :].rearrange("p c t -> p (c t)")
                    dve.wait_ge(h_ready, i * QUARTERS + (q + 1 + QUARTERS))
                    dve.tensor_scalar(hi, whole, to_cut, None, ALU.mult).then_inc(cut_hi, 1)
                    dve.wait_ge(cut_hi, i * QUARTERS + (q + 1))
                    dve.scalar_tensor_tensor(out=lo, in0=whole, scalar=to_cut, in1=hi, op0=ALU.mult,
                                             op1=ALU.subtract).then_inc(cut_ready, 1)

            def finish(i, r):
                b = r % 2
                e = expert_of(dve, i)
                dve.wait_ge(y_psum, i + 1)
                dve.wait_ge(added, i * EACH + (FIRST - EACH))
                for s in range(SUB):
                    dve.scalar_tensor_tensor(out=yb[b][:, s, :], in0=bankY[b][:, s * D:(s + 1) * D],
                                             scalar=yscale[:, bass.ds(e, 1)],
                                             in1=b2b[:, bass.ds(e, 1), :].rearrange("p o d -> p (o d)"),
                                             op0=ALU.mult, op1=ALU.add).then_inc(y_sum, 1)
                dve.wait_ge(y_sum, i * SUB + SUB)
                for s in range(SUB):
                    ins = dve.tensor_scalar(yb[b][:, s, :], yb[b][:, s, :], rec[r][:, s, 1:2].bitcast(F32), None, ALU.mult)
                ins.then_inc(y_ready, 1)

            def body(i, n, r):
                b = r % 2
                if_block(dve, reach, i + 2, lambda: cut_x(i + 2, b, n * (RING // 2) + (r // 2 + 1)))
                if_block(dve, reach, i + 1, lambda: cut(i + 1, 1 - b))
                if_block(dve, reach, i + 2, lambda: take_x(i + 2, b))
                if_block(dve, reach, i, lambda: finish(i, r))

            reach = reach_of(dve)
            cut_x(0, 0, 0)
            take_x(0, 0)
            cut_x(1, 1, 0)
            take_x(1, 1)
            cut(0, 0)
            dve.wait_ge(b2_loaded, 16)
            blocks(dve, body)


_NAMES = {"x": "x", "src": "src", "edge": "edge_attr_32"} | {
    k: f"L0_gnn_{k}" for k in ("W_down", "b_down", "W_time", "b_time", "W_fusion", "b_fusion", "W_up", "b_up")} | {
    k: f"L0_ffn_{k}" for k in ("Wr", "br", "ln_g", "ln_b", "W1", "b1", "W2", "b2")}


def kernel(**inputs):
    import numpy as _np
    import concourse.bacc as _bacc
    from concourse import mybir as _mybir
    from concourse.bass_utils import run_bass_kernel_spmd as _run

    arrays = {k: _np.ascontiguousarray(inputs[name]) for k, name in _NAMES.items()}
    for k, rows, fill in (("x", NPAD, 0), ("edge", EPAD, 0), ("src", EPAD, N)):
        a = arrays[k]
        padded = _np.full((rows,) + a.shape[1:], fill, a.dtype)
        padded[:a.shape[0]] = a
        arrays[k] = padded
    nc = _bacc.Bacc("TRN2", target_bir_lowering=False, num_devices=1)
    args = {k: nc.dram_tensor(f"in_{k}", a.shape, _mybir.dt.from_np(a.dtype), kind="ExternalInput").ap()
            for k, a in arrays.items()}
    res = nc.dram_tensor("out_0_dram", (ROWS, D), F32, kind="ExternalOutput").ap()
    program(nc, **args, out=res)
    r = _run(nc, [{f"in_{k}": a for k, a in arrays.items()}], core_ids=[0])
    return r.results[0]["out_0_dram"][:N]
```
